# Optimizing a Trainium2 kernel written in Bass

```python
import numpy as np
import jax
import jax.numpy as jnp

def _softmax(x, axis=-1):
    return jax.nn.softmax(x, axis=axis)

def _gelu(x):
    return jax.nn.gelu(x, approximate=True)

def _silu(x):
    return jax.nn.silu(x)

def _sigmoid(x):
    return jax.nn.sigmoid(x)

def _layernorm(x, axis=-1, eps=1e-05):
    m = jnp.mean(x, axis=axis, keepdims=True)
    v = jnp.var(x, axis=axis, keepdims=True)
    return (x - m) / jnp.sqrt(v + eps)

def _scatter_add(tgt, idx, src, axis=0):
    return tgt.at[idx].add(src)

def _segment_sum(src, seg, n):
    return jax.ops.segment_sum(src, seg, n)
kernel_name = 'mk_adaln_attn_ffn_d1_seqx_r8_ce6c6a'

def setup_inputs(seed: int=0):
    np.random.seed(seed)
    _w = jnp.asarray

    def _rec_inputs():
        import jax
        import jax.numpy as jnp
        _rk = jax.random.key(seed)
        x = -7.109e-05 + 0.9999 * jax.random.normal(jax.random.fold_in(_rk, 1), (32, 32, 512), jnp.float32)
        _lenS = 32 - jax.random.randint(jax.random.fold_in(_rk, 7), (32,), 0, max(1, 32 // 4) + 1, jnp.int32)
        _lenS2 = 32 - jax.random.randint(jax.random.fold_in(_rk, 8), (32,), 0, max(1, 32 // 4) + 1, jnp.int32)
        itok_B_0_15 = jax.random.randint(jax.random.fold_in(_rk, 11), (32,), 0, 16, jnp.int32)
        itok_B_78_3631 = jax.random.randint(jax.random.fold_in(_rk, 12), (32,), 78, 454, jnp.int32)
        return (x, itok_B_0_15, itok_B_78_3631)
    x, itok_B_0_15, itok_B_78_3631 = _rec_inputs()

    def _L0_cond_setup():
        import jax, jax.numpy as jnp
        import numpy as np
        NUM_CONDITIONS = 16
        IN_CH = 32
        OUT_CH = 32
        B = 64
        T = 512
        key = jax.random.key(seed)
        k_x, k_w, k_c = jax.random.split(key, 3)
        x = jax.random.normal(k_x, (B, IN_CH, T), dtype=jnp.float32)
        bound = float(np.sqrt(6.0 / IN_CH))
        weights = jax.random.uniform(k_w, (NUM_CONDITIONS, IN_CH, OUT_CH), dtype=jnp.float32, minval=-bound, maxval=bound)
        condition = jax.random.randint(k_c, (B,), 0, NUM_CONDITIONS, dtype=jnp.int64)
        return {'x': x, 'weights': weights, 'condition': condition}
    _L0_cond_all = _L0_cond_setup()
    _L0_cond_in = {k: v for k, v in _L0_cond_all.items() if k in ('weights',)}
    del _L0_cond_all

    def _L0_attn_setup():
        import jax, jax.numpy as jnp
        import numpy as np
        Q_DIM = 512
        N_HEADS = 32
        HEAD_DIM = 128
        INNER = N_HEADS * HEAD_DIM
        EPS = 1e-06

        def rms_norm(x, w):
            xf = x.astype(jnp.float32)
            var = jnp.mean(xf * xf, axis=-1, keepdims=True)
            return (w.astype(jnp.float32) * xf * jax.lax.rsqrt(var + EPS)).astype(x.dtype)
        key = jax.random.key(seed)
        ks = jax.random.split(key, 12)
        s = 1.0 / np.sqrt(Q_DIM)
        return {'hidden_states': jax.random.normal(ks[0], (2, 256, Q_DIM), dtype=jnp.float32), 'Wq': jax.random.normal(ks[1], (Q_DIM, INNER), dtype=jnp.float32) * s, 'bq': jnp.zeros((INNER,), dtype=jnp.float32), 'Wk': jax.random.normal(ks[2], (Q_DIM, INNER), dtype=jnp.float32) * s, 'bk': jnp.zeros((INNER,), dtype=jnp.float32), 'Wv': jax.random.normal(ks[3], (Q_DIM, INNER), dtype=jnp.float32) * s, 'bv': jnp.zeros((INNER,), dtype=jnp.float32), 'Wo': jax.random.normal(ks[4], (INNER, Q_DIM), dtype=jnp.float32) * s, 'bo': jnp.zeros((Q_DIM,), dtype=jnp.float32), 'gq': jnp.ones((INNER,), dtype=jnp.float32), 'gk': jnp.ones((INNER,), dtype=jnp.float32)}
    _L0_attn_all = _L0_attn_setup()
    _L0_attn_in = {k: v for k, v in _L0_attn_all.items() if k in ('Wq', 'bq', 'Wk', 'bk', 'Wv', 'bv', 'Wo', 'bo', 'gq', 'gk')}
    del _L0_attn_all

    def _L0_cond2_setup():
        import math
        import jax, jax.numpy as jnp
        import numpy as np
        B, H, N, L = (16, 32, 64, 512)
        DT_MIN, DT_MAX = (0.001, 0.1)

        def _get_kernel(log_dt, C, log_A_real, A_imag, length):
            dt = jnp.exp(log_dt)
            Cc = C[..., 0] + 1j * C[..., 1]
            A = -jnp.exp(log_A_real) + 1j * A_imag
            dtA = A * dt[:, None]
            Ct = Cc * (jnp.exp(dtA) - 1.0) / A
            P = dtA[:, :, None] * jnp.arange(length, dtype=jnp.float32)
            K = 2.0 * jnp.einsum('hn,hnl->hl', Ct, jnp.exp(P)).real
            return K
        key = jax.random.key(seed)
        ks = jax.random.split(key, 5)
        u = jax.random.normal(ks[0], (B, H, L), dtype=jnp.float32)
        log_dt = jax.random.uniform(ks[1], (H,), dtype=jnp.float32) * (math.log(DT_MAX) - math.log(DT_MIN)) + math.log(DT_MIN)
        C = jax.random.normal(ks[2], (H, N, 2), dtype=jnp.float32)
        log_A_real = jnp.log(0.5 * jnp.ones((H, N), dtype=jnp.float32))
        A_imag = math.pi * jnp.broadcast_to(jnp.arange(N, dtype=jnp.float32), (H, N))
        D = jax.random.normal(ks[3], (H,), dtype=jnp.float32)
        length = jax.random.randint(ks[4], (B,), 1, L + 1, dtype=jnp.int32)
        return {'u': u, 'log_dt': log_dt, 'C': C, 'log_A_real': log_A_real, 'A_imag': A_imag, 'D': D, 'length': length}
    _L0_cond2_all = _L0_cond2_setup()
    _L0_cond2_in = {k: v for k, v in _L0_cond2_all.items() if k in ('log_dt', 'C', 'log_A_real', 'A_imag', 'D')}
    del _L0_cond2_all

    def _L0_ffn_setup():
        import jax, jax.numpy as jnp
        import numpy as np
        B, T, D_IN, D_OUT = (8, 256, 512, 512)
        N_LORAS, RANK = (16, 32)
        SCALING = 1.0
        key = jax.random.key(seed)
        ks = jax.random.split(key, 8)
        std = 1.0 / D_IN ** 0.5
        x = jax.random.normal(ks[0], (B, T, D_IN), dtype=jnp.float32)
        idx = jax.random.randint(ks[1], (B,), 0, N_LORAS)
        gate = jax.nn.one_hot(idx, N_LORAS, dtype=jnp.float32)
        kernel = jax.random.normal(ks[2], (D_IN, D_OUT), dtype=jnp.float32) * std
        bias = jnp.zeros((D_OUT,), dtype=jnp.float32)
        lora_A = jax.random.normal(ks[3], (N_LORAS, RANK, D_IN), dtype=jnp.float32) * std
        lora_B = jax.random.normal(ks[4], (N_LORAS, D_OUT, RANK), dtype=jnp.float32) * 0.01
        lora_A_shared = jax.random.normal(ks[5], (RANK, D_IN), dtype=jnp.float32) * std
        lora_B_shared = jax.random.normal(ks[6], (D_OUT, RANK), dtype=jnp.float32) * 0.01
        return {'x': x, 'gate': gate, 'kernel': kernel, 'bias': bias, 'lora_A': lora_A, 'lora_B': lora_B, 'lora_A_shared': lora_A_shared, 'lora_B_shared': lora_B_shared}
    _L0_ffn_all = _L0_ffn_setup()
    _L0_ffn_in = {k: v for k, v in _L0_ffn_all.items() if k in ('gate', 'kernel', 'bias', 'lora_A', 'lora_B', 'lora_A_shared', 'lora_B_shared')}
    del _L0_ffn_all
    return {'x': x, 'itok_B_0_15': itok_B_0_15, 'itok_B_78_3631': itok_B_78_3631, 'L0_cond_weights': _L0_cond_in['weights'], 'L0_attn_Wq': _L0_attn_in['Wq'], 'L0_attn_bq': _L0_attn_in['bq'], 'L0_attn_Wk': _L0_attn_in['Wk'], 'L0_attn_bk': _L0_attn_in['bk'], 'L0_attn_Wv': _L0_attn_in['Wv'], 'L0_attn_bv': _L0_attn_in['bv'], 'L0_attn_Wo': _L0_attn_in['Wo'], 'L0_attn_bo': _L0_attn_in['bo'], 'L0_attn_gq': _L0_attn_in['gq'], 'L0_attn_gk': _L0_attn_in['gk'], 'L0_cond2_log_dt': _L0_cond2_in['log_dt'], 'L0_cond2_C': _L0_cond2_in['C'], 'L0_cond2_log_A_real': _L0_cond2_in['log_A_real'], 'L0_cond2_A_imag': _L0_cond2_in['A_imag'], 'L0_cond2_D': _L0_cond2_in['D'], 'L0_ffn_gate': _L0_ffn_in['gate'], 'L0_ffn_kernel': _L0_ffn_in['kernel'], 'L0_ffn_bias': _L0_ffn_in['bias'], 'L0_ffn_lora_A': _L0_ffn_in['lora_A'], 'L0_ffn_lora_B': _L0_ffn_in['lora_B'], 'L0_ffn_lora_A_shared': _L0_ffn_in['lora_A_shared'], 'L0_ffn_lora_B_shared': _L0_ffn_in['lora_B_shared']}

def reference(x, itok_B_0_15, itok_B_78_3631, L0_cond_weights, L0_attn_Wq, L0_attn_bq, L0_attn_Wk, L0_attn_bk, L0_attn_Wv, L0_attn_bv, L0_attn_Wo, L0_attn_bo, L0_attn_gq, L0_attn_gk, L0_cond2_log_dt, L0_cond2_C, L0_cond2_log_A_real, L0_cond2_A_imag, L0_cond2_D, L0_ffn_gate, L0_ffn_kernel, L0_ffn_bias, L0_ffn_lora_A, L0_ffn_lora_B, L0_ffn_lora_A_shared, L0_ffn_lora_B_shared):
    import jax
    import jax.numpy as jnp

    def _L0_cond_ref(x, weights, condition):
        import jax, jax.numpy as jnp
        import numpy as np
        NUM_CONDITIONS = 16
        IN_CH = 32
        OUT_CH = 32
        B = 64
        T = 512
        W = weights[condition]
        return jnp.einsum('bct,bcd->bdt', x, W)

    def _L0_attn_ref(hidden_states, Wq, bq, Wk, bk, Wv, bv, Wo, bo, gq, gk):
        import jax, jax.numpy as jnp
        import numpy as np
        Q_DIM = 512
        N_HEADS = 32
        HEAD_DIM = 128
        INNER = N_HEADS * HEAD_DIM
        EPS = 1e-06

        def rms_norm(x, w):
            xf = x.astype(jnp.float32)
            var = jnp.mean(xf * xf, axis=-1, keepdims=True)
            return (w.astype(jnp.float32) * xf * jax.lax.rsqrt(var + EPS)).astype(x.dtype)
        B, S, _ = hidden_states.shape
        q = hidden_states @ Wq + bq
        k = hidden_states @ Wk + bk
        v = hidden_states @ Wv + bv
        q = rms_norm(q, gq)
        k = rms_norm(k, gk)
        q = q.reshape(B, S, N_HEADS, HEAD_DIM).transpose(0, 2, 1, 3)
        k = k.reshape(B, S, N_HEADS, HEAD_DIM).transpose(0, 2, 1, 3)
        v = v.reshape(B, S, N_HEADS, HEAD_DIM).transpose(0, 2, 1, 3)
        scale = 1.0 / np.sqrt(HEAD_DIM)
        attn = jnp.einsum('bhqd,bhkd->bhqk', q.astype(jnp.float32), k.astype(jnp.float32)) * scale
        attn = jax.nn.softmax(attn, axis=-1)
        out = jnp.einsum('bhqk,bhkd->bhqd', attn, v.astype(jnp.float32))
        out = out.transpose(0, 2, 1, 3).reshape(B, S, INNER).astype(hidden_states.dtype)
        return out @ Wo + bo

    def _L0_cond2_ref(u, log_dt, C, log_A_real, A_imag, D, length):
        import math
        import jax, jax.numpy as jnp
        import numpy as np
        B, H, N, L = (16, 32, 64, 512)
        DT_MIN, DT_MAX = (0.001, 0.1)

        def _get_kernel(log_dt, C, log_A_real, A_imag, length):
            dt = jnp.exp(log_dt)
            Cc = C[..., 0] + 1j * C[..., 1]
            A = -jnp.exp(log_A_real) + 1j * A_imag
            dtA = A * dt[:, None]
            Ct = Cc * (jnp.exp(dtA) - 1.0) / A
            P = dtA[:, :, None] * jnp.arange(length, dtype=jnp.float32)
            K = 2.0 * jnp.einsum('hn,hnl->hl', Ct, jnp.exp(P)).real
            return K
        Bq, Hq, Lq = u.shape
        K = _get_kernel(log_dt, C, log_A_real, A_imag, Lq)
        n = 2 * Lq
        kf = jnp.fft.rfft(K, n=n)
        uf = jnp.fft.rfft(u, n=n)
        y = jnp.fft.irfft(uf * kf[None], n=n)[..., :Lq]
        y = y + u * D[:, None]
        mask = (jnp.arange(Lq)[None, :] < length[:, None]).astype(u.dtype)
        return y * mask[:, None, :]

    def _L0_ffn_ref(x, gate, kernel, bias, lora_A, lora_B, lora_A_shared, lora_B_shared):
        import jax, jax.numpy as jnp
        import numpy as np
        B, T, D_IN, D_OUT = (8, 256, 512, 512)
        N_LORAS, RANK = (16, 32)
        SCALING = 1.0
        base_out = jnp.matmul(x, kernel) + bias
        b = gate.shape[0]
        x_flat = x.reshape(b, -1, x.shape[-1])
        A_eff = jnp.einsum('bn,nri->bri', gate, lora_A)
        B_eff = jnp.einsum('bn,nor->bor', gate, lora_B)
        Ax = jnp.einsum('bri,bti->btr', A_eff, x_flat)
        delta_flat = jnp.einsum('bor,btr->bto', B_eff, Ax)
        Ax_s = jnp.einsum('ri,bti->btr', lora_A_shared, x_flat)
        delta_flat = delta_flat + jnp.einsum('or,btr->bto', lora_B_shared, Ax_s)
        delta = delta_flat.reshape(x.shape[:-1] + (kernel.shape[-1],))
        return base_out + (SCALING * delta).astype(base_out.dtype)
    x = x + _L0_attn_ref(_L0_cond_ref(x, L0_cond_weights, itok_B_0_15), L0_attn_Wq, L0_attn_bq, L0_attn_Wk, L0_attn_bk, L0_attn_Wv, L0_attn_bv, L0_attn_Wo, L0_attn_bo, L0_attn_gq, L0_attn_gk)
    x = x + _L0_ffn_ref(_L0_cond2_ref(x, L0_cond2_log_dt, L0_cond2_C, L0_cond2_log_A_real, L0_cond2_A_imag, L0_cond2_D, itok_B_78_3631), L0_ffn_gate, L0_ffn_kernel, L0_ffn_bias, L0_ffn_lora_A, L0_ffn_lora_B, L0_ffn_lora_A_shared, L0_ffn_lora_B_shared)
    return x

_drawn_inputs = setup_inputs


def setup_inputs(seed=0):
    import zlib

    import numpy as np

    out = dict(_drawn_inputs(seed))
    spreads = {'L0_attn_bq': (0.0, 0.1),
     'L0_attn_bk': (0.0, 0.8),
     'L0_attn_bv': (0.0, 0.1),
     'L0_attn_bo': (0.0, 0.1),
     'L0_attn_gq': (1.0, 0.2),
     'L0_attn_gk': (1.0, 0.2),
     'L0_cond2_log_A_real': (-0.6931471824645996, 0.2),
     'L0_ffn_bias': (0.0, 0.1)}
    factors = {}
    for name, (base, spread) in spreads.items():
        noise = np.random.default_rng([zlib.crc32(name.encode()), seed]).standard_normal(out[name].shape)
        drawn = base * np.exp(spread * noise) if base else spread * noise
        out[name] = jnp.asarray(drawn.astype(out[name].dtype))
    for name, factor in factors.items():
        out[name] = (out[name] * factor).astype(out[name].dtype)
    return out
```

```python
from contextlib import ExitStack

import concourse.bass as bass
from concourse import mybir

F32 = mybir.dt.float32
F32R = mybir.dt.float32r
I32 = mybir.dt.int32
ALU = mybir.AluOpType
ACT = mybir.ActivationFunctionType
AX_X = mybir.AxisListType.X

P = 128
BATCH, SEQ, FEAT = 32, 32, 512
TOK = BATCH * SEQ
HEADS, HD = 32, 128
INNER = HEADS * HD
KC = FEAT // P
G = TOK // P
BPG = P // SEQ
HALF = TOK // 2
QUAD = 4
NQ = HEADS // QUAD
NCOND, NLORA, RANK = 16, 16, 32
NSTATE = 64
CL, CA = 32, FEAT // 32
PADL = P + FEAT
RMS_EPS = 1e-6
PI = 3.141592653589793
C1 = 6.28125
C2 = 0.0019350051879882812
C3 = 2 * PI - C1 - C2
MAGIC = 12582912.0
PI_F32 = 3.1415925
LN2_HI, LN2_LO = 0.693359375, -2.12194440e-4
EXP_COEFFS = [1 / 5040, 1 / 720, 1 / 120, 1 / 24, 1 / 6, 1 / 2, 1.0, 1.0]


def build_program(nc, x, cond_idx, lengths, cond_w, wq, bq, wk, bk, wv, bv, wo, bo, gq, gk,
                  log_dt, ssm_c, log_a, a_im, ssm_d, gate, ffn_w, ffn_b, lora_a, lora_b,
                  lora_as, lora_bs, kpad, out):
    ctx = ExitStack()
    with ctx:
        def sb(name, shape, dt=F32, scope=ctx):
            return scope.enter_context(nc.sbuf_tensor(name, shape, dt))

        def sem(name):
            return ctx.enter_context(nc.semaphore(name))

        def overlay(*lots):
            made = []
            for n, lot in enumerate(lots):
                scope = ctx if n == len(lots) - 1 else ExitStack()
                made.append([sb(name, shape, dt, scope) for name, shape, dt in lot])
                if scope is not ctx:
                    scope.close()
            return made

        psum = ctx.enter_context(nc.psum_tensor("psum", [P, 8 * 512], F32))

        def bank(n, width=512):
            return psum[:, n * 512:n * 512 + width]

        ident = sb("ident", [P, P])
        ones = sb("ones", [P, P])
        delta32 = sb("delta32", [P, 32])
        rowgrp = sb("rowgrp", [P, 4])
        params = sb("params", [P, 9, 32])
        bo_t = sb("bo_t", [P, KC])
        gqk = sb("gqk", [P, HEADS])
        inv_norm = sb("inv_norm", [P, G, 32])
        var_k = sb("var_k", [P, G, 32])
        var_q = sb("var_q", [P, G])
        row_max = sb("row_max", [P, QUAD * G])
        row_sum = sb("row_sum", [P, QUAD * G])
        row_inv = sb("row_inv", [P, QUAD * G])
        lidx = sb("lidx", [P, KC])
        mask = sb("mask", [P, KC, BATCH])
        gate_p = sb("gate_p", [P, 4, G])
        d_row = sb("d_row", [1, 32])
        PARAM = dict(bq=0, bk=1, gq=2, gk=3, bv=4, log_a=5, a_im=6, c_re=7, c_im=8)

        def param(name):
            return params[:, PARAM[name], :]

        (toep1,), (mix_hi, mix_lo) = overlay(
            [("toep1", [P, 16, 512], F32)],
            [("mix_hi", [P, KC, TOK], F32R), ("mix_lo", [P, KC, TOK], F32R)])
        (select, mix_w, cond_nat, cond_i, cond_f, onehot, prm_nat, bo_nat, bo_rev, delta, len_i, len_f, gate_b), (toep0,), (scores,) = overlay(
            [("select", [P, 4, BATCH, 32], F32), ("mix_w", [P, G, P], F32), ("cond_nat", [P, 4, 32], F32),
             ("cond_i", [P, BATCH], I32), ("cond_f", [P, BATCH], F32), ("onehot", [P, 4, BATCH], F32),
             ("prm_nat", [32, 10, P], F32), ("bo_nat", [KC, P], F32), ("bo_rev", [KC, P], F32), ("delta", [P, BPG, 32], F32),
             ("len_i", [P, BATCH], I32), ("len_f", [P, BATCH], F32), ("gate_b", [P, G, NLORA], F32)],
            [("toep0", [P, 16, 512], F32)],
            [("scores", [P, HEADS, G, 32], F32)])
        (ang, expo, mult, quarter), (acc,) = overlay(
            [("ang", [P, 67, 32], F32), ("expo", [P, 48, 32], F32), ("mult", [P, 67], F32),
             ("quarter", [P, 67], F32)],
            [("acc", [P, KC, TOK], F32)])
        (turns, prod), (k_sb, kzero), (gate_sel,), (sm_s, sm_e) = overlay(
            [("turns", [P, 32, 32], F32), ("prod", [P, 32, 32], F32)],
            [("k_sb", [CA, 32, CL], F32), ("kzero", [32, P], F32)],
            [("gate_sel", [P, 4, G, RANK], F32)],
            [("sm_s", [P, QUAD, G, 32], F32), ("sm_e", [P, QUAD, G, 32], F32)])
        (lb_nat,), (wv_raw,) = overlay([("lb_nat", [P, KC, NLORA * RANK], F32)], [("wv_raw", [P, KC, 512], F32)])
        (la_nat,), (wv_hi,) = overlay([("la_nat", [P, 4, FEAT], F32)], [("wv_hi", [P, KC, 512], F32R)])
        (ffn_sb,), (wv_lo,) = overlay([("ffn_sb", [P, KC, FEAT], F32)], [("wv_lo", [P, KC, 512], F32R)])
        wo_raw = sb("wo_raw", [P, QUAD, FEAT])
        ((w_hi, w_lo, sq, qk_sb, x_nat, sumsq, w_raw),
         (x2p, y_t, lora_a_t, lora_b_t, b_eff, b_t, ax, o_stage, flip, las_nat, lbs_nat),
         (v_sb, p_blocks, attn_hi, attn_lo, wo_hi, wo_lo)) = overlay(
            [("w_hi", [P, 2, 2, KC, HD], F32R), ("w_lo", [P, 2, 2, KC, HD], F32R),
             ("sq", [P, 2, 2, TOK], F32), ("qk_sb", [P, 2, 2, TOK], F32), ("x_nat", [P, G, FEAT], F32),
             ("sumsq", [P, 2, TOK], F32), ("w_raw", [P, 2, 2, KC, HD], F32)],
            [("x2p", [P, SEQ, KC, BATCH], F32), ("y_t", [P, KC, BATCH, SEQ], F32),
             ("lora_a_t", [P, KC, G, 2 * RANK], F32), ("lora_b_t", [2 * RANK + 1, G, FEAT], F32),
             ("b_eff", [P, 2, FEAT], F32), ("b_t", [P, 4, FEAT], F32), ("ax", [2 * RANK + 1, 2, P], F32),
             ("o_stage", [P, 2, FEAT], F32), ("flip", [P, P], F32), ("las_nat", [RANK, FEAT], F32), ("lbs_nat", [P, KC, RANK], F32)],
            [("v_sb", [P, G, 512], F32), ("p_blocks", [P, QUAD, G, P], F32),
             ("attn_hi", [P, QUAD, TOK], F32R), ("attn_lo", [P, QUAD, TOK], F32R),
             ("wo_hi", [P, QUAD, FEAT], F32R), ("wo_lo", [P, QUAD, FEAT], F32R)])
        small = sb("small", [P, 16, 32])
        SM = {n: i for i, n in enumerate("log_dt dt ea xr th den rden thx ex t0 t1 er ei nr ni t2".split())}
        SM["cr2"], SM["ci2"] = SM["xr"], SM["th"]

        def sm(name, lo=0, hi=P):
            return small[lo:hi, SM[name], :]

        x_in = [sem("x_in0"), sem("x_in1")]
        cond_in, prm_in, c_in, misc_in = sem("cond_in"), sem("prm_in"), sem("c_in"), sem("misc_in")
        c_dup = sem("c_dup")
        const_ok, sel_const, delta_ok = sem("const_ok"), sem("sel_const"), sem("delta_ok")
        condf_ok, hot_ok, sel_ok = sem("condf_ok"), sem("hot_ok"), sem("sel_ok")
        zero_ok = sem("zero_ok")
        prm_mm, prm_ok = sem("prm_mm"), sem("prm_ok")
        mixw_mm, mixw_ok = sem("mixw_mm"), sem("mixw_ok")
        mix_mm, mixhi_ok, mixlo_ok = sem("mix_mm"), sem("mixhi_ok"), sem("mixlo_ok")
        gqk_ok = sem("gqk_ok")
        w_in = [sem("w_in0"), sem("w_in1")]
        whi_ok, wlo_ok = sem("whi_ok"), sem("wlo_ok")
        q_mm, k_mm, s_mm = sem("q_mm"), sem("k_mm"), sem("s_mm")
        q_sq, k_sq, q_ok, k_ok, s_ok, sum_ok = (sem(n) for n in ("q_sq", "k_sq", "q_ok", "k_ok", "s_ok", "sum_ok"))
        ssm, ang_ok, fn_ok, tab_ok = (sem(n) for n in ("ssm", "ang_ok", "fn_ok", "tab_ok"))
        kern_mm, kern_ok, kern_d, kpad_out = sem("kern_mm"), sem("kern_ok"), sem("kern_d"), sem("kpad_out")
        vk_mm, vq_mm, var_ok, std_ok, norm = (sem(n) for n in ("vk_mm", "vq_mm", "var_ok", "std_ok", "norm"))
        xt_mm, xt_ok = sem("xt_mm"), sem("xt_ok")
        wv_in, wo_in = sem("wv_in"), sem("wo_in")
        wvhi_ok, wvlo_ok, wohi_ok, wolo_ok = sem("wvhi_ok"), sem("wvlo_ok"), sem("wohi_ok"), sem("wolo_ok")
        v_mm, v_ok, pv_mm, ahi_ok, alo_ok = (sem(n) for n in ("v_mm", "v_ok", "pv_mm", "ahi_ok", "alo_ok"))
        wo_mm, acc_ok = sem("wo_mm"), sem("acc_ok")
        blocks_zero, soft, e_ok, p_ok = sem("blocks_zero"), sem("soft"), sem("e_ok"), sem("p_ok")
        toep_in0, toep_in1, lb_in, la_in, ffn_in, sh_in = (sem(n) for n in ("toep_in0", "toep_in1", "lb_in", "la_in", "ffn_in", "sh_in"))
        bias_in, flip_ok, xrev_ok = sem("bias_in"), sem("flip_ok"), sem("xrev_ok")
        gatep_ok, gsel_ok, mask_ok = sem("gatep_ok"), sem("gsel_ok"), sem("mask_ok")
        x2p_ok, bt_mm, bt_ok, sh_mm, sh_ok = (sem(n) for n in ("x2p_ok", "bt_mm", "bt_ok", "sh_mm", "sh_ok"))
        ae_mm, ae_ok, be_mm, be_ok, be_in = (sem(n) for n in ("ae_mm", "ae_ok", "be_mm", "be_ok", "be_in"))
        conv_mm, y_ok, ax_one, ax_mm, ax_ok = (sem(n) for n in ("conv_mm", "y_ok", "ax_one", "ax_mm", "ax_ok"))
        out_mm, out_ok = sem("out_mm"), sem("out_ok")
        out_dma = [sem("out_dma0"), sem("out_dma1")]

        x_rows = x.rearrange("(g p) f -> p g f", p=P)
        out_rows = out.rearrange("(g p) f -> g p f", p=P)
        wqk_cols = [w.rearrange("(c p) n -> p c n", p=P) for w in (wq, wk)]
        wv_cols = wv.rearrange("(c p) n -> p c n", p=P)
        wo_rows = wo.rearrange("(h d) n -> d h n", d=HD)

        def every_partition(ap, n, parts=P):
            return bass.AP(ap.tensor, 0, [[0, parts], [1, n]])

        def repeat(ap, axis, n):
            dims = [list(d) for d in ap.ap]
            dims.insert(axis, [0, n])
            return bass.AP(ap.tensor, ap.offset, dims)

        def backwards(ap):
            dims = [list(d) for d in ap.ap]
            n = dims[-1][1]
            dims[-1] = [-1, n]
            return bass.AP(ap.tensor, ap.offset + n - 1, dims)

        def chunks_backwards(tile):
            return backwards(tile[:].rearrange("p h (c n) -> p (h c) n", n=P))

        def quadrant(b):
            return slice(32 * b, 32 * b + 32)

        block = ctx.enter_context(nc.Block())

        @block.sync
        def _(sp):
            sp.dma_start(x_nat[:, 0:4, :], x_rows[:, 0:4, :]).then_inc(x_in[0], 16)

            def load_qk(h, slot):
                for m in range(2):
                    sp.dma_start(w_raw[:, slot, m], wqk_cols[m][:, :, bass.ds(h * HD, HD)]).then_inc(w_in[slot], 16)

            load_qk(0, 0)
            sp.dma_start(x_nat[:, 4:8, :], x_rows[:, 4:8, :]).then_inc(x_in[1], 16)
            load_qk(1, 1)
            with sp.Fori(1, HEADS // 2) as i:
                for j in range(2):
                    sp.wait_ge(wlo_ok, i * 2 + (j - 1))
                    load_qk(i * 2 + j, j)

            def load_v(t):
                sp.dma_start(wv_raw[:], wv_cols[:, :, bass.ds(t * 512, 512)]).then_inc(wv_in, 16)

            def load_o(t):
                sp.dma_start(wo_raw[:], wo_rows[:, bass.ds(t * QUAD, QUAD), :]).then_inc(wo_in, 16)

            load_v(0)
            load_o(0)
            sp.wait_ge(kern_d, 2)
            sp.dma_start(kpad[:, 0:P], kzero[:, :]).then_inc(kpad_out, 16)
            sp.dma_start(kpad[:, P:].rearrange("h (a c) -> a h c", a=CA), k_sb[:]).then_inc(kpad_out, 16)
            with sp.Fori(1, NQ) as t:
                sp.wait_ge(wvlo_ok, t)
                load_v(t)
                sp.wait_ge(wolo_ok, t)
                load_o(t)
            sp.wait_ge(kpad_out, 32)
            sp.wait_ge(soft, 6 * (NQ - 1) + 1)
            sp.dma_start(toep0[:], bass.AP(kpad.tensor, 1, [[1, P], [PADL, 16], [1, 512]])).then_inc(toep_in0, 16)
            sp.wait_ge(wvlo_ok, NQ)
            for c in range(KC):
                sp.dma_start(lb_nat[:, c, :].rearrange("p (n r) -> p n r", n=NLORA),
                             lora_b.rearrange("n (c p) r -> c p n r", p=P)[c]).then_inc(lb_in, 16)
            sp.wait_ge(v_mm, G * NQ)
            sp.dma_start(la_nat[:], lora_a.rearrange("(k j) r i -> (j r) k i", j=4)).then_inc(la_in, 16)
            sp.dma_start(toep1[:], bass.AP(kpad.tensor, 16 * PADL + 1, [[1, P], [PADL, 16], [1, 512]])).then_inc(toep_in1, 16)
            sp.dma_start(ffn_sb[:], ffn_w.rearrange("(c p) n -> p c n", p=P)).then_inc(ffn_in, 16)
            sp.wait_ge(wo_mm, G * NQ)
            sp.dma_start(las_nat[:], lora_as).then_inc(sh_in, 16)
            sp.dma_start(lbs_nat[:], lora_bs.rearrange("(c p) r -> p c r", p=P)).then_inc(sh_in, 16)
            for g in range(G):
                sp.dma_start(lora_b_t[2 * RANK:2 * RANK + 1, g, :], every_partition(ffn_b, FEAT, 1)).then_inc(bias_in, 16)
            sp.wait_ge(be_ok, 2)
            for g in range(G):
                sp.dma_start(lora_b_t[RANK:2 * RANK, g, :], b_eff[quadrant(g % 4), g // 4, :]).then_inc(be_in, 16)
            for g in range(G):
                sp.wait_ge(out_ok, g + 1)
                sp.dma_start(out_rows[g], o_stage[:, g % 2, :]).then_inc(out_dma[g % 2], 16)
            for n in range(2):
                sp.wait_ge(out_dma[n], 16 * G // 2)

        @block.gpsimd
        def _(pool):
            gp = nc.gpsimd
            for j in range(4):
                gp.iota(rowgrp[quadrant(j), :], [[4, 4]], base=j, channel_multiplier=0,
                        allow_small_or_imprecise_dtypes=True).then_inc(sel_const, 1)
                pool.wait_ge(sel_const, j + 1)
            gp.memset(delta[:], 0.0).then_inc(delta_ok, 1)
            pool.wait_ge(delta_ok, 1)
            gp.affine_select(out=delta[:], in_=delta[:], compare_op=ALU.not_equal, fill=1.0, base=0,
                             pattern=[[-32, 4], [-1, 32]], channel_multiplier=1).then_inc(delta_ok, 1)
            pool.wait_ge(delta_ok, 2)
            gp.tensor_tensor(delta[:, 0:2, :], delta[:, 0:2, :], delta[:, 2:4, :], ALU.add).then_inc(delta_ok, 1)
            pool.wait_ge(delta_ok, 3)
            gp.tensor_tensor(delta32[:], delta[:, 0, :], delta[:, 1, :], ALU.add).then_inc(delta_ok, 1)
            gp.memset(ident[:], 0.0).then_inc(const_ok, 1)
            pool.wait_ge(const_ok, 1)
            gp.affine_select(out=ident[:], in_=ident[:], compare_op=ALU.not_equal, fill=1.0, base=0,
                             pattern=[[-1, P]], channel_multiplier=1).then_inc(const_ok, 1)
            pool.wait_ge(c_in, 16)
            for part in range(2):
                src = prm_nat[:, 9, :].rearrange("h (n two) -> h n two", two=2)[:, :, part]
                gp.tensor_copy(prm_nat[:, 7 + part, :].rearrange("h (d n) -> h d n", d=2),
                               repeat(src, 1, 2)).then_inc(c_dup, 1)
            pool.wait_ge(prm_in, 16 * 10)
            gp.tensor_copy(bo_rev[:, :], backwards(bo_nat[:, :])).then_inc(c_dup, 1)
            gp.memset(ones[:], 1.0).then_inc(const_ok, 1)
            gp.memset(sumsq[:], 0.0).then_inc(zero_ok, 1)

            pool.wait_ge(misc_in, 64)
            count = [0]

            def step(ins):
                count[0] += 1
                ins.then_inc(ssm, 1)
                pool.wait_ge(ssm, count[0])

            gp.iota(lidx[:], [[P, KC]], base=0, channel_multiplier=1, allow_small_or_imprecise_dtypes=True)
            step(gp.tensor_copy(len_f[:], len_i[:]))
            for c in range(KC):
                last = gp.tensor_scalar(mask[:, c, :], len_f[:], lidx[:, c:c + 1], None, ALU.is_gt)
            last.then_inc(mask_ok, 1)
            for j in range(4):
                gp.tensor_copy(gate_p[quadrant(j), :, :],
                               gate_b[quadrant(j), :, j::4].rearrange("p b k -> p k b")).then_inc(gatep_ok, 1)
                pool.wait_ge(gatep_ok, j + 1)
            pool.wait_ge(prm_ok, 1)
            gp.tensor_tensor(gqk[:], param("gq"), param("gk"), ALU.mult).then_inc(gqk_ok, 1)

            pool.wait_ge(mix_mm, G)
            for g in range(G):
                row = x_nat[:, g, :].rearrange("p (c n) -> p c n", n=P)
                tmp = turns[:, 0:16, :].rearrange("p a b -> p (a b)")
                step(gp.tensor_copy(tmp, x_nat[:, g, :]))
                step(gp.tensor_copy(row, backwards(tmp.rearrange("p (c n) -> p c n", n=P))))
            gp.memset(sm("t2"), 0.0).then_inc(xrev_ok, 1)

            gp.iota(mult[:, 0:32], [[1, 32]], base=0, channel_multiplier=0, allow_small_or_imprecise_dtypes=True)
            gp.iota(mult[:, 32:64], [[0, 2], [32, 16]], base=0, channel_multiplier=0, allow_small_or_imprecise_dtypes=True)
            gp.memset(mult[:, 64:66], 1.0)
            step(gp.memset(mult[:, 66:67], 0.5))
            step(gp.memset(quarter[:], 0.0))
            step(gp.memset(quarter[0:64, 0:32], 0.25))
            step(gp.memset(quarter[:, 48:64], 0.25))
            step(gp.memset(quarter[:, 65:66], 0.25))
            def exp_in_place(x, k, poly):
                step(gp.tensor_scalar(x, x, 88.0, -87.0, ALU.min, ALU.max))
                step(gp.tensor_scalar(k, x, 1.4426950408889634, None, ALU.mult))
                step(gp.tensor_scalar(k, k, MAGIC, None, ALU.add))
                step(gp.tensor_scalar(k, k, -MAGIC, None, ALU.add))
                for part in (LN2_HI, LN2_LO):
                    step(gp.tensor_scalar(poly, k, -part, None, ALU.mult))
                    step(gp.tensor_tensor(x, x, poly, ALU.add))
                step(gp.tensor_scalar(poly, x, EXP_COEFFS[0], EXP_COEFFS[1], ALU.mult, ALU.add))
                for coeff in EXP_COEFFS[2:]:
                    step(gp.tensor_tensor(poly, poly, x, ALU.mult))
                    step(gp.tensor_scalar(poly, poly, coeff, None, ALU.add))
                step(gp.tensor_scalar(k, k, 127.0, None, ALU.add))
                step(gp.tensor_scalar(k.bitcast(I32), k, 8388608.0, None, ALU.mult))
                step(gp.tensor_tensor(x, poly, k, ALU.mult))

            step(gp.tensor_copy(sm("dt"), sm("log_dt")))
            exp_in_place(sm("dt"), sm("t0"), sm("t1"))
            step(gp.tensor_copy(sm("ea"), param("log_a")))
            exp_in_place(sm("ea"), sm("t0"), sm("t1"))
            step(gp.tensor_tensor(sm("t0"), sm("ea"), sm("dt"), ALU.mult))
            step(gp.tensor_scalar(sm("xr"), sm("t0"), -1.0, None, ALU.mult))
            step(gp.tensor_tensor(sm("th"), param("a_im"), sm("dt"), ALU.mult))
            step(gp.tensor_tensor(sm("t0"), sm("ea"), sm("ea"), ALU.mult))
            step(gp.tensor_tensor(sm("t1"), param("a_im"), param("a_im"), ALU.mult))
            step(gp.tensor_tensor(sm("den"), sm("t0"), sm("t1"), ALU.add))
            step(gp.memset(sm("t2"), -1.0))
            step(gp.tensor_tensor(sm("rden"), sm("den"), sm("t2"), ALU.pow))
            step(gp.tensor_copy(sm("ex"), sm("xr")))
            exp_in_place(sm("ex"), sm("t0"), sm("t1"))
            step(gp.tensor_tensor(ang[:], repeat(mult[:], 2, 32), repeat(sm("th"), 1, 67), ALU.mult))
            step(gp.tensor_tensor(expo[:], repeat(mult[:, 0:48], 2, 32), repeat(sm("xr"), 1, 48), ALU.mult))
            for a, b in ((0, 32), (32, 64), (64, 67)):
                k, pr, an = turns[:, 0:b - a, :], prod[:, 0:b - a, :], ang[:, a:b, :]
                qt = repeat(quarter[:, a:b], 2, 32)
                step(gp.tensor_scalar(k, an, 1.0 / (2 * PI), None, ALU.mult))
                step(gp.tensor_tensor(k, k, qt, ALU.add))
                step(gp.tensor_scalar(k, k, MAGIC, None, ALU.add))
                step(gp.tensor_scalar(k, k, -MAGIC, None, ALU.add))
                for part in (C1, C2, C3):
                    step(gp.tensor_scalar(pr, k, -part, None, ALU.mult))
                    step(gp.tensor_tensor(an, an, pr, ALU.add))
                step(gp.tensor_scalar(pr, qt, 2 * PI, None, ALU.mult))
                step(gp.tensor_tensor(an, an, pr, ALU.add))
                step(gp.tensor_scalar(an, an, PI_F32, -PI_F32, ALU.min, ALU.max))
            for a, b in ((0, 32), (32, 48)):
                exp_in_place(expo[:, a:b, :], turns[:, 0:b - a, :], prod[:, 0:b - a, :])
            gp.memset(sm("t2"), 0.0).then_inc(ang_ok, 1)
            pool.wait_ge(fn_ok, 2)
            sin_th, cos_th, sin_half = ang[:, 64, :], ang[:, 65, :], ang[:, 66, :]
            step(gp.tensor_scalar(sm("t0"), sm("ex"), 1.0, None, ALU.add))
            step(gp.tensor_tensor(sm("t0"), sm("t0"), sm("thx"), ALU.mult))
            step(gp.tensor_tensor(sm("er"), sm("t0"), cos_th, ALU.mult))
            step(gp.tensor_tensor(sm("t1"), sin_half, sin_half, ALU.mult))
            step(gp.tensor_scalar(sm("t1"), sm("t1"), -2.0, None, ALU.mult))
            step(gp.tensor_tensor(sm("er"), sm("er"), sm("t1"), ALU.add))
            step(gp.tensor_tensor(sm("ei"), sm("ex"), sin_th, ALU.mult))
            step(gp.tensor_tensor(sm("t0"), sm("ei"), param("a_im"), ALU.mult))
            step(gp.tensor_tensor(sm("t1"), sm("er"), sm("ea"), ALU.mult))
            step(gp.tensor_tensor(sm("nr"), sm("t0"), sm("t1"), ALU.subtract))
            step(gp.tensor_tensor(sm("t0"), sm("er"), param("a_im"), ALU.mult))
            step(gp.tensor_tensor(sm("t1"), sm("ei"), sm("ea"), ALU.mult))
            step(gp.tensor_tensor(sm("ni"), sm("t0"), sm("t1"), ALU.add))
            step(gp.tensor_scalar(sm("t2"), sm("rden"), 2.0, None, ALU.mult))
            step(gp.tensor_tensor(sm("nr"), sm("nr"), sm("t2"), ALU.mult))
            step(gp.tensor_tensor(sm("ni"), sm("ni"), sm("t2"), ALU.mult))
            step(gp.tensor_scalar(sm("ni"), sm("ni"), -1.0, None, ALU.mult))
            step(gp.tensor_tensor(sm("t0"), param("c_re"), sm("nr"), ALU.mult))
            step(gp.tensor_tensor(sm("t1"), param("c_im"), sm("ni"), ALU.mult))
            step(gp.tensor_tensor(sm("cr2"), sm("t0"), sm("t1"), ALU.subtract))
            step(gp.tensor_tensor(sm("t0"), param("c_re"), sm("ni"), ALU.mult))
            step(gp.tensor_tensor(sm("t1"), param("c_im"), sm("nr"), ALU.mult))
            step(gp.tensor_tensor(sm("ci2"), sm("t0"), sm("t1"), ALU.add))
            step(gp.tensor_copy(sm("er", 0, 64), sm("cr2", 0, 64)))
            step(gp.tensor_scalar(sm("er", 64, P), sm("ci2", 64, P), -1.0, None, ALU.mult))
            step(gp.tensor_scalar(sm("ei", 0, 64), sm("ci2", 0, 64), -1.0, None, ALU.mult))
            step(gp.tensor_scalar(sm("ei", 64, P), sm("cr2", 64, P), -1.0, None, ALU.mult))
            step(gp.tensor_tensor(expo[:, 0:32, :], expo[:, 0:32, :], ang[:, 0:32, :], ALU.mult))
            for cols, coeff in ((slice(32, 48), "ei"), (slice(48, 64), "er")):
                step(gp.tensor_tensor(ang[:, cols, :], ang[:, cols, :], expo[:, 32:48, :], ALU.mult))
                step(gp.tensor_tensor(ang[:, cols, :], ang[:, cols, :], repeat(sm(coeff), 1, 16), ALU.mult))
            gp.tensor_tensor(ang[:, 32:48, :], ang[:, 32:48, :], ang[:, 48:64, :], ALU.add).then_inc(tab_ok, 1)
            gp.memset(kzero[:], 0.0).then_inc(kern_d, 1)
            pool.wait_ge(kern_ok, 1)
            gp.tensor_tensor(k_sb[0:1, :, 0], k_sb[0:1, :, 0], d_row[:, :], ALU.add).then_inc(kern_d, 1)
            pool.wait_ge(sum_ok, 2 * HEADS)
            gp.memset(p_blocks[:], 0.0).then_inc(blocks_zero, 1)
            pool.wait_ge(p_ok, NQ)
            for c in range(4):
                last = gp.tensor_tensor(gate_sel[:, c, :, :], repeat(gate_p[:, c, :], 2, RANK),
                                        repeat(delta32[:], 1, G), ALU.mult)
            last.then_inc(gsel_ok, 1)
            pool.wait_ge(gsel_ok, 1)
            pool.wait_ge(wo_mm, G * NQ)
            gp.memset(ax[2 * RANK:2 * RANK + 1, :, :], 1.0).then_inc(ax_one, 1)
            pool.wait_ge(ax_one, 1)
            gp.memset(flip[:], 0.0).then_inc(flip_ok, 1)
            pool.wait_ge(flip_ok, 1)
            gp.affine_select(out=flip[:], in_=flip[:], compare_op=ALU.not_equal, fill=1.0, base=-(P - 1),
                             pattern=[[1, P]], channel_multiplier=1).then_inc(flip_ok, 1)

        @block.tensor
        def _(pe):
            mm = nc.tensor.matmul

            def product3(out, terms):
                last = None
                for n, (lh, ll, rh, rl) in enumerate(terms):
                    mm(out, lh, rh, start=(n == 0), stop=False)
                    mm(out, lh, rl, start=False, stop=False)
                    last = mm(out, ll, rh, start=False, stop=(n == len(terms) - 1))
                return last

            pe.wait_ge(cond_in, 32)
            for c in range(4):
                pe.wait_ge(sel_ok, c + 1)
                for g in range(G):
                    last = mm(bank(1)[:, 32 * g:32 * g + 32], select[:, c, BPG * g:BPG * g + BPG, :],
                              cond_nat[:, c, :], start=(c == 0 and g == 0), stop=(c == 3), skip_group_check=True)
            last.then_inc(mixw_mm, 1)

            pe.wait_ge(const_ok, 2)
            pe.wait_ge(prm_in, 16 * 10)
            pe.wait_ge(c_dup, 3)
            for n in range(9):
                nc.tensor.transpose(bank(0)[:, 32 * n:32 * n + 32], prm_nat[:, n, :], ident[0:32, 0:32])
            nc.tensor.transpose(bank(0)[:, 320:320 + KC], bo_rev[:, :], ident[0:KC, 0:KC]).then_inc(prm_mm, 1)

            pe.wait_ge(mixw_ok, 1)
            for g in range(G):
                pe.wait_ge(x_in[g // 4], 16)
                if g >= 6:
                    pe.wait_ge(mixlo_ok, g - 5)
                for c in range(KC):
                    last = mm(bank(2 + g % 6)[:, P * c:P * c + P], x_nat[:, g, P * c:P * c + P],
                              mix_w[:, g, :], start=True, stop=True)
                last.then_inc(mix_mm, 1)

            def head_scores(h, slot):
                pe.wait_ge(q_ok, h * 2 + 2)
                pe.wait_ge(k_ok, h * 2 + 2)
                if not (isinstance(h, int) and h < 1):
                    pe.wait_ge(s_ok, h)
                for g in range(G):
                    last = mm(bank(4, 1024)[:, P * g:P * g + P], qk_sb[:, slot, 0, P * g:P * g + P],
                              qk_sb[:, slot, 1, P * g:P * g + P], start=True, stop=True)
                last.then_inc(s_mm, 1)

            def head_qk(h, slot, first=False):
                pe.wait_ge(wlo_ok, h + 1)
                for m, (done, free) in enumerate(((q_mm, q_ok), (k_mm, k_ok))):
                    for n in range(2):
                        if not first:
                            pe.wait_ge(free, h * 2 + (n - 1))
                        elif m == 0:
                            pe.wait_ge(mixlo_ok, 4 * n + 4)
                        product3(bank(2 * m + n),
                                 [(w_hi[:, slot, m, c, :], w_lo[:, slot, m, c, :],
                                   mix_hi[:, c, HALF * n:HALF * n + HALF], mix_lo[:, c, HALF * n:HALF * n + HALF])
                                  for c in range(KC)]).then_inc(done, 1)
                        if m == 0 and n == 0 and not first:
                            head_scores(h - 1, 1 - slot)

            pe.wait_ge(prm_ok, 1)
            head_qk(0, 0, first=True)
            head_qk(1, 1)
            with pe.Fori(1, HEADS // 2 - 1) as i:
                for j in range(2):
                    head_qk(i * 2 + j, j)
            head_qk(HEADS - 2, 0)
            pe.wait_ge(tab_ok, 1)
            for h in range(SEQ):
                last = mm(bank(6, 1024)[0:CA, CL * h:CL * h + CL], ang[:, 32:48, h], expo[:, 0:CL, h],
                          start=True, stop=True)
            last.then_inc(kern_mm, 1)
            head_qk(HEADS - 1, 1)
            head_scores(HEADS - 1, 1)

            def value_group(t, g, free=True):
                if free:
                    pe.wait_ge(v_ok, t * G + (g - 1))
                product3(bank(g % 2),
                         [(mix_hi[:, c, P * g:P * g + P], mix_lo[:, c, P * g:P * g + P],
                           wv_hi[:, c, :], wv_lo[:, c, :]) for c in range(KC)]).then_inc(v_mm, 1)

            def attend(t, first=False):
                pe.wait_ge(p_ok, t + 1)
                pe.wait_ge(v_ok, t * G + G)
                for u in range(8):
                    h, half = u // 2, u % 2
                    if not (first and u < 4):
                        pe.wait_ge(alo_ok, t * 8 + (u - 3))
                    for g in range(4 * half, 4 * half + 4):
                        last = mm(bank(2 + u % 4)[:, P * (g % 4):P * (g % 4) + P],
                                  v_sb[:, g, HD * h:HD * h + HD], p_blocks[:, h, g, :], start=True, stop=True)
                    last.then_inc(pv_mm, 1)

            def project(t, first=False):
                pe.wait_ge(wolo_ok, t + 1)
                pe.wait_ge(alo_ok, t * 8 + 8)
                for u in range(8):
                    c, half = u // 2, u % 2
                    if not (first and u < 2):
                        pe.wait_ge(acc_ok, t * 8 + (u - 1))
                    tok = slice(HALF * half, HALF * half + HALF)
                    product3(bank(6 + u % 2),
                             [(wo_hi[:, h, P * c:P * c + P], wo_lo[:, h, P * c:P * c + P],
                               attn_hi[:, h, tok], attn_lo[:, h, tok]) for h in range(QUAD)]).then_inc(wo_mm, 1)

            pe.wait_ge(q_ok, 2 * HEADS)
            pe.wait_ge(wvlo_ok, 1)
            value_group(0, 0, free=False)
            value_group(0, 1, free=False)
            pe.wait_ge(sum_ok, 2 * HEADS)
            pe.wait_ge(kern_ok, 1)
            for n in range(2):
                last = mm(bank(6 + n), ones[:, :], sumsq[:, 1, HALF * n:HALF * n + HALF], start=True, stop=True)
            last.then_inc(vk_mm, 1)
            pe.wait_ge(k_ok, 2 * HEADS)
            for g in range(G):
                last = mm(bank(2)[:, g:g + 1], sumsq[:, 0, P * g:P * g + P], ones[:, 0:1], start=True, stop=True)
            last.then_inc(vq_mm, 1)
            for g in range(2, G):
                value_group(0, g)
            pe.wait_ge(xrev_ok, 1)
            pe.wait_ge(var_ok, 5)
            pe.wait_ge(s_ok, HEADS)
            for u in range(8):
                c, half = u // 2, u % 2
                if u >= 4:
                    pe.wait_ge(xt_ok, u - 3)
                for g in range(4 * half, 4 * half + 4):
                    last = nc.tensor.transpose(bank(2 + u % 4)[:, P * (g % 4):P * (g % 4) + P],
                                               x_nat[:, g, P * c:P * c + P], ident[:, :])
                last.then_inc(xt_mm, 1)
            pe.wait_ge(xt_ok, 8)
            attend(0, first=True)
            pe.wait_ge(wvlo_ok, 2)
            for g in range(G):
                value_group(1, g)
            project(0, first=True)
            with pe.Fori(1, NQ - 1) as t:
                attend(t)
                pe.wait_ge(wvlo_ok, t + 2)
                for g in range(G):
                    value_group(t + 1, g)
                project(t)
            attend(NQ - 1)
            project(NQ - 1)

            pe.wait_ge(lb_in, 64)
            pe.wait_ge(alo_ok, 8 * NQ)
            for c in range(4):
                for o in range(KC):
                    last = nc.tensor.transpose(bank(c)[:, P * o:P * o + P], lb_nat[:, o, P * c:P * c + P], ident[:, :])
                last.then_inc(bt_mm, 1)
            pe.wait_ge(sh_in, 32)
            for c in range(KC):
                nc.tensor.transpose(bank(4)[:, RANK * c:RANK * c + RANK], las_nat[:, P * c:P * c + P],
                                    ident[0:RANK, 0:RANK])
            for o in range(KC):
                last = nc.tensor.transpose(bank(5)[0:RANK, P * o:P * o + P], lbs_nat[:, o, :], ident[:, :])
            last.then_inc(sh_mm, 1)
            pe.wait_ge(gsel_ok, 1)
            pe.wait_ge(la_in, 16)
            pe.wait_ge(acc_ok, 8 * NQ)
            for c in range(KC):
                for k in range(4):
                    last = mm(bank(6 + c // 2)[:, 256 * (c % 2):256 * (c % 2) + 256],
                              la_nat[:, k, P * c:P * c + P], gate_sel[:, k, :, :], start=(k == 0), stop=(k == 3))
            last.then_inc(ae_mm, 1)
            pe.wait_ge(bt_ok, 4)
            for n in range(2):
                for k in range(4):
                    last = mm(bank(n), gate_sel[:, k, 4 * n:4 * n + 4, :], b_t[:, k, :], start=(k == 0), stop=(k == 3))
            last.then_inc(be_mm, 1)

            pe.wait_ge(x2p_ok, KC)
            for s in range(SEQ):
                if s % 4 == 0:
                    u = s // 4
                    if u >= 2:
                        pe.wait_ge(y_ok, u - 1)
                    if s == 0:
                        pe.wait_ge(toep_in0, 16)
                    if s == 16:
                        pe.wait_ge(toep_in1, 16)
                toep = toep0 if s < 16 else toep1
                for d in range(KC):
                    last = mm(bank(2 + (s // 4) % 2)[:, P * (s % 4) + 32 * d:P * (s % 4) + P],
                              toep[:, s % 16, P * d:P * d + P], x2p[:, s, 0:KC - d, :],
                              start=(d == 0), stop=(d == KC - 1), skip_group_check=True)
                if s % 4 == 3:
                    last.then_inc(conv_mm, 1)

            def down(g):
                if g >= 2:
                    pe.wait_ge(ax_ok, g - 1)
                for c in range(KC):
                    last = mm(bank(4 + g % 2)[0:2 * RANK, 0:P], lora_a_t[:, c, g, :],
                              y_t[:, c, BPG * g:BPG * g + BPG, :], start=(c == 0), stop=(c == KC - 1))
                last.then_inc(ax_mm, 1)

            pe.wait_ge(y_ok, 8)
            pe.wait_ge(ae_ok, KC)
            pe.wait_ge(sh_ok, KC + 1)
            down(0)
            pe.wait_ge(ffn_in, 16)
            pe.wait_ge(flip_ok, 2)
            for g in range(G):
                o = bank(6 + g % 2)
                if g >= 2:
                    pe.wait_ge(out_ok, g - 1)
                for c in range(KC):
                    mm(o, y_t[:, c, BPG * g:BPG * g + BPG, :], ffn_sb[:, c, :], start=(c == 0), stop=False,
                       skip_group_check=True)
                for c in range(KC):
                    mm(o[:, P * c:P * c + P], acc[:, c, P * g:P * g + P], flip[:, :], start=False, stop=False,
                       skip_group_check=True)
                if g + 1 < G:
                    down(g + 1)
                pe.wait_ge(ax_ok, g + 1)
                if g == 0:
                    pe.wait_ge(ax_one, 1)
                    pe.wait_ge(bias_in, 16 * G)
                    pe.wait_ge(be_in, 16 * G)
                mm(o, ax[:, g % 2, :], lora_b_t[:, g, :], start=False, stop=True,
                   skip_group_check=True).then_inc(out_mm, 1)

        @block.scalar
        def _(act):
            sc = nc.scalar
            spacer = act.alloc_register("spacer")

            def here(index):
                if isinstance(index, int):
                    return index
                act.reg_mov(spacer, index)
                return act.snap(spacer, min_val=0, max_val=HEADS - 1)
            act.dma_start(cond_i[:], every_partition(cond_idx, BATCH)).then_inc(cond_in, 16)
            act.dma_start(cond_nat[:], cond_w.rearrange("(k j) c d -> (j c) k d", j=4)).then_inc(cond_in, 16)
            act.dma_start(prm_nat[:, 9, :], ssm_c.rearrange("h n two -> h (n two)")).then_inc(c_in, 16)
            for n, v in enumerate((bq, bk, gq, gk, bv)):
                act.dma_start(prm_nat[:, n, :], v.rearrange("(h d) -> h d", d=HD)).then_inc(prm_in, 16)
            for n, v in ((5, log_a), (6, a_im)):
                for k in range(2):
                    act.dma_start(prm_nat[:, n, NSTATE * k:NSTATE * k + NSTATE], v).then_inc(prm_in, 16)
            act.dma_start(bo_nat[:], bo.rearrange("(c p) -> c p", p=P)).then_inc(prm_in, 16)
            act.dma_start(small[:, SM["log_dt"], :], every_partition(log_dt, 32)).then_inc(misc_in, 16)
            act.dma_start(len_i[:], every_partition(lengths, BATCH)).then_inc(misc_in, 16)
            act.dma_start(gate_b[:].rearrange("p b n -> p (b n)"), every_partition(gate, G * NLORA)).then_inc(misc_in, 16)
            act.dma_start(d_row[:], every_partition(ssm_d, 32, 1)).then_inc(misc_in, 16)

            def split_hi(h, slot):
                for m in range(2):
                    last = sc.activation(w_hi[:, slot, m].rearrange("p c n -> p (c n)"),
                                         w_raw[:, slot, m].rearrange("p c n -> p (c n)"), ACT.Copy)
                last.then_inc(whi_ok, 1)

            act.wait_ge(w_in[0], 32)
            split_hi(0, 0)
            act.wait_ge(prm_mm, 1)
            sc.activation(params[:].rearrange("p n h -> p (n h)"), bank(0, 288), ACT.Copy)
            sc.activation(bo_t[:], bank(0)[:, 320:320 + KC], ACT.Copy).then_inc(prm_ok, 1)

            for g in range(G):
                act.wait_ge(mix_mm, g + 1)
                sc.activation(mix_hi[:, :, P * g:P * g + P],
                              bank(2 + g % 6).rearrange("p (c t) -> p c t", c=KC), ACT.Copy).then_inc(mixhi_ok, 1)

            def head(h, slot, first=False, last_head=False, w_count=None):
                if not last_head:
                    act.wait_ge(w_in[1 - slot], w_count)
                    if not first:
                        act.wait_ge(k_mm, h * 2)
                    split_hi(h + 1, 1 - slot)
                for n in range(2):
                    tok = slice(HALF * n, HALF * n + HALF)
                    act.wait_ge(q_mm, h * 2 + n + 1)
                    if n == 0 and not (isinstance(h, int) and h < 2):
                        act.wait_ge(sum_ok, h * 2 - 2)
                    at = here(h)
                    sc.activation(sq[:, slot, 0, tok], bank(n), ACT.Square,
                                  bias=params[:, PARAM["bq"], bass.ds(at, 1)]).then_inc(q_sq, 1)
                for n in range(2):
                    tok = slice(HALF * n, HALF * n + HALF)
                    act.wait_ge(k_mm, h * 2 + n + 1)
                    at = here(h)
                    sc.activation(sq[:, slot, 1, tok], bank(2 + n), ACT.Square,
                                  bias=params[:, PARAM["bk"], bass.ds(at, 1)]).then_inc(k_sq, 1)
                    if n == 0 and not (isinstance(h, int) and h < 2):
                        act.wait_ge(s_mm, h - 1)
                    at = here(h)
                    sc.activation(qk_sb[:, slot, 1, tok], bank(2 + n), ACT.Identity,
                                  bias=params[:, PARAM["bk"], bass.ds(at, 1)]).then_inc(k_ok, 1)

            def heads(lo, hi):
                with act.Fori(lo, hi) as i:
                    head(i * 2, 0, w_count=i * 32 + 32)
                    head(i * 2 + 1, 1, w_count=i * 32 + 64)

            head(0, 0, first=True, w_count=32)
            head(1, 1, w_count=64)
            heads(1, 12)
            act.wait_ge(ang_ok, 1)
            sc.activation(sm("thx"), sm("xr"), ACT.Tanh, scale=0.5).then_inc(fn_ok, 1)
            sc.activation(ang[:], ang[:], ACT.Sin).then_inc(fn_ok, 1)
            heads(12, HEADS // 2 - 1)
            head(HEADS - 2, 0, w_count=16 * HEADS)
            act.wait_ge(kern_mm, 1)
            act.wait_ge(kern_d, 1)
            sc.activation(k_sb[:].rearrange("a h c -> a (h c)"), bank(6, 1024)[0:CA, :], ACT.Copy).then_inc(kern_ok, 1)
            act.wait_ge(wv_in, 16)
            sc.activation(wv_hi[:].rearrange("p c n -> p (c n)"), wv_raw[:].rearrange("p c n -> p (c n)"),
                          ACT.Copy).then_inc(wvhi_ok, 1)
            head(HEADS - 1, 1, last_head=True)

            def value_out(t, g):
                act.wait_ge(v_mm, t * G + (g + 1))
                sc.activation(v_sb[:, g, :], bank(g % 2), ACT.Copy).then_inc(v_ok, 1)

            def exp_scores(t):
                act.wait_ge(soft, t * 6 + 3)
                sc.activation(sm_e[:], sm_s[:], ACT.Exp).then_inc(e_ok, 1)

            def attn_out(t):
                for u in range(8):
                    h, half = u // 2, u % 2
                    act.wait_ge(pv_mm, t * 8 + (u + 1))
                    at = here(t * QUAD + h)
                    sc.activation(attn_hi[:, h, HALF * half:HALF * half + HALF], bank(2 + u % 4), ACT.Identity,
                                  bias=params[:, PARAM["bv"], bass.ds(at, 1)]).then_inc(ahi_ok, 1)

            def split_o(t):
                act.wait_ge(wo_in, t * 16 + 16)
                sc.activation(chunks_backwards(wo_hi), wo_raw[:].rearrange("p h (c n) -> p (h c) n", n=P),
                              ACT.Copy).then_inc(wohi_ok, 1)

            def split_v(t):
                act.wait_ge(wv_in, t * 16 + 16)
                act.wait_ge(v_mm, t * G)
                sc.activation(wv_hi[:].rearrange("p c n -> p (c n)"), wv_raw[:].rearrange("p c n -> p (c n)"),
                              ACT.Copy).then_inc(wvhi_ok, 1)

            value_out(0, 0)
            value_out(0, 1)
            act.wait_ge(norm, 1)
            sc.activation(var_k[:], inv_norm[:], ACT.Sqrt).then_inc(std_ok, 1)
            for g in range(2, 6):
                value_out(0, g)
            exp_scores(0)
            for g in range(6, G):
                value_out(0, g)
            split_v(1)
            for u in range(8):
                c, half = u // 2, u % 2
                act.wait_ge(xt_mm, u + 1)
                if u == 0:
                    act.wait_ge(kern_mm, 1)
                sc.activation(acc[:, c, HALF * half:HALF * half + HALF], bank(2 + u % 4), ACT.Identity,
                              bias=bo_t[:, c:c + 1]).then_inc(xt_ok, 1)

            def quad(t):
                attn_out(t)
                split_o(t)
                for g in range(5):
                    value_out(t + 1, g)
                exp_scores(t + 1)
                for g in range(5, G):
                    value_out(t + 1, g)

            quad(0)
            split_v(2)
            with act.Fori(1, NQ - 2) as t:
                quad(t)
                split_v(t + 2)
            quad(NQ - 2)
            attn_out(NQ - 1)
            split_o(NQ - 1)

            for n in range(2):
                act.wait_ge(acc_ok, 8 * (NQ - 1) + 2 * n + 2)
                sc.activation(x2p[:, :, n, :], acc[:, n, :].rearrange("p (b s) -> p s b", s=SEQ),
                              ACT.Copy).then_inc(x2p_ok, 1)
            for c in range(4):
                act.wait_ge(bt_mm, c + 1)
                sc.activation(b_t[:, c, :], bank(c), ACT.Copy).then_inc(bt_ok, 1)
            act.wait_ge(sh_mm, 1)
            for c in range(KC):
                sc.activation(lora_a_t[:, c, :, 0:RANK], repeat(bank(4)[:, RANK * c:RANK * c + RANK], 1, G),
                              ACT.Copy).then_inc(sh_ok, 1)
            sc.activation(lora_b_t[0:RANK, :, :], repeat(bank(5)[0:RANK, :], 1, G), ACT.Copy).then_inc(sh_ok, 1)
            for g in range(G):
                act.wait_ge(out_mm, g + 1)
                if g >= 2:
                    act.wait_ge(out_dma[g % 2], 16 * (g // 2))
                sc.activation(o_stage[:, g % 2, :], bank(6 + g % 2), ACT.Copy).then_inc(out_ok, 1)

        @block.vector
        def _(dve):
            v = nc.vector
            v.memset(mix_w[:], 0.0).then_inc(zero_ok, 1)
            dve.wait_ge(cond_in, 32)
            v.tensor_copy(cond_f[:], cond_i[:]).then_inc(condf_ok, 1)
            dve.wait_ge(condf_ok, 1)
            dve.wait_ge(sel_const, 4)
            for k in range(4):
                last = v.tensor_scalar(onehot[:, k, :], cond_f[:], rowgrp[:, k:k + 1], None, ALU.is_equal)
            last.then_inc(hot_ok, 1)
            dve.wait_ge(hot_ok, 1)
            dve.wait_ge(delta_ok, 4)
            for k in range(4):
                v.tensor_tensor(select[:, k], repeat(onehot[:, k, :], 2, 32), repeat(delta32[:], 1, BATCH),
                                ALU.mult).then_inc(sel_ok, 1)

            def split_lo(h, slot):
                dve.wait_ge(whi_ok, h + 1)
                for m in range(2):
                    last = v.tensor_tensor(w_lo[:, slot, m].rearrange("p c n -> p (c n)"),
                                           w_raw[:, slot, m].rearrange("p c n -> p (c n)"),
                                           w_hi[:, slot, m].rearrange("p c n -> p (c n)").bitcast(F32), ALU.subtract)
                last.then_inc(wlo_ok, 1)

            dve.wait_ge(mixw_mm, 1)
            dve.wait_ge(zero_ok, 2)
            for b in range(BPG):
                last = v.tensor_copy(mix_w[quadrant(b), :, quadrant(b)],
                                     bank(1, 256)[quadrant(b), :].rearrange("p (g d) -> p g d", g=G))
            last.then_inc(mixw_ok, 1)
            split_lo(0, 0)
            for g in range(G):
                tok = slice(P * g, P * g + P)
                dve.wait_ge(mixhi_ok, g + 1)
                v.tensor_tensor(mix_lo[:, :, tok], bank(2 + g % 6).rearrange("p (c t) -> p c t", c=KC),
                                mix_hi[:, :, tok].bitcast(F32), ALU.subtract).then_inc(mixlo_ok, 1)

            def extract(h):
                dve.wait_ge(s_mm, h + 1)
                dst = scores[:].rearrange("p h g k -> p (h g k)")[:, bass.ds(h * (G * 32), G * 32)]
                for b in range(BPG):
                    src = bank(4, 1024)[quadrant(b), :].rearrange("p (g k) -> p g k", g=G)[:, :, quadrant(b)]
                    last = v.tensor_copy(dst[quadrant(b), :].rearrange("p (g k) -> p g k", g=G), src)
                last.then_inc(s_ok, 1)

            def head(h, slot, first=False, last_head=False):
                if not last_head:
                    if not first:
                        dve.wait_ge(k_mm, h * 2)
                    split_lo(h + 1, 1 - slot)
                for n in range(2):
                    tok = slice(HALF * n, HALF * n + HALF)
                    dve.wait_ge(q_sq, h * 2 + n + 1)
                    if n == 0 and not (isinstance(h, int) and h < 2):
                        dve.wait_ge(s_mm, h - 1)
                    v.tensor_scalar(qk_sb[:, slot, 0, tok], bank(n), params[:, PARAM["bq"], bass.ds(h, 1)],
                                    gqk[:, bass.ds(h, 1)], ALU.add, ALU.mult).then_inc(q_ok, 1)
                    if n == 0 and not first:
                        if isinstance(h, int) and h == 1:
                            dve.wait_ge(mask_ok, 1)
                            dve.wait_ge(gatep_ok, 4)
                        extract(h - 1)
                for m, done in enumerate((q_sq, k_sq)):
                    if m == 1:
                        dve.wait_ge(done, h * 2 + 2)
                    if not first:
                        dve.wait_ge(sum_ok, h * 2 + (m - 1))
                    v.tensor_tensor(sumsq[:, m, :], sumsq[:, m, :], sq[:, slot, m, :], ALU.add).then_inc(sum_ok, 1)

            dve.wait_ge(gqk_ok, 1)
            head(0, 0, first=True)
            head(1, 1)
            with dve.Fori(1, HEADS // 2 - 1) as i:
                for j in range(2):
                    head(i * 2 + j, j)
            head(HEADS - 2, 0)

            def split_v(t, parts=(0, 1, 2, 3)):
                if 0 in parts:
                    dve.wait_ge(wvhi_ok, t + 1)
                for c in parts:
                    last = v.tensor_tensor(wv_lo[:, c, :], wv_raw[:, c, :], wv_hi[:, c, :].bitcast(F32), ALU.subtract)
                if KC - 1 in parts:
                    last.then_inc(wvlo_ok, 1)

            split_v(0)
            head(HEADS - 1, 1, last_head=True)
            extract(HEADS - 1)

            dve.wait_ge(vk_mm, 1)
            for b in range(BPG):
                src = bank(6, 1024)[quadrant(b), :].rearrange("p (g k) -> p g k", g=G)[:, :, quadrant(b)]
                v.tensor_scalar(var_k[quadrant(b)], src, 1.0 / INNER, RMS_EPS, ALU.mult, ALU.add).then_inc(var_ok, 1)
            dve.wait_ge(vq_mm, 1)
            v.tensor_scalar(var_q[:], bank(2, G), 1.0 / INNER, RMS_EPS, ALU.mult, ALU.add).then_inc(var_ok, 1)
            dve.wait_ge(var_ok, 5)
            v.scalar_tensor_tensor(inv_norm[:], var_k[:], float(HD), repeat(var_q[:], 2, 32),
                                   ALU.mult, ALU.mult).then_inc(norm, 1)
            dve.wait_ge(std_ok, 1)
            tmp = sm_s[:, 0]
            dve.wait_ge(kpad_out, 32)
            v.reciprocal(tmp, var_k[:]).then_inc(norm, 1)
            dve.wait_ge(norm, 2)
            v.tensor_tensor(tmp, tmp, inv_norm[:], ALU.mult).then_inc(norm, 1)
            dve.wait_ge(norm, 3)
            v.tensor_tensor(tmp, tmp, var_k[:], ALU.add).then_inc(norm, 1)
            dve.wait_ge(norm, 4)
            v.tensor_scalar(tmp, tmp, 0.5, None, ALU.mult).then_inc(norm, 1)
            dve.wait_ge(norm, 5)
            v.reciprocal(inv_norm[:], tmp).then_inc(norm, 1)
            dve.wait_ge(norm, 6)

            def flat(tile):
                return tile[:].rearrange("p h g k -> p (h g) k")

            def soft_max(t):
                src = scores[:].rearrange("p h g k -> p (h g k)")[:, bass.ds(t * (QUAD * G * 32), QUAD * G * 32)]
                v.tensor_tensor(sm_s[:].rearrange("p h g k -> p h (g k)"),
                                src.rearrange("p (h n) -> p h n", h=QUAD),
                                repeat(inv_norm[:].rearrange("p g k -> p (g k)"), 1, QUAD), ALU.mult).then_inc(soft, 1)
                dve.wait_ge(soft, t * 6 + 1)
                v.tensor_reduce(row_max[:], flat(sm_s), AX_X, ALU.max).then_inc(soft, 1)
                dve.wait_ge(soft, t * 6 + 2)
                v.tensor_tensor(flat(sm_s), flat(sm_s), repeat(row_max[:], 2, 32), ALU.subtract).then_inc(soft, 1)

            def soft_norm(t):
                dve.wait_ge(e_ok, t + 1)
                v.tensor_reduce(row_sum[:], flat(sm_e), AX_X, ALU.add).then_inc(soft, 1)
                dve.wait_ge(soft, t * 6 + 4)
                v.reciprocal(row_inv[:], row_sum[:]).then_inc(soft, 1)
                dve.wait_ge(soft, t * 6 + 5)
                v.tensor_tensor(flat(sm_e), flat(sm_e), repeat(row_inv[:], 2, 32), ALU.mult).then_inc(soft, 1)
                dve.wait_ge(soft, t * 6 + 6)
                dve.wait_ge(pv_mm, t * 8) if not isinstance(t, int) or t > 0 else None
                for b in range(BPG):
                    last = v.transpose(p_blocks[quadrant(b), :, :, quadrant(b)].rearrange("p h g q -> p (h g) q"),
                                       sm_e[quadrant(b)].rearrange("p h g k -> p (h g) k"))
                last.then_inc(p_ok, 1)

            soft_max(0)
            dve.wait_ge(blocks_zero, 1)
            soft_norm(0)
            split_v(1)

            def attn_out(t):
                for u in range(8):
                    h, half = u // 2, u % 2
                    tok = slice(HALF * half, HALF * half + HALF)
                    dve.wait_ge(ahi_ok, t * 8 + (u + 1))
                    v.scalar_tensor_tensor(attn_lo[:, h, tok], bank(2 + u % 4),
                                           params[:, PARAM["bv"], bass.ds(t * QUAD + h, 1)],
                                           attn_hi[:, h, tok].bitcast(F32), ALU.add, ALU.subtract).then_inc(alo_ok, 1)

            def split_o(t):
                dve.wait_ge(wohi_ok, t + 1)
                v.tensor_tensor(chunks_backwards(wo_lo), wo_raw[:].rearrange("p h (c n) -> p (h c) n", n=P),
                                chunks_backwards(wo_hi).bitcast(F32), ALU.subtract).then_inc(wolo_ok, 1)

            def accumulate(t, units, first=False):
                for u in units:
                    c, half = u // 2, u % 2
                    dve.wait_ge(wo_mm, t * 8 + (u + 1))
                    if not first:
                        dve.wait_ge(acc_ok, t * 8 + (u - 7))
                    part = acc[:, c, HALF * half:HALF * half + HALF]
                    v.tensor_tensor(part, bank(6 + u % 2), part, ALU.add).then_inc(acc_ok, 1)

            def quad(t, first=False, split=True):
                attn_out(t)
                split_o(t)
                soft_max(t + 1)
                soft_norm(t + 1)
                accumulate(t, (0, 1, 2), first)
                for c in range(KC):
                    if split:
                        split_v(t + 2, (c,))
                    accumulate(t, (3 + c,), first)
                accumulate(t, (7,), first)

            dve.wait_ge(xt_ok, 8)
            quad(0, first=True)
            with dve.Fori(1, NQ - 2) as t:
                quad(t)
            quad(NQ - 2, split=False)
            attn_out(NQ - 1)
            split_o(NQ - 1)
            accumulate(NQ - 1, range(8))

            dve.wait_ge(acc_ok, 8 * NQ)
            for n in range(2, KC):
                v.tensor_copy(x2p[:, :, n, :], acc[:, n, :].rearrange("p (b s) -> p s b", s=SEQ)).then_inc(x2p_ok, 1)
            dve.wait_ge(ae_mm, 1)
            for c in range(KC):
                v.tensor_copy(lora_a_t[:, c, :, RANK:2 * RANK],
                              bank(6 + c // 2)[:, 256 * (c % 2):256 * (c % 2) + 256]
                              .rearrange("p (g r) -> p g r", g=G)).then_inc(ae_ok, 1)
            dve.wait_ge(be_mm, 1)
            for n in range(2):
                v.tensor_copy(b_eff[:, n, :], bank(n)).then_inc(be_ok, 1)
            dve.wait_ge(mask_ok, 1)
            for u in range(8):
                dve.wait_ge(conv_mm, u + 1)
                for c in range(KC):
                    src = bank(2 + u % 2).rearrange("p (s c b) -> p s c b", s=4, c=KC)[:, :, c, :]
                    last = v.tensor_tensor(y_t[:, c, :, 4 * u:4 * u + 4].rearrange("p b s -> p s b"), src,
                                           repeat(mask[:, c, :], 1, 4), ALU.mult)
                last.then_inc(y_ok, 1)
            for g in range(G):
                dve.wait_ge(ax_mm, g + 1)
                if g >= 2:
                    dve.wait_ge(out_mm, g - 1)
                v.tensor_copy(ax[0:2 * RANK, g % 2, :], bank(4 + g % 2)[0:2 * RANK, 0:P]).then_inc(ax_ok, 1)


_INS = [("x", "x", (TOK, FEAT), F32), ("cond_idx", "itok_B_0_15", (BATCH,), I32),
        ("lengths", "itok_B_78_3631", (BATCH,), I32), ("cond_w", "L0_cond_weights", (NCOND, 32, 32), F32),
        ("wq", "L0_attn_Wq", (FEAT, INNER), F32), ("bq", "L0_attn_bq", (INNER,), F32),
        ("wk", "L0_attn_Wk", (FEAT, INNER), F32), ("bk", "L0_attn_bk", (INNER,), F32),
        ("wv", "L0_attn_Wv", (FEAT, INNER), F32), ("bv", "L0_attn_bv", (INNER,), F32),
        ("wo", "L0_attn_Wo", (INNER, FEAT), F32), ("bo", "L0_attn_bo", (FEAT,), F32),
        ("gq", "L0_attn_gq", (INNER,), F32), ("gk", "L0_attn_gk", (INNER,), F32),
        ("log_dt", "L0_cond2_log_dt", (SEQ,), F32), ("ssm_c", "L0_cond2_C", (SEQ, NSTATE, 2), F32),
        ("log_a", "L0_cond2_log_A_real", (SEQ, NSTATE), F32), ("a_im", "L0_cond2_A_imag", (SEQ, NSTATE), F32),
        ("ssm_d", "L0_cond2_D", (SEQ,), F32), ("gate", "L0_ffn_gate", (G, NLORA), F32),
        ("ffn_w", "L0_ffn_kernel", (FEAT, FEAT), F32), ("ffn_b", "L0_ffn_bias", (FEAT,), F32),
        ("lora_a", "L0_ffn_lora_A", (NLORA, RANK, FEAT), F32), ("lora_b", "L0_ffn_lora_B", (NLORA, FEAT, RANK), F32),
        ("lora_as", "L0_ffn_lora_A_shared", (RANK, FEAT), F32), ("lora_bs", "L0_ffn_lora_B_shared", (FEAT, RANK), F32)]


def kernel(**inputs):
    import numpy as np
    import concourse.bacc as bacc
    from concourse.bass_utils import run_bass_kernel_spmd

    nc = bacc.Bacc("TRN2", target_bir_lowering=False, num_devices=1)
    arrays, args = {}, {}
    for name, key, shape, dt in _INS:
        arrays[f"in_{name}"] = np.ascontiguousarray(inputs[key]).reshape(shape)
        args[name] = nc.dram_tensor(f"in_{name}", shape, dt, kind="ExternalInput").ap()
    args["kpad"] = nc.dram_tensor("kpad_dram", (SEQ, PADL), F32, kind="Internal").ap()
    args["out"] = nc.dram_tensor("out_dram", (TOK, FEAT), F32, kind="ExternalOutput").ap()
    build_program(nc, **args)
    result = run_bass_kernel_spmd(nc, [arrays], core_ids=[0])
    return result.results[0]["out_dram"].reshape(BATCH, SEQ, FEAT)
```

```python
from contextlib import ExitStack

import concourse.bass as bass
from concourse import mybir

F32 = mybir.dt.float32
F32R = mybir.dt.float32r
I32 = mybir.dt.int32
ALU = mybir.AluOpType
ACT = mybir.ActivationFunctionType
AX_X = mybir.AxisListType.X

P = 128
BATCH, SEQ, FEAT = 32, 32, 512
TOK = BATCH * SEQ
HEADS, HD = 32, 128
INNER = HEADS * HD
KC = FEAT // P
G = TOK // P
BPG = P // SEQ
HALF = TOK // 2
QUAD = 4
NQ = HEADS // QUAD
NCOND, NLORA, RANK = 16, 16, 32
NSTATE = 64
CL, CA = 32, FEAT // 32
PADL = P + FEAT
RMS_EPS = 1e-6
PI = 3.141592653589793
C1 = 6.28125
C2 = 0.0019350051879882812
C3 = 2 * PI - C1 - C2
MAGIC = 12582912.0
PI_F32 = 3.1415925
LN2_HI, LN2_LO = 0.693359375, -2.12194440e-4
EXP_COEFFS = [1 / 5040, 1 / 720, 1 / 120, 1 / 24, 1 / 6, 1 / 2, 1.0, 1.0]


def build_program(nc, x, cond_idx, lengths, cond_w, wq, bq, wk, bk, wv, bv, wo, bo, gq, gk,
                  log_dt, ssm_c, log_a, a_im, ssm_d, gate, ffn_w, ffn_b, lora_a, lora_b,
                  lora_as, lora_bs, kpad, out):
    ctx = ExitStack()
    with ctx:
        def sb(name, shape, dt=F32, scope=ctx):
            return scope.enter_context(nc.sbuf_tensor(name, shape, dt))

        def sem(name):
            return ctx.enter_context(nc.semaphore(name))

        def overlay(*lots):
            made = []
            for n, lot in enumerate(lots):
                scope = ctx if n == len(lots) - 1 else ExitStack()
                made.append([sb(name, shape, dt, scope) for name, shape, dt in lot])
                if scope is not ctx:
                    scope.close()
            return made

        psum = ctx.enter_context(nc.psum_tensor("psum", [P, 8 * 512], F32))

        def bank(n, width=512):
            return psum[:, n * 512:n * 512 + width]

        ident = sb("ident", [P, P])
        ones = sb("ones", [P, P])
        delta32 = sb("delta32", [P, 32])
        params = sb("params", [P, 9, 32])
        gqk = sb("gqk", [P, HEADS])
        inv_norm = sb("inv_norm", [P, G, 32])
        var_k = sb("var_k", [P, G, 32])
        var_q = sb("var_q", [P, G])
        row_max = sb("row_max", [P, QUAD * G])
        row_sum = sb("row_sum", [P, QUAD * G])
        row_inv = sb("row_inv", [P, QUAD * G])
        lidx = sb("lidx", [P, KC])
        mask = sb("mask", [P, KC, BATCH])
        gate_p = sb("gate_p", [P, 4, G])
        d_row = sb("d_row", [1, 32])
        PARAM = dict(bq=0, bk=1, gq=2, gk=3, bv=4, log_a=5, a_im=6, c_re=7, c_im=8)

        def param(name):
            return params[:, PARAM[name], :]

        (toep1,), (mix_hi, mix_lo) = overlay(
            [("toep1", [P, 16, 512], F32)],
            [("mix_hi", [P, KC, TOK], F32R), ("mix_lo", [P, KC, TOK], F32R)])
        (mix_w, mix_t, cond_nat, cond_i, cond_f, cond_no, onehot, prm_nat, delta, len_i, len_f, gate_b), (toep0,), (scores,) = overlay(
            [("mix_w", [P, G, P], F32), ("mix_t", [P, 32, BATCH], F32), ("cond_nat", [NCOND, 32 * 32], F32),
             ("cond_i", [NCOND, BATCH], I32), ("cond_f", [NCOND, BATCH], F32), ("cond_no", [NCOND, 1], F32),
             ("onehot", [NCOND, BPG, BATCH], F32),
             ("prm_nat", [32, 10, P], F32), ("delta", [P, BPG, 32], F32),
             ("len_i", [P, BATCH], I32), ("len_f", [P, BATCH], F32), ("gate_b", [P, G, NLORA], F32)],
            [("toep0", [P, 16, 512], F32)],
            [("scores", [P, HEADS, G, 32], F32)])
        (ang, expo, mult, quarter), (acc,) = overlay(
            [("ang", [P, 67, 32], F32), ("expo", [P, 48, 32], F32), ("mult", [P, 67], F32),
             ("quarter", [P, 67], F32)],
            [("acc", [P, G, FEAT], F32)])
        (turns, prod), (k_sb, kzero, bo_rows), (gate_sel,), (sm_s, sm_e) = overlay(
            [("turns", [P, 32, 32], F32), ("prod", [P, 32, 32], F32)],
            [("k_sb", [CA, 32, CL], F32), ("kzero", [32, P], F32), ("bo_rows", [P, FEAT], F32)],
            [("gate_sel", [P, 4, G, RANK], F32)],
            [("sm_s", [P, QUAD, G, 32], F32), ("sm_e", [P, QUAD, G, 32], F32)])
        (lb_nat,), (wv_raw,) = overlay([("lb_nat", [P, KC, NLORA * RANK], F32)], [("wv_raw", [P, KC, 512], F32)])
        (la_nat,), (wv_hi,) = overlay([("la_nat", [P, 4, FEAT], F32)], [("wv_hi", [P, KC, 512], F32R)])
        (ffn_sb,), (wv_lo,) = overlay([("ffn_sb", [P, KC, FEAT], F32)], [("wv_lo", [P, KC, 512], F32R)])
        wo_raw = sb("wo_raw", [P, QUAD, FEAT])
        ((w_hi, w_lo, sq, qk_sb, x_nat, sumsq, w_raw),
         (x2p, y_t, lora_a_t, lora_b_t, b_eff, b_t, ax, o_stage, las_nat, lbs_nat),
         (v_sb, p_blocks, attn_hi, attn_lo, wo_hi, wo_lo)) = overlay(
            [("w_hi", [P, 2, 2, KC, HD], F32R), ("w_lo", [P, 2, 2, KC, HD], F32R),
             ("sq", [P, 2, 2, TOK], F32), ("qk_sb", [P, 2, 2, TOK], F32), ("x_nat", [P, G, FEAT], F32),
             ("sumsq", [P, 2, TOK], F32), ("w_raw", [P, 2, 2, KC, HD], F32)],
            [("x2p", [P, SEQ, KC, BATCH], F32), ("y_t", [P, KC, BATCH, SEQ], F32),
             ("lora_a_t", [P, KC, G, 2 * RANK], F32), ("lora_b_t", [2 * RANK + 1, G, FEAT], F32),
             ("b_eff", [P, 2, FEAT], F32), ("b_t", [P, 4, FEAT], F32), ("ax", [2 * RANK + 1, 2, P], F32),
             ("o_stage", [P, 2, FEAT], F32), ("las_nat", [RANK, FEAT], F32), ("lbs_nat", [P, KC, RANK], F32)],
            [("v_sb", [P, G, 512], F32), ("p_blocks", [P, QUAD, G, P], F32),
             ("attn_hi", [P, QUAD, TOK], F32R), ("attn_lo", [P, QUAD, TOK], F32R),
             ("wo_hi", [P, QUAD, FEAT], F32R), ("wo_lo", [P, QUAD, FEAT], F32R)])
        small = sb("small", [P, 16, 32])
        SM = {n: i for i, n in enumerate("log_dt dt ea xr th den rden thx ex t0 t1 er ei nr ni t2".split())}
        SM["cr2"], SM["ci2"] = SM["xr"], SM["th"]

        def sm(name, lo=0, hi=P):
            return small[lo:hi, SM[name], :]

        x_in = [sem(f"x_in{n}") for n in range(4)]
        cond_in, prm_in, c_in, misc_in = sem("cond_in"), sem("prm_in"), sem("c_in"), sem("misc_in")
        c_dup = sem("c_dup")
        const_ok, sel_const, delta_ok = sem("const_ok"), sem("sel_const"), sem("delta_ok")
        condf_ok, hot_ok, mixt_ok = sem("condf_ok"), sem("hot_ok"), sem("mixt_ok")
        zero_ok, sumsq_set = sem("zero_ok"), sem("sumsq_set")
        prm_mm, prm_ok = sem("prm_mm"), sem("prm_ok")
        mixw_mm, mixw_ok = sem("mixw_mm"), sem("mixw_ok")
        mix_mm, mixhi_ok, mixlo_ok = sem("mix_mm"), sem("mixhi_ok"), sem("mixlo_ok")
        gqk_ok = sem("gqk_ok")
        w_in = [sem("w_in0"), sem("w_in1")]
        whi_ok, wlo_ok = sem("whi_ok"), sem("wlo_ok")
        q_mm, k_mm, s_mm = sem("q_mm"), sem("k_mm"), sem("s_mm")
        q_sq, k_sq, q_ok, k_ok, s_ok, sum_ok = (sem(n) for n in ("q_sq", "k_sq", "q_ok", "k_ok", "s_ok", "sum_ok"))
        ssm, ang_ok, fn_ok, tab_ok = (sem(n) for n in ("ssm", "ang_ok", "fn_ok", "tab_ok"))
        kern_mm, kern_ok, kern_d, kpad_out = sem("kern_mm"), sem("kern_ok"), sem("kern_d"), sem("kpad_out")
        vk_mm, vq_mm, var_ok, std_ok, norm = (sem(n) for n in ("vk_mm", "vq_mm", "var_ok", "std_ok", "norm"))
        bo_in, acc_set = sem("bo_in"), sem("acc_set")
        wv_in, wo_in = sem("wv_in"), sem("wo_in")
        wvhi_ok, wvlo_ok, wohi_ok, wolo_ok = sem("wvhi_ok"), sem("wvlo_ok"), sem("wohi_ok"), sem("wolo_ok")
        v_mm, v_ok, pv_mm, ahi_ok, alo_ok = (sem(n) for n in ("v_mm", "v_ok", "pv_mm", "ahi_ok", "alo_ok"))
        wo_mm, acc_ok = sem("wo_mm"), sem("acc_ok")
        blocks_zero, soft, e_ok, p_ok = sem("blocks_zero"), sem("soft"), sem("e_ok"), sem("p_ok")
        toep_in0, toep_in1, lb_in, la_in, ffn_in, sh_in = (sem(n) for n in ("toep_in0", "toep_in1", "lb_in", "la_in", "ffn_in", "sh_in"))
        bias_in, xt_mm = sem("bias_in"), sem("xt_mm")
        gatep_ok, gsel_ok, mask_ok = sem("gatep_ok"), sem("gsel_ok"), sem("mask_ok")
        x2p_ok, bt_mm, bt_ok, sh_mm, sh_ok = (sem(n) for n in ("x2p_ok", "bt_mm", "bt_ok", "sh_mm", "sh_ok"))
        ae_mm, ae_ok, be_mm, be_ok, be_in = (sem(n) for n in ("ae_mm", "ae_ok", "be_mm", "be_ok", "be_in"))
        conv_mm, y_ok, ax_one, ax_mm, ax_ok = (sem(n) for n in ("conv_mm", "y_ok", "ax_one", "ax_mm", "ax_ok"))
        out_mm, out_ok = sem("out_mm"), sem("out_ok")
        out_dma = [sem("out_dma0"), sem("out_dma1")]

        x_rows = x.rearrange("(g p) f -> p g f", p=P)
        out_rows = out.rearrange("(g p) f -> g p f", p=P)
        wqk_cols = [w.rearrange("(c p) n -> p c n", p=P) for w in (wq, wk)]
        wv_cols = wv.rearrange("(c p) n -> p c n", p=P)
        wo_rows = wo.rearrange("(h d) n -> d h n", d=HD)

        def every_partition(ap, n, parts=P):
            return bass.AP(ap.tensor, 0, [[0, parts], [1, n]])

        def repeat(ap, axis, n):
            dims = [list(d) for d in ap.ap]
            dims.insert(axis, [0, n])
            return bass.AP(ap.tensor, ap.offset, dims)

        def backwards(ap):
            dims = [list(d) for d in ap.ap]
            n = dims[-1][1]
            dims[-1] = [-1, n]
            return bass.AP(ap.tensor, ap.offset + n - 1, dims)

        def chunks_backwards(tile):
            return backwards(tile[:].rearrange("p h (c n) -> p (h c) n", n=P))

        def quadrant(b):
            return slice(32 * b, 32 * b + 32)

        block = ctx.enter_context(nc.Block())

        @block.sync
        def _(sp):
            def load_x(n):
                sp.dma_start(x_nat[:, 2 * n:2 * n + 2, :], x_rows[:, 2 * n:2 * n + 2, :]).then_inc(x_in[n], 16)

            load_x(0)
            load_x(1)

            def load_qk(h, slot):
                for m in range(2):
                    sp.dma_start(w_raw[:, slot, m], wqk_cols[m][:, :, bass.ds(h * HD, HD)]).then_inc(w_in[slot], 16)

            load_qk(0, 0)
            load_x(2)
            load_x(3)
            load_qk(1, 1)
            with sp.Fori(1, HEADS // 2) as i:
                for j in range(2):
                    sp.wait_ge(wlo_ok, i * 2 + (j - 1))
                    load_qk(i * 2 + j, j)

            def load_v(t):
                sp.dma_start(wv_raw[:], wv_cols[:, :, bass.ds(t * 512, 512)]).then_inc(wv_in, 16)

            def load_o(t):
                sp.dma_start(wo_raw[:], wo_rows[:, bass.ds(t * QUAD, QUAD), :]).then_inc(wo_in, 16)

            load_v(0)
            load_o(0)
            sp.wait_ge(kern_d, 2)
            sp.dma_start(kpad[:, 0:P], kzero[:, :]).then_inc(kpad_out, 16)
            sp.dma_start(kpad[:, P:].rearrange("h (a c) -> a h c", a=CA), k_sb[:]).then_inc(kpad_out, 16)
            with sp.Fori(1, NQ) as t:
                sp.wait_ge(wvlo_ok, t)
                load_v(t)
                sp.wait_ge(wolo_ok, t)
                load_o(t)
            sp.wait_ge(kpad_out, 32)
            sp.wait_ge(soft, 6 * (NQ - 1) + 1)
            sp.dma_start(toep0[:], bass.AP(kpad.tensor, 1, [[1, P], [PADL, 16], [1, 512]])).then_inc(toep_in0, 16)
            sp.wait_ge(wvlo_ok, NQ)
            for c in range(KC):
                sp.dma_start(lb_nat[:, c, :].rearrange("p (n r) -> p n r", n=NLORA),
                             lora_b.rearrange("n (c p) r -> c p n r", p=P)[c]).then_inc(lb_in, 16)
            sp.wait_ge(v_mm, G * NQ)
            sp.dma_start(la_nat[:], lora_a.rearrange("(k j) r i -> (j r) k i", j=4)).then_inc(la_in, 16)
            sp.dma_start(toep1[:], bass.AP(kpad.tensor, 16 * PADL + 1, [[1, P], [PADL, 16], [1, 512]])).then_inc(toep_in1, 16)
            sp.dma_start(ffn_sb[:], ffn_w.rearrange("(c p) n -> p c n", p=P)).then_inc(ffn_in, 16)
            sp.wait_ge(wo_mm, G * NQ)
            sp.dma_start(las_nat[:], lora_as).then_inc(sh_in, 16)
            sp.dma_start(lbs_nat[:], lora_bs.rearrange("(c p) r -> p c r", p=P)).then_inc(sh_in, 16)
            for g in range(G):
                sp.dma_start(lora_b_t[2 * RANK:2 * RANK + 1, g, :], every_partition(ffn_b, FEAT, 1)).then_inc(bias_in, 16)
            sp.wait_ge(be_ok, 2)
            for g in range(G):
                sp.dma_start(lora_b_t[RANK:2 * RANK, g, :], b_eff[quadrant(g % 4), g // 4, :]).then_inc(be_in, 16)
            for g in range(G):
                sp.wait_ge(out_ok, g + 1)
                sp.dma_start(out_rows[g], o_stage[:, g % 2, :]).then_inc(out_dma[g % 2], 16)
            for n in range(2):
                sp.wait_ge(out_dma[n], 16 * G // 2)

        @block.gpsimd
        def _(pool):
            gp = nc.gpsimd
            gp.iota(cond_no[:], [[0, 1]], base=0, channel_multiplier=1,
                    allow_small_or_imprecise_dtypes=True).then_inc(sel_const, 1)
            pool.wait_ge(sel_const, 1)
            gp.memset(delta[:], 0.0).then_inc(delta_ok, 1)
            pool.wait_ge(delta_ok, 1)
            gp.affine_select(out=delta[:], in_=delta[:], compare_op=ALU.not_equal, fill=1.0, base=0,
                             pattern=[[-32, 4], [-1, 32]], channel_multiplier=1).then_inc(delta_ok, 1)
            pool.wait_ge(delta_ok, 2)
            gp.tensor_tensor(delta[:, 0:2, :], delta[:, 0:2, :], delta[:, 2:4, :], ALU.add).then_inc(delta_ok, 1)
            pool.wait_ge(delta_ok, 3)
            gp.tensor_tensor(delta32[:], delta[:, 0, :], delta[:, 1, :], ALU.add).then_inc(delta_ok, 1)
            gp.memset(ident[:], 0.0).then_inc(const_ok, 1)
            pool.wait_ge(const_ok, 1)
            gp.affine_select(out=ident[:], in_=ident[:], compare_op=ALU.not_equal, fill=1.0, base=0,
                             pattern=[[-1, P]], channel_multiplier=1).then_inc(const_ok, 1)
            pool.wait_ge(c_in, 16)
            for part in range(2):
                src = prm_nat[:, 9, :].rearrange("h (n two) -> h n two", two=2)[:, :, part]
                gp.tensor_copy(prm_nat[:, 7 + part, :].rearrange("h (d n) -> h d n", d=2),
                               repeat(src, 1, 2)).then_inc(c_dup, 1)
            gp.memset(ones[:], 1.0).then_inc(const_ok, 1)
            gp.memset(sumsq[:], 0.0).then_inc(sumsq_set, 1)

            pool.wait_ge(misc_in, 64)
            count = [0]

            def step(ins):
                count[0] += 1
                ins.then_inc(ssm, 1)
                pool.wait_ge(ssm, count[0])

            gp.iota(lidx[:], [[P, KC]], base=0, channel_multiplier=1, allow_small_or_imprecise_dtypes=True)
            step(gp.tensor_copy(len_f[:], len_i[:]))
            for c in range(KC):
                last = gp.tensor_scalar(mask[:, c, :], len_f[:], lidx[:, c:c + 1], None, ALU.is_gt)
            last.then_inc(mask_ok, 1)
            for j in range(4):
                gp.tensor_copy(gate_p[quadrant(j), :, :],
                               gate_b[quadrant(j), :, j::4].rearrange("p b k -> p k b")).then_inc(gatep_ok, 1)
                pool.wait_ge(gatep_ok, j + 1)
            pool.wait_ge(prm_ok, 1)
            gp.tensor_tensor(gqk[:], param("gq"), param("gk"), ALU.mult).then_inc(gqk_ok, 1)

            gp.iota(mult[:, 0:32], [[1, 32]], base=0, channel_multiplier=0, allow_small_or_imprecise_dtypes=True)
            gp.iota(mult[:, 32:64], [[0, 2], [32, 16]], base=0, channel_multiplier=0, allow_small_or_imprecise_dtypes=True)
            gp.memset(mult[:, 64:66], 1.0)
            step(gp.memset(mult[:, 66:67], 0.5))
            step(gp.memset(quarter[:], 0.0))
            step(gp.memset(quarter[0:64, 0:32], 0.25))
            step(gp.memset(quarter[:, 48:64], 0.25))
            step(gp.memset(quarter[:, 65:66], 0.25))
            def exp_in_place(x, k, poly):
                step(gp.tensor_scalar(x, x, 88.0, -87.0, ALU.min, ALU.max))
                step(gp.tensor_scalar(k, x, 1.4426950408889634, None, ALU.mult))
                step(gp.tensor_scalar(k, k, MAGIC, None, ALU.add))
                step(gp.tensor_scalar(k, k, -MAGIC, None, ALU.add))
                for part in (LN2_HI, LN2_LO):
                    step(gp.tensor_scalar(poly, k, -part, None, ALU.mult))
                    step(gp.tensor_tensor(x, x, poly, ALU.add))
                step(gp.tensor_scalar(poly, x, EXP_COEFFS[0], EXP_COEFFS[1], ALU.mult, ALU.add))
                for coeff in EXP_COEFFS[2:]:
                    step(gp.tensor_tensor(poly, poly, x, ALU.mult))
                    step(gp.tensor_scalar(poly, poly, coeff, None, ALU.add))
                step(gp.tensor_scalar(k, k, 127.0, None, ALU.add))
                step(gp.tensor_scalar(k.bitcast(I32), k, 8388608.0, None, ALU.mult))
                step(gp.tensor_tensor(x, poly, k, ALU.mult))

            step(gp.tensor_copy(sm("dt"), sm("log_dt")))
            exp_in_place(sm("dt"), sm("t0"), sm("t1"))
            step(gp.tensor_copy(sm("ea"), param("log_a")))
            exp_in_place(sm("ea"), sm("t0"), sm("t1"))
            step(gp.tensor_tensor(sm("t0"), sm("ea"), sm("dt"), ALU.mult))
            step(gp.tensor_scalar(sm("xr"), sm("t0"), -1.0, None, ALU.mult))
            step(gp.tensor_tensor(sm("th"), param("a_im"), sm("dt"), ALU.mult))
            step(gp.tensor_tensor(sm("t0"), sm("ea"), sm("ea"), ALU.mult))
            step(gp.tensor_tensor(sm("t1"), param("a_im"), param("a_im"), ALU.mult))
            step(gp.tensor_tensor(sm("den"), sm("t0"), sm("t1"), ALU.add))
            step(gp.memset(sm("t2"), -1.0))
            step(gp.tensor_tensor(sm("rden"), sm("den"), sm("t2"), ALU.pow))
            step(gp.tensor_copy(sm("ex"), sm("xr")))
            exp_in_place(sm("ex"), sm("t0"), sm("t1"))
            step(gp.tensor_tensor(ang[:], repeat(mult[:], 2, 32), repeat(sm("th"), 1, 67), ALU.mult))
            step(gp.tensor_tensor(expo[:], repeat(mult[:, 0:48], 2, 32), repeat(sm("xr"), 1, 48), ALU.mult))
            for a, b in ((0, 32), (32, 64), (64, 67)):
                k, pr, an = turns[:, 0:b - a, :], prod[:, 0:b - a, :], ang[:, a:b, :]
                qt = repeat(quarter[:, a:b], 2, 32)
                step(gp.tensor_scalar(k, an, 1.0 / (2 * PI), None, ALU.mult))
                step(gp.tensor_tensor(k, k, qt, ALU.add))
                step(gp.tensor_scalar(k, k, MAGIC, None, ALU.add))
                step(gp.tensor_scalar(k, k, -MAGIC, None, ALU.add))
                for part in (C1, C2, C3):
                    step(gp.tensor_scalar(pr, k, -part, None, ALU.mult))
                    step(gp.tensor_tensor(an, an, pr, ALU.add))
                step(gp.tensor_scalar(pr, qt, 2 * PI, None, ALU.mult))
                step(gp.tensor_tensor(an, an, pr, ALU.add))
                step(gp.tensor_scalar(an, an, PI_F32, -PI_F32, ALU.min, ALU.max))
            for a, b in ((0, 32), (32, 48)):
                exp_in_place(expo[:, a:b, :], turns[:, 0:b - a, :], prod[:, 0:b - a, :])
            gp.memset(sm("t2"), 0.0).then_inc(ang_ok, 1)
            pool.wait_ge(fn_ok, 2)
            sin_th, cos_th, sin_half = ang[:, 64, :], ang[:, 65, :], ang[:, 66, :]
            step(gp.tensor_scalar(sm("t0"), sm("ex"), 1.0, None, ALU.add))
            step(gp.tensor_tensor(sm("t0"), sm("t0"), sm("thx"), ALU.mult))
            step(gp.tensor_tensor(sm("er"), sm("t0"), cos_th, ALU.mult))
            step(gp.tensor_tensor(sm("t1"), sin_half, sin_half, ALU.mult))
            step(gp.tensor_scalar(sm("t1"), sm("t1"), -2.0, None, ALU.mult))
            step(gp.tensor_tensor(sm("er"), sm("er"), sm("t1"), ALU.add))
            step(gp.tensor_tensor(sm("ei"), sm("ex"), sin_th, ALU.mult))
            step(gp.tensor_tensor(sm("t0"), sm("ei"), param("a_im"), ALU.mult))
            step(gp.tensor_tensor(sm("t1"), sm("er"), sm("ea"), ALU.mult))
            step(gp.tensor_tensor(sm("nr"), sm("t0"), sm("t1"), ALU.subtract))
            step(gp.tensor_tensor(sm("t0"), sm("er"), param("a_im"), ALU.mult))
            step(gp.tensor_tensor(sm("t1"), sm("ei"), sm("ea"), ALU.mult))
            step(gp.tensor_tensor(sm("ni"), sm("t0"), sm("t1"), ALU.add))
            step(gp.tensor_scalar(sm("t2"), sm("rden"), 2.0, None, ALU.mult))
            step(gp.tensor_tensor(sm("nr"), sm("nr"), sm("t2"), ALU.mult))
            step(gp.tensor_tensor(sm("ni"), sm("ni"), sm("t2"), ALU.mult))
            step(gp.tensor_scalar(sm("ni"), sm("ni"), -1.0, None, ALU.mult))
            step(gp.tensor_tensor(sm("t0"), param("c_re"), sm("nr"), ALU.mult))
            step(gp.tensor_tensor(sm("t1"), param("c_im"), sm("ni"), ALU.mult))
            step(gp.tensor_tensor(sm("cr2"), sm("t0"), sm("t1"), ALU.subtract))
            step(gp.tensor_tensor(sm("t0"), param("c_re"), sm("ni"), ALU.mult))
            step(gp.tensor_tensor(sm("t1"), param("c_im"), sm("nr"), ALU.mult))
            step(gp.tensor_tensor(sm("ci2"), sm("t0"), sm("t1"), ALU.add))
            step(gp.tensor_copy(sm("er", 0, 64), sm("cr2", 0, 64)))
            step(gp.tensor_scalar(sm("er", 64, P), sm("ci2", 64, P), -1.0, None, ALU.mult))
            step(gp.tensor_scalar(sm("ei", 0, 64), sm("ci2", 0, 64), -1.0, None, ALU.mult))
            step(gp.tensor_scalar(sm("ei", 64, P), sm("cr2", 64, P), -1.0, None, ALU.mult))
            step(gp.tensor_tensor(expo[:, 0:32, :], expo[:, 0:32, :], ang[:, 0:32, :], ALU.mult))
            for cols, coeff in ((slice(32, 48), "ei"), (slice(48, 64), "er")):
                step(gp.tensor_tensor(ang[:, cols, :], ang[:, cols, :], expo[:, 32:48, :], ALU.mult))
                step(gp.tensor_tensor(ang[:, cols, :], ang[:, cols, :], repeat(sm(coeff), 1, 16), ALU.mult))
            gp.tensor_tensor(ang[:, 32:48, :], ang[:, 32:48, :], ang[:, 48:64, :], ALU.add).then_inc(tab_ok, 1)
            gp.memset(kzero[:], 0.0).then_inc(kern_d, 1)
            pool.wait_ge(kern_ok, 1)
            gp.tensor_tensor(k_sb[0:1, :, 0], k_sb[0:1, :, 0], d_row[:, :], ALU.add).then_inc(kern_d, 1)
            pool.wait_ge(bo_in, 16)
            for g in range(G):
                gp.tensor_tensor(backwards(acc[:, g, :].rearrange("p (c n) -> p c n", n=P)),
                                 x_nat[:, g, :].rearrange("p (c n) -> p c n", n=P),
                                 bo_rows[:].rearrange("p (c n) -> p c n", n=P), ALU.add).then_inc(acc_set, 1)
            pool.wait_ge(sum_ok, 2 * HEADS)
            gp.memset(p_blocks[:], 0.0).then_inc(blocks_zero, 1)
            pool.wait_ge(p_ok, NQ)
            for c in range(4):
                last = gp.tensor_tensor(gate_sel[:, c, :, :], repeat(gate_p[:, c, :], 2, RANK),
                                        repeat(delta32[:], 1, G), ALU.mult)
            last.then_inc(gsel_ok, 1)
            pool.wait_ge(gsel_ok, 1)
            pool.wait_ge(wo_mm, G * NQ)
            gp.memset(ax[2 * RANK:2 * RANK + 1, :, :], 1.0).then_inc(ax_one, 1)

        @block.tensor
        def _(pe):
            mm = nc.tensor.matmul

            def product3(out, terms):
                last = None
                for n, (lh, ll, rh, rl) in enumerate(terms):
                    mm(out, lh, rh, start=(n == 0), stop=False)
                    mm(out, lh, rl, start=False, stop=False)
                    last = mm(out, ll, rh, start=False, stop=(n == len(terms) - 1))
                return last

            pe.wait_ge(cond_in, 32)
            pe.wait_ge(hot_ok, 1)
            for n in range(2):
                last = mm(bank(n), onehot[:].rearrange("n q b -> n (q b)"), cond_nat[:, 512 * n:512 * n + 512],
                          start=True, stop=True)
            last.then_inc(mixw_mm, 1)

            pe.wait_ge(mixw_ok, 1)
            for g in range(G):
                pe.wait_ge(x_in[g // 2], 16)
                if g >= 6:
                    pe.wait_ge(mixlo_ok, g - 5)
                for c in range(KC):
                    last = mm(bank(2 + g % 6)[:, P * c:P * c + P], x_nat[:, g, P * c:P * c + P],
                              mix_w[:, g, :], start=True, stop=True)
                last.then_inc(mix_mm, 1)

            pe.wait_ge(mixt_ok, 1)
            pe.wait_ge(const_ok, 2)
            pe.wait_ge(prm_in, 16 * 9)
            pe.wait_ge(c_dup, 2)
            for n in range(9):
                last = nc.tensor.transpose(bank(1)[:, 32 * n:32 * n + 32], prm_nat[:, n, :], ident[0:32, 0:32])
            last.then_inc(prm_mm, 1)

            def head_scores(h, slot):
                pe.wait_ge(q_ok, h * 2 + 2)
                pe.wait_ge(k_ok, h * 2 + 2)
                if not (isinstance(h, int) and h < 1):
                    pe.wait_ge(s_ok, h)
                for g in range(G):
                    last = mm(bank(4, 1024)[:, P * g:P * g + P], qk_sb[:, slot, 0, P * g:P * g + P],
                              qk_sb[:, slot, 1, P * g:P * g + P], start=True, stop=True)
                last.then_inc(s_mm, 1)

            def head_qk(h, slot, first=False):
                pe.wait_ge(wlo_ok, h + 1)
                for m, (done, free) in enumerate(((q_mm, q_ok), (k_mm, k_ok))):
                    for n in range(2):
                        if not first:
                            pe.wait_ge(free, h * 2 + (n - 1))
                        elif m == 0:
                            pe.wait_ge(mixlo_ok, 4 * n + 4)
                        product3(bank(2 * m + n),
                                 [(w_hi[:, slot, m, c, :], w_lo[:, slot, m, c, :],
                                   mix_hi[:, c, HALF * n:HALF * n + HALF], mix_lo[:, c, HALF * n:HALF * n + HALF])
                                  for c in range(KC)]).then_inc(done, 1)
                        if m == 0 and n == 0 and not first:
                            head_scores(h - 1, 1 - slot)

            pe.wait_ge(prm_ok, 1)
            head_qk(0, 0, first=True)
            head_qk(1, 1)
            with pe.Fori(1, HEADS // 2 - 1) as i:
                for j in range(2):
                    head_qk(i * 2 + j, j)
            head_qk(HEADS - 2, 0)
            pe.wait_ge(tab_ok, 1)
            for h in range(SEQ):
                last = mm(bank(6, 1024)[0:CA, CL * h:CL * h + CL], ang[:, 32:48, h], expo[:, 0:CL, h],
                          start=True, stop=True)
            last.then_inc(kern_mm, 1)
            head_qk(HEADS - 1, 1)
            head_scores(HEADS - 1, 1)

            def value_group(t, g, free=True):
                if free:
                    pe.wait_ge(v_ok, t * G + (g - 1))
                product3(bank(g % 2),
                         [(mix_hi[:, c, P * g:P * g + P], mix_lo[:, c, P * g:P * g + P],
                           wv_hi[:, c, :], wv_lo[:, c, :]) for c in range(KC)]).then_inc(v_mm, 1)

            def attend(t, first=False):
                pe.wait_ge(p_ok, t + 1)
                pe.wait_ge(v_ok, t * G + G)
                for u in range(8):
                    h, half = u // 2, u % 2
                    if not (first and u < 4):
                        pe.wait_ge(alo_ok, t * 8 + (u - 3))
                    for g in range(4 * half, 4 * half + 4):
                        last = mm(bank(2 + u % 4)[:, P * (g % 4):P * (g % 4) + P],
                                  v_sb[:, g, HD * h:HD * h + HD], p_blocks[:, h, g, :], start=True, stop=True)
                    last.then_inc(pv_mm, 1)

            def project_group(t, g, free=True):
                if free:
                    pe.wait_ge(acc_ok, t * 8 + (g - 1))
                tok = slice(P * g, P * g + P)
                product3(bank(6 + g % 2),
                         [(attn_hi[:, h, tok], attn_lo[:, h, tok], wo_hi[:, h, :], wo_lo[:, h, :])
                          for h in range(QUAD)]).then_inc(wo_mm, 1)

            def project(t, first=False):
                pe.wait_ge(wolo_ok, t + 1)
                pe.wait_ge(alo_ok, t * 8 + 8)
                for g in range(G):
                    project_group(t, g, free=not (first and g < 2))

            pe.wait_ge(q_ok, 2 * HEADS)
            pe.wait_ge(wvlo_ok, 1)
            value_group(0, 0, free=False)
            pe.wait_ge(sum_ok, 2 * HEADS)
            pe.wait_ge(kern_ok, 1)
            for n in range(2):
                last = mm(bank(6 + n), ones[:, :], sumsq[:, 1, HALF * n:HALF * n + HALF], start=True, stop=True)
            last.then_inc(vk_mm, 1)
            pe.wait_ge(k_ok, 2 * HEADS)
            for g in range(G):
                last = mm(bank(2)[:, g:g + 1], sumsq[:, 0, P * g:P * g + P], ones[:, 0:1], start=True, stop=True)
            last.then_inc(vq_mm, 1)
            value_group(0, 1, free=False)
            for g in range(2, G):
                value_group(0, g)
            pe.wait_ge(var_ok, 5)
            pe.wait_ge(s_ok, HEADS)
            attend(0, first=True)
            pe.wait_ge(wvlo_ok, 2)
            for g in range(G):
                value_group(1, g)
            project(0, first=True)
            with pe.Fori(1, NQ - 1) as t:
                attend(t)
                pe.wait_ge(wvlo_ok, t + 2)
                for g in range(G):
                    value_group(t + 1, g)
                project(t)
            attend(NQ - 1)
            pe.wait_ge(gsel_ok, 1)
            pe.wait_ge(la_in, 16)
            pe.wait_ge(v_ok, G * NQ)
            for c in range(KC):
                for k in range(4):
                    last = mm(bank(c // 2)[:, 256 * (c % 2):256 * (c % 2) + 256],
                              la_nat[:, k, P * c:P * c + P], gate_sel[:, k, :, :], start=(k == 0), stop=(k == 3))
            last.then_inc(ae_mm, 1)

            def transpose_x2(g):
                pe.wait_ge(acc_ok, 8 * (NQ - 1) + g + 1)
                if g >= 4:
                    pe.wait_ge(x2p_ok, g - 3)
                for c in range(KC):
                    last = nc.tensor.transpose(bank(2 + g % 4)[:, P * c:P * c + P], acc[:, g, P * c:P * c + P],
                                               ident[:, :])
                last.then_inc(xt_mm, 1)

            pe.wait_ge(wolo_ok, NQ)
            pe.wait_ge(alo_ok, 8 * NQ)
            for g in range(G):
                project_group(NQ - 1, g)
                if g >= 2:
                    transpose_x2(g - 2)

            def transpose_b(c):
                for o in range(KC):
                    last = nc.tensor.transpose(bank((6, 7, 2, 3)[c])[:, P * o:P * o + P],
                                               lb_nat[:, o, P * c:P * c + P], ident[:, :])
                last.then_inc(bt_mm, 1)

            pe.wait_ge(lb_in, 64)
            transpose_x2(6)
            pe.wait_ge(acc_ok, 8 * NQ)
            transpose_b(0)
            transpose_b(1)
            transpose_x2(7)
            pe.wait_ge(x2p_ok, 6)
            transpose_b(2)
            transpose_b(3)
            pe.wait_ge(sh_in, 32)
            pe.wait_ge(x2p_ok, 8)
            for c in range(KC):
                nc.tensor.transpose(bank(4)[:, RANK * c:RANK * c + RANK], las_nat[:, P * c:P * c + P],
                                    ident[0:RANK, 0:RANK])
            for o in range(KC):
                last = nc.tensor.transpose(bank(5)[0:RANK, P * o:P * o + P], lbs_nat[:, o, :], ident[:, :])
            last.then_inc(sh_mm, 1)
            pe.wait_ge(bt_ok, 4)
            for n in range(2):
                for k in range(4):
                    last = mm(bank(6 + n), gate_sel[:, k, 4 * n:4 * n + 4, :], b_t[:, k, :], start=(k == 0), stop=(k == 3))
            last.then_inc(be_mm, 1)

            for s in range(SEQ):
                if s % 4 == 0:
                    u = s // 4
                    if u >= 2:
                        pe.wait_ge(y_ok, u - 1)
                    if s == 0:
                        pe.wait_ge(toep_in0, 16)
                    if s == 16:
                        pe.wait_ge(toep_in1, 16)
                toep = toep0 if s < 16 else toep1
                for d in range(KC):
                    last = mm(bank(2 + (s // 4) % 2)[:, P * (s % 4) + 32 * d:P * (s % 4) + P],
                              toep[:, s % 16, P * d:P * d + P], x2p[:, s, 0:KC - d, :],
                              start=(d == 0), stop=(d == KC - 1), skip_group_check=True)
                if s % 4 == 3:
                    last.then_inc(conv_mm, 1)

            def down(g):
                if g >= 2:
                    pe.wait_ge(ax_ok, g - 1)
                for c in range(KC):
                    last = mm(bank(4 + g % 2)[0:2 * RANK, 0:P], lora_a_t[:, c, g, :],
                              y_t[:, c, BPG * g:BPG * g + BPG, :], start=(c == 0), stop=(c == KC - 1))
                last.then_inc(ax_mm, 1)

            pe.wait_ge(y_ok, 8)
            pe.wait_ge(ae_ok, KC)
            pe.wait_ge(sh_ok, KC + 1)
            down(0)
            pe.wait_ge(ffn_in, 16)
            pe.wait_ge(be_ok, 2)
            for g in range(G):
                o = bank(6 + g % 2)
                if g >= 2:
                    pe.wait_ge(out_ok, g - 1)
                for c in range(KC):
                    mm(o, y_t[:, c, BPG * g:BPG * g + BPG, :], ffn_sb[:, c, :], start=(c == 0), stop=False,
                       skip_group_check=True)
                if g + 1 < G:
                    down(g + 1)
                pe.wait_ge(ax_ok, g + 1)
                if g == 0:
                    pe.wait_ge(ax_one, 1)
                    pe.wait_ge(bias_in, 16 * G)
                    pe.wait_ge(be_in, 16 * G)
                mm(o, ax[:, g % 2, :], lora_b_t[:, g, :], start=False, stop=True,
                   skip_group_check=True).then_inc(out_mm, 1)

        @block.scalar
        def _(act):
            sc = nc.scalar
            spacer = act.alloc_register("spacer")

            def here(index):
                if isinstance(index, int):
                    return index
                act.reg_mov(spacer, index)
                return act.snap(spacer, min_val=0, max_val=HEADS - 1)
            act.dma_start(cond_i[:], every_partition(cond_idx, BATCH, NCOND)).then_inc(cond_in, 16)
            act.dma_start(cond_nat[:], cond_w.rearrange("n c d -> n (c d)")).then_inc(cond_in, 16)
            act.dma_start(prm_nat[:, 9, :], ssm_c.rearrange("h n two -> h (n two)")).then_inc(c_in, 16)
            for n, v in enumerate((bq, bk, gq, gk, bv)):
                act.dma_start(prm_nat[:, n, :], v.rearrange("(h d) -> h d", d=HD)).then_inc(prm_in, 16)
            for n, v in ((5, log_a), (6, a_im)):
                for k in range(2):
                    act.dma_start(prm_nat[:, n, NSTATE * k:NSTATE * k + NSTATE], v).then_inc(prm_in, 16)
            act.dma_start(small[:, SM["log_dt"], :], every_partition(log_dt, 32)).then_inc(misc_in, 16)
            act.dma_start(len_i[:], every_partition(lengths, BATCH)).then_inc(misc_in, 16)
            act.dma_start(gate_b[:].rearrange("p b n -> p (b n)"), every_partition(gate, G * NLORA)).then_inc(misc_in, 16)
            act.dma_start(d_row[:], every_partition(ssm_d, 32, 1)).then_inc(misc_in, 16)

            def split_hi(h, slot):
                for m in range(2):
                    last = sc.activation(w_hi[:, slot, m].rearrange("p c n -> p (c n)"),
                                         w_raw[:, slot, m].rearrange("p c n -> p (c n)"), ACT.Copy)
                last.then_inc(whi_ok, 1)

            act.wait_ge(w_in[0], 32)
            split_hi(0, 0)
            for g in range(G):
                act.wait_ge(mix_mm, g + 1)
                sc.activation(mix_hi[:, :, P * g:P * g + P],
                              bank(2 + g % 6).rearrange("p (c t) -> p c t", c=KC), ACT.Copy).then_inc(mixhi_ok, 1)
            act.wait_ge(prm_mm, 1)
            sc.activation(params[:].rearrange("p n h -> p (n h)"), bank(1, 288), ACT.Copy).then_inc(prm_ok, 1)


            def head(h, slot, first=False, last_head=False, w_count=None):
                if not last_head:
                    act.wait_ge(w_in[1 - slot], w_count)
                    if not first:
                        act.wait_ge(k_mm, h * 2)
                    split_hi(h + 1, 1 - slot)
                for n in range(2):
                    tok = slice(HALF * n, HALF * n + HALF)
                    act.wait_ge(q_mm, h * 2 + n + 1)
                    if n == 0 and not (isinstance(h, int) and h < 2):
                        act.wait_ge(sum_ok, h * 2 - 2)
                    at = here(h)
                    sc.activation(sq[:, slot, 0, tok], bank(n), ACT.Square,
                                  bias=params[:, PARAM["bq"], bass.ds(at, 1)]).then_inc(q_sq, 1)
                for n in range(2):
                    tok = slice(HALF * n, HALF * n + HALF)
                    act.wait_ge(k_mm, h * 2 + n + 1)
                    at = here(h)
                    sc.activation(sq[:, slot, 1, tok], bank(2 + n), ACT.Square,
                                  bias=params[:, PARAM["bk"], bass.ds(at, 1)]).then_inc(k_sq, 1)
                    if n == 0 and not (isinstance(h, int) and h < 2):
                        act.wait_ge(s_mm, h - 1)
                    at = here(h)
                    sc.activation(qk_sb[:, slot, 1, tok], bank(2 + n), ACT.Identity,
                                  bias=params[:, PARAM["bk"], bass.ds(at, 1)]).then_inc(k_ok, 1)

            def heads(lo, hi):
                with act.Fori(lo, hi) as i:
                    head(i * 2, 0, w_count=i * 32 + 32)
                    head(i * 2 + 1, 1, w_count=i * 32 + 64)

            head(0, 0, first=True, w_count=32)
            head(1, 1, w_count=64)
            heads(1, 12)
            act.wait_ge(ang_ok, 1)
            sc.activation(sm("thx"), sm("xr"), ACT.Tanh, scale=0.5).then_inc(fn_ok, 1)
            sc.activation(ang[:], ang[:], ACT.Sin).then_inc(fn_ok, 1)
            heads(12, HEADS // 2 - 1)
            head(HEADS - 2, 0, w_count=16 * HEADS)
            act.wait_ge(kern_mm, 1)
            act.wait_ge(kern_d, 1)
            sc.activation(k_sb[:].rearrange("a h c -> a (h c)"), bank(6, 1024)[0:CA, :], ACT.Copy).then_inc(kern_ok, 1)
            act.dma_start(bo_rows[:], every_partition(bo, FEAT)).then_inc(bo_in, 16)
            act.wait_ge(wv_in, 16)
            sc.activation(wv_hi[:].rearrange("p c n -> p (c n)"), wv_raw[:].rearrange("p c n -> p (c n)"),
                          ACT.Copy).then_inc(wvhi_ok, 1)
            head(HEADS - 1, 1, last_head=True)

            def value_out(t, g):
                act.wait_ge(v_mm, t * G + (g + 1))
                sc.activation(v_sb[:, g, :], bank(g % 2), ACT.Copy).then_inc(v_ok, 1)

            def exp_scores(t):
                act.wait_ge(soft, t * 6 + 3)
                sc.activation(sm_e[:], sm_s[:], ACT.Exp).then_inc(e_ok, 1)

            def attn_out(t):
                for u in range(8):
                    h, half = u // 2, u % 2
                    act.wait_ge(pv_mm, t * 8 + (u + 1))
                    at = here(t * QUAD + h)
                    sc.activation(attn_hi[:, h, HALF * half:HALF * half + HALF], bank(2 + u % 4), ACT.Identity,
                                  bias=params[:, PARAM["bv"], bass.ds(at, 1)]).then_inc(ahi_ok, 1)

            def split_o(t):
                act.wait_ge(wo_in, t * 16 + 16)
                sc.activation(chunks_backwards(wo_hi), wo_raw[:].rearrange("p h (c n) -> p (h c) n", n=P),
                              ACT.Copy).then_inc(wohi_ok, 1)

            def split_v(t):
                act.wait_ge(wv_in, t * 16 + 16)
                act.wait_ge(v_mm, t * G)
                sc.activation(wv_hi[:].rearrange("p c n -> p (c n)"), wv_raw[:].rearrange("p c n -> p (c n)"),
                              ACT.Copy).then_inc(wvhi_ok, 1)

            value_out(0, 0)
            act.wait_ge(norm, 1)
            sc.activation(var_k[:], inv_norm[:], ACT.Sqrt).then_inc(std_ok, 1)
            for g in range(1, 4):
                value_out(0, g)
            act.wait_ge(acc_set, G)
            exp_scores(0)
            for g in range(4, G):
                value_out(0, g)
            split_v(1)

            def quad(t):
                attn_out(t)
                split_o(t)
                for g in range(5):
                    value_out(t + 1, g)
                exp_scores(t + 1)
                for g in range(5, G):
                    value_out(t + 1, g)

            quad(0)
            split_v(2)
            with act.Fori(1, NQ - 2) as t:
                quad(t)
                split_v(t + 2)
            quad(NQ - 2)
            attn_out(NQ - 1)
            split_o(NQ - 1)

            def x2_out(g):
                act.wait_ge(xt_mm, g + 1)
                sc.activation(x2p[:, :, :, BPG * g:BPG * g + BPG].rearrange("p s c b -> p c b s"),
                              bank(2 + g % 4).rearrange("p (c b s) -> p c b s", c=KC, b=BPG), ACT.Copy).then_inc(x2p_ok, 1)

            def b_out(c):
                act.wait_ge(bt_mm, c + 1)
                sc.activation(b_t[:, c, :], bank((6, 7, 2, 3)[c]), ACT.Copy).then_inc(bt_ok, 1)

            for g in range(G - 1):
                x2_out(g)
            b_out(0)
            b_out(1)
            x2_out(G - 1)
            b_out(2)
            b_out(3)
            act.wait_ge(sh_mm, 1)
            for c in range(KC):
                sc.activation(lora_a_t[:, c, :, 0:RANK], repeat(bank(4)[:, RANK * c:RANK * c + RANK], 1, G),
                              ACT.Copy).then_inc(sh_ok, 1)
            sc.activation(lora_b_t[0:RANK, :, :], repeat(bank(5)[0:RANK, :], 1, G), ACT.Copy).then_inc(sh_ok, 1)

        @block.vector
        def _(dve):
            v = nc.vector
            v.memset(mix_w[:], 0.0).then_inc(zero_ok, 1)
            dve.wait_ge(cond_in, 32)
            v.tensor_copy(cond_f[:], cond_i[:]).then_inc(condf_ok, 1)
            dve.wait_ge(condf_ok, 1)
            dve.wait_ge(sel_const, 1)
            v.tensor_scalar(onehot[:], repeat(cond_f[:], 1, BPG), cond_no[:, 0:1], None, ALU.is_equal).then_inc(hot_ok, 1)

            def split_lo(h, slot):
                dve.wait_ge(whi_ok, h + 1)
                for m in range(2):
                    last = v.tensor_tensor(w_lo[:, slot, m].rearrange("p c n -> p (c n)"),
                                           w_raw[:, slot, m].rearrange("p c n -> p (c n)"),
                                           w_hi[:, slot, m].rearrange("p c n -> p (c n)").bitcast(F32), ALU.subtract)
                last.then_inc(wlo_ok, 1)

            dve.wait_ge(mixw_mm, 1)
            v.transpose(mix_t[:], bank(0, 1024).rearrange("p (c d) -> p d c", d=32)).then_inc(mixt_ok, 1)
            dve.wait_ge(mixt_ok, 1)
            dve.wait_ge(zero_ok, 1)
            for b in range(BPG):
                last = v.tensor_copy(mix_w[quadrant(b), :, quadrant(b)],
                                     mix_t[quadrant(b)].rearrange("p d (g b) -> p g d b", b=BPG)[:, :, :, b])
            last.then_inc(mixw_ok, 1)
            split_lo(0, 0)
            for g in range(G):
                tok = slice(P * g, P * g + P)
                dve.wait_ge(mixhi_ok, g + 1)
                v.tensor_tensor(mix_lo[:, :, tok], bank(2 + g % 6).rearrange("p (c t) -> p c t", c=KC),
                                mix_hi[:, :, tok].bitcast(F32), ALU.subtract).then_inc(mixlo_ok, 1)

            def extract(h):
                dve.wait_ge(s_mm, h + 1)
                dst = scores[:].rearrange("p h g k -> p (h g k)")[:, bass.ds(h * (G * 32), G * 32)]
                for b in range(BPG):
                    src = bank(4, 1024)[quadrant(b), :].rearrange("p (g k) -> p g k", g=G)[:, :, quadrant(b)]
                    last = v.tensor_copy(dst[quadrant(b), :].rearrange("p (g k) -> p g k", g=G), src)
                last.then_inc(s_ok, 1)

            def head(h, slot, first=False, last_head=False):
                if not last_head:
                    if not first:
                        dve.wait_ge(k_mm, h * 2)
                    split_lo(h + 1, 1 - slot)
                for n in range(2):
                    tok = slice(HALF * n, HALF * n + HALF)
                    dve.wait_ge(q_sq, h * 2 + n + 1)
                    if n == 0 and not (isinstance(h, int) and h < 2):
                        dve.wait_ge(s_mm, h - 1)
                    v.tensor_scalar(qk_sb[:, slot, 0, tok], bank(n), params[:, PARAM["bq"], bass.ds(h, 1)],
                                    gqk[:, bass.ds(h, 1)], ALU.add, ALU.mult).then_inc(q_ok, 1)
                    if n == 0 and not first:
                        if isinstance(h, int) and h == 1:
                            dve.wait_ge(mask_ok, 1)
                            dve.wait_ge(gatep_ok, 4)
                        extract(h - 1)
                for m, done in enumerate((q_sq, k_sq)):
                    if m == 1:
                        dve.wait_ge(done, h * 2 + 2)
                    if not first:
                        dve.wait_ge(sum_ok, h * 2 + (m - 1))
                    v.tensor_tensor(sumsq[:, m, :], sumsq[:, m, :], sq[:, slot, m, :], ALU.add).then_inc(sum_ok, 1)

            dve.wait_ge(gqk_ok, 1)
            dve.wait_ge(sumsq_set, 1)
            head(0, 0, first=True)
            head(1, 1)
            with dve.Fori(1, HEADS // 2 - 1) as i:
                for j in range(2):
                    head(i * 2 + j, j)
            head(HEADS - 2, 0)

            def split_v(t, parts=(0, 1, 2, 3)):
                if 0 in parts:
                    dve.wait_ge(wvhi_ok, t + 1)
                for c in parts:
                    last = v.tensor_tensor(wv_lo[:, c, :], wv_raw[:, c, :], wv_hi[:, c, :].bitcast(F32), ALU.subtract)
                if KC - 1 in parts:
                    last.then_inc(wvlo_ok, 1)

            split_v(0)
            head(HEADS - 1, 1, last_head=True)

            dve.wait_ge(vk_mm, 1)
            for b in range(BPG):
                src = bank(6, 1024)[quadrant(b), :].rearrange("p (g k) -> p g k", g=G)[:, :, quadrant(b)]
                v.tensor_scalar(var_k[quadrant(b)], src, 1.0 / INNER, RMS_EPS, ALU.mult, ALU.add).then_inc(var_ok, 1)
            dve.wait_ge(vq_mm, 1)
            v.tensor_scalar(var_q[:], bank(2, G), 1.0 / INNER, RMS_EPS, ALU.mult, ALU.add).then_inc(var_ok, 1)
            dve.wait_ge(var_ok, 5)
            v.scalar_tensor_tensor(inv_norm[:], var_k[:], float(HD), repeat(var_q[:], 2, 32),
                                   ALU.mult, ALU.mult).then_inc(norm, 1)
            dve.wait_ge(std_ok, 1)
            tmp = sm_s[:, 0]
            dve.wait_ge(kpad_out, 32)
            v.reciprocal(tmp, var_k[:]).then_inc(norm, 1)
            dve.wait_ge(norm, 2)
            v.tensor_tensor(tmp, tmp, inv_norm[:], ALU.mult).then_inc(norm, 1)
            dve.wait_ge(norm, 3)
            v.tensor_tensor(tmp, tmp, var_k[:], ALU.add).then_inc(norm, 1)
            dve.wait_ge(norm, 4)
            v.tensor_scalar(tmp, tmp, 0.5, None, ALU.mult).then_inc(norm, 1)
            dve.wait_ge(norm, 5)
            v.reciprocal(inv_norm[:], tmp).then_inc(norm, 1)
            dve.wait_ge(norm, 6)
            extract(HEADS - 1)

            def flat(tile):
                return tile[:].rearrange("p h g k -> p (h g) k")

            def soft_max(t):
                src = scores[:].rearrange("p h g k -> p (h g k)")[:, bass.ds(t * (QUAD * G * 32), QUAD * G * 32)]
                v.tensor_tensor(sm_s[:].rearrange("p h g k -> p h (g k)"),
                                src.rearrange("p (h n) -> p h n", h=QUAD),
                                repeat(inv_norm[:].rearrange("p g k -> p (g k)"), 1, QUAD), ALU.mult).then_inc(soft, 1)
                dve.wait_ge(soft, t * 6 + 1)
                v.tensor_reduce(row_max[:], flat(sm_s), AX_X, ALU.max).then_inc(soft, 1)
                dve.wait_ge(soft, t * 6 + 2)
                v.tensor_tensor(flat(sm_s), flat(sm_s), repeat(row_max[:], 2, 32), ALU.subtract).then_inc(soft, 1)

            def soft_norm(t):
                dve.wait_ge(e_ok, t + 1)
                v.tensor_reduce(row_sum[:], flat(sm_e), AX_X, ALU.add).then_inc(soft, 1)
                dve.wait_ge(soft, t * 6 + 4)
                v.reciprocal(row_inv[:], row_sum[:]).then_inc(soft, 1)
                dve.wait_ge(soft, t * 6 + 5)
                v.tensor_tensor(flat(sm_e), flat(sm_e), repeat(row_inv[:], 2, 32), ALU.mult).then_inc(soft, 1)
                dve.wait_ge(soft, t * 6 + 6)
                dve.wait_ge(pv_mm, t * 8) if not isinstance(t, int) or t > 0 else None
                for b in range(BPG):
                    last = v.transpose(p_blocks[quadrant(b), :, :, quadrant(b)].rearrange("p h g q -> p (h g) q"),
                                       sm_e[quadrant(b)].rearrange("p h g k -> p (h g) k"))
                last.then_inc(p_ok, 1)

            soft_max(0)
            dve.wait_ge(blocks_zero, 1)
            soft_norm(0)
            split_v(1)

            def attn_out(t):
                for u in range(8):
                    h, half = u // 2, u % 2
                    tok = slice(HALF * half, HALF * half + HALF)
                    dve.wait_ge(ahi_ok, t * 8 + (u + 1))
                    v.scalar_tensor_tensor(attn_lo[:, h, tok], bank(2 + u % 4),
                                           params[:, PARAM["bv"], bass.ds(t * QUAD + h, 1)],
                                           attn_hi[:, h, tok].bitcast(F32), ALU.add, ALU.subtract).then_inc(alo_ok, 1)

            def split_o(t):
                dve.wait_ge(wohi_ok, t + 1)
                v.tensor_tensor(chunks_backwards(wo_lo), wo_raw[:].rearrange("p h (c n) -> p (h c) n", n=P),
                                chunks_backwards(wo_hi).bitcast(F32), ALU.subtract).then_inc(wolo_ok, 1)

            def accumulate(t, groups, first=False):
                for g in groups:
                    dve.wait_ge(wo_mm, t * 8 + (g + 1))
                    if not first:
                        dve.wait_ge(acc_ok, t * 8 + (g - 7))
                    v.tensor_tensor(acc[:, g, :], bank(6 + g % 2), acc[:, g, :], ALU.add).then_inc(acc_ok, 1)

            def quad(t, first=False, split=True):
                attn_out(t)
                split_o(t)
                soft_max(t + 1)
                soft_norm(t + 1)
                accumulate(t, (0, 1, 2), first)
                for c in range(KC):
                    if split:
                        split_v(t + 2, (c,))
                    accumulate(t, (3 + c,), first)
                accumulate(t, (7,), first)

            dve.wait_ge(acc_set, G)
            quad(0, first=True)
            with dve.Fori(1, NQ - 2) as t:
                quad(t)
            quad(NQ - 2, split=False)
            attn_out(NQ - 1)
            split_o(NQ - 1)
            accumulate(NQ - 1, range(8))

            dve.wait_ge(ae_mm, 1)
            dve.wait_ge(wo_mm, G * NQ)
            for c in range(KC):
                v.tensor_copy(lora_a_t[:, c, :, RANK:2 * RANK],
                              bank(c // 2)[:, 256 * (c % 2):256 * (c % 2) + 256]
                              .rearrange("p (g r) -> p g r", g=G)).then_inc(ae_ok, 1)
            dve.wait_ge(be_mm, 1)
            for n in range(2):
                v.tensor_copy(b_eff[:, n, :], bank(6 + n)).then_inc(be_ok, 1)
            dve.wait_ge(mask_ok, 1)
            for u in range(8):
                dve.wait_ge(conv_mm, u + 1)
                for c in range(KC):
                    src = bank(2 + u % 2).rearrange("p (s c b) -> p s c b", s=4, c=KC)[:, :, c, :]
                    last = v.tensor_tensor(y_t[:, c, :, 4 * u:4 * u + 4].rearrange("p b s -> p s b"), src,
                                           repeat(mask[:, c, :], 1, 4), ALU.mult)
                last.then_inc(y_ok, 1)
            def down_out(g):
                dve.wait_ge(ax_mm, g + 1)
                if g >= 2:
                    dve.wait_ge(out_mm, g - 1)
                v.tensor_copy(ax[0:2 * RANK, g % 2, :], bank(4 + g % 2)[0:2 * RANK, 0:P]).then_inc(ax_ok, 1)

            down_out(0)
            for g in range(G):
                if g + 1 < G:
                    down_out(g + 1)
                dve.wait_ge(out_mm, g + 1)
                if g >= 2:
                    dve.wait_ge(out_dma[g % 2], 16 * (g // 2))
                v.tensor_tensor(o_stage[:, g % 2, :].rearrange("p (c n) -> p c n", n=P),
                                bank(6 + g % 2).rearrange("p (c n) -> p c n", n=P),
                                backwards(acc[:, g, :].rearrange("p (c n) -> p c n", n=P)), ALU.add).then_inc(out_ok, 1)


_INS = [("x", "x", (TOK, FEAT), F32), ("cond_idx", "itok_B_0_15", (BATCH,), I32),
        ("lengths", "itok_B_78_3631", (BATCH,), I32), ("cond_w", "L0_cond_weights", (NCOND, 32, 32), F32),
        ("wq", "L0_attn_Wq", (FEAT, INNER), F32), ("bq", "L0_attn_bq", (INNER,), F32),
        ("wk", "L0_attn_Wk", (FEAT, INNER), F32), ("bk", "L0_attn_bk", (INNER,), F32),
        ("wv", "L0_attn_Wv", (FEAT, INNER), F32), ("bv", "L0_attn_bv", (INNER,), F32),
        ("wo", "L0_attn_Wo", (INNER, FEAT), F32), ("bo", "L0_attn_bo", (FEAT,), F32),
        ("gq", "L0_attn_gq", (INNER,), F32), ("gk", "L0_attn_gk", (INNER,), F32),
        ("log_dt", "L0_cond2_log_dt", (SEQ,), F32), ("ssm_c", "L0_cond2_C", (SEQ, NSTATE, 2), F32),
        ("log_a", "L0_cond2_log_A_real", (SEQ, NSTATE), F32), ("a_im", "L0_cond2_A_imag", (SEQ, NSTATE), F32),
        ("ssm_d", "L0_cond2_D", (SEQ,), F32), ("gate", "L0_ffn_gate", (G, NLORA), F32),
        ("ffn_w", "L0_ffn_kernel", (FEAT, FEAT), F32), ("ffn_b", "L0_ffn_bias", (FEAT,), F32),
        ("lora_a", "L0_ffn_lora_A", (NLORA, RANK, FEAT), F32), ("lora_b", "L0_ffn_lora_B", (NLORA, FEAT, RANK), F32),
        ("lora_as", "L0_ffn_lora_A_shared", (RANK, FEAT), F32), ("lora_bs", "L0_ffn_lora_B_shared", (FEAT, RANK), F32)]


def kernel(**inputs):
    import numpy as np
    import concourse.bacc as bacc
    from concourse.bass_utils import run_bass_kernel_spmd

    nc = bacc.Bacc("TRN2", target_bir_lowering=False, num_devices=1)
    arrays, args = {}, {}
    for name, key, shape, dt in _INS:
        arrays[f"in_{name}"] = np.ascontiguousarray(inputs[key]).reshape(shape)
        args[name] = nc.dram_tensor(f"in_{name}", shape, dt, kind="ExternalInput").ap()
    args["kpad"] = nc.dram_tensor("kpad_dram", (SEQ, PADL), F32, kind="Internal").ap()
    args["out"] = nc.dram_tensor("out_dram", (TOK, FEAT), F32, kind="ExternalOutput").ap()
    build_program(nc, **args)
    result = run_bass_kernel_spmd(nc, [arrays], core_ids=[0])
    return result.results[0]["out_dram"].reshape(BATCH, SEQ, FEAT)
```

```python
from contextlib import ExitStack

import concourse.bass as bass
from concourse import mybir

F32 = mybir.dt.float32
F32R = mybir.dt.float32r
I32 = mybir.dt.int32
ALU = mybir.AluOpType
ACT = mybir.ActivationFunctionType
AX_X = mybir.AxisListType.X

P = 128
BATCH, SEQ, FEAT = 32, 32, 512
TOK = BATCH * SEQ
HEADS, HD = 32, 128
INNER = HEADS * HD
KC = FEAT // P
G = TOK // P
BPG = P // SEQ
HALF = TOK // 2
QUAD = 4
NQ = HEADS // QUAD
NCOND, NLORA, RANK = 16, 16, 32
NSTATE = 64
CL, CA = 32, FEAT // 32
PADL = P + FEAT
RMS_EPS = 1e-6
PI = 3.141592653589793
C1 = 6.28125
C2 = 0.0019350051879882812
C3 = 2 * PI - C1 - C2
MAGIC = 12582912.0
PI_F32 = 3.1415925
LN2_HI, LN2_LO = 0.693359375, -2.12194440e-4
EXP_COEFFS = [1 / 5040, 1 / 720, 1 / 120, 1 / 24, 1 / 6, 1 / 2, 1.0, 1.0]


def build_program(nc, x, cond_idx, lengths, cond_w, wq, bq, wk, bk, wv, bv, wo, bo, gq, gk,
                  log_dt, ssm_c, log_a, a_im, ssm_d, gate, ffn_w, ffn_b, lora_a, lora_b,
                  lora_as, lora_bs, kpad, a_scr, b_scr, bs_scr, out):
    ctx = ExitStack()
    with ctx:
        def sb(name, shape, dt=F32, scope=ctx):
            return scope.enter_context(nc.sbuf_tensor(name, shape, dt))

        def sem(name):
            return ctx.enter_context(nc.semaphore(name))

        def overlay(*lots):
            made = []
            for n, lot in enumerate(lots):
                scope = ctx if n == len(lots) - 1 else ExitStack()
                made.append([sb(name, shape, dt, scope) for name, shape, dt in lot])
                if scope is not ctx:
                    scope.close()
            return made

        psum = ctx.enter_context(nc.psum_tensor("psum", [P, 8 * 512], F32))

        def bank(n, width=512):
            return psum[:, n * 512:n * 512 + width]

        ident = sb("ident", [P, P])
        ones = sb("ones", [P, P])
        params = sb("params", [P, 9, 32])
        gqk = sb("gqk", [P, HEADS])
        inv_norm = sb("inv_norm", [P, G, 32])
        var_k = sb("var_k", [P, G, 32])
        var_q = sb("var_q", [P, G])
        row_max = sb("row_max", [P, QUAD * G])
        row_sum = sb("row_sum", [P, QUAD * G])
        row_inv = sb("row_inv", [P, QUAD * G])
        lidx = sb("lidx", [P, KC])
        mask = sb("mask", [P, KC, BATCH])
        d_row = sb("d_row", [1, 32])
        PARAM = dict(bq=0, bk=1, gq=2, gk=3, bv=4, log_a=5, a_im=6, c_re=7, c_im=8)

        def param(name):
            return params[:, PARAM[name], :]

        (toep1,), (mix_hi, mix_lo) = overlay(
            [("toep1", [P, 16, 512], F32)],
            [("mix_hi", [P, KC, TOK], F32R), ("mix_lo", [P, KC, TOK], F32R)])
        (mix_w, mix_t, cond_nat, cond_i, cond_f, cond_no, onehot, prm_nat, len_i, len_f), (toep0,), (scores,) = overlay(
            [("mix_w", [P, G, P], F32), ("mix_t", [P, 32, BATCH], F32), ("cond_nat", [NCOND, 32 * 32], F32),
             ("cond_i", [NCOND, BATCH], I32), ("cond_f", [NCOND, BATCH], F32), ("cond_no", [NCOND, 1], F32),
             ("onehot", [NCOND, BPG, BATCH], F32),
             ("prm_nat", [32, 10, P], F32),
             ("len_i", [P, BATCH], I32), ("len_f", [P, BATCH], F32)],
            [("toep0", [P, 16, 512], F32)],
            [("scores", [P, HEADS, G, 32], F32)])
        (ang, expo, mult, quarter), (acc,) = overlay(
            [("ang", [P, 67, 32], F32), ("expo", [P, 48, 32], F32), ("mult", [P, 67], F32),
             ("quarter", [P, 67], F32)],
            [("acc", [P, G, FEAT], F32)])
        (turns, prod), (k_sb, kzero, bo_rows), (o_stage, ax), (sm_s, sm_e) = overlay(
            [("turns", [P, 32, 32], F32), ("prod", [P, 32, 32], F32)],
            [("k_sb", [CA, 32, CL], F32), ("kzero", [32, P], F32), ("bo_rows", [P, FEAT], F32)],
            [("o_stage", [P, 2, FEAT], F32), ("ax", [2 * RANK + 1, 2, P], F32)],
            [("sm_s", [P, QUAD, G, 32], F32), ("sm_e", [P, QUAD, G, 32], F32)])
        (lb_nat,), (ffn_raw,), (wv_raw,) = overlay([("lb_nat", [P, KC, NLORA, RANK], F32)],
            [("ffn_raw", [P, KC, FEAT], F32)], [("wv_raw", [P, KC, 512], F32)])
        (la_t,), (b_out,), (ffn_hi,), (wv_hi,) = overlay([("la_t", [P, KC, NLORA, RANK], F32)],
            [("b_out", [P, G, KC, 32], F32)], [("ffn_hi", [P, KC, FEAT], F32R)], [("wv_hi", [P, KC, 512], F32R)])
        (la_nat,), (a_sum, b_sum), (ffn_lo,), (wv_lo,) = overlay([("la_nat", [P, KC, NLORA, 32], F32)],
            [("a_sum", [P, KC, G, RANK], F32), ("b_sum", [P, G, KC, RANK], F32)],
            [("ffn_lo", [P, KC, FEAT], F32R)], [("wv_lo", [P, KC, 512], F32R)])
        (gated, gate_b, las_nat, las_t, lbs_nat, lbs_t), (a_all,), (wo_raw,) = overlay(
            [("gated", [P, KC * G * RANK], F32), ("gate_b", [P, G, NLORA], F32), ("las_nat", [P, KC, 32], F32),
             ("las_t", [P, KC, RANK], F32), ("lbs_nat", [P, KC, RANK], F32), ("lbs_t", [P, KC, 32], F32)],
            [("a_all", [P, KC, G, 2 * RANK], F32)],
            [("wo_raw", [P, QUAD, FEAT], F32)])
        ((w_hi, w_lo, sq, qk_sb, x_nat, sumsq, w_raw),
         (x2p, y_t, y_hi, y_lo, b_all),
         (v_sb, p_blocks, attn_hi, attn_lo, wo_hi, wo_lo)) = overlay(
            [("w_hi", [P, 2, 2, KC, HD], F32R), ("w_lo", [P, 2, 2, KC, HD], F32R),
             ("sq", [P, 2, 2, TOK], F32), ("qk_sb", [P, 2, 2, TOK], F32), ("x_nat", [P, G, FEAT], F32),
             ("sumsq", [P, 2, TOK], F32), ("w_raw", [P, 2, 2, KC, HD], F32)],
            [("x2p", [P, SEQ, KC, BATCH], F32), ("y_t", [P, KC, BATCH, SEQ], F32),
             ("y_hi", [P, KC, BATCH, SEQ], F32R), ("y_lo", [P, KC, BATCH, SEQ], F32R),
             ("b_all", [2 * RANK + 1, G, FEAT], F32)],
            [("v_sb", [P, G, 512], F32), ("p_blocks", [P, QUAD, G, P], F32),
             ("attn_hi", [P, QUAD, TOK], F32R), ("attn_lo", [P, QUAD, TOK], F32R),
             ("wo_hi", [P, QUAD, FEAT], F32R), ("wo_lo", [P, QUAD, FEAT], F32R)])
        small = sb("small", [P, 16, 32])
        SM = {n: i for i, n in enumerate("log_dt dt ea xr th den rden thx ex t0 t1 er ei nr ni t2".split())}
        SM["cr2"], SM["ci2"] = SM["xr"], SM["th"]

        def sm(name, lo=0, hi=P):
            return small[lo:hi, SM[name], :]

        x_in = [sem(f"x_in{n}") for n in range(4)]
        cond_in, prm_in, c_in, misc_in = sem("cond_in"), sem("prm_in"), sem("c_in"), sem("misc_in")
        c_dup = sem("c_dup")
        const_ok, sel_const = sem("const_ok"), sem("sel_const")
        condf_ok, hot_ok, mixt_ok = sem("condf_ok"), sem("hot_ok"), sem("mixt_ok")
        zero_ok, sumsq_set = sem("zero_ok"), sem("sumsq_set")
        prm_mm, prm_ok = sem("prm_mm"), sem("prm_ok")
        mixw_mm, mixw_ok = sem("mixw_mm"), sem("mixw_ok")
        mix_mm, mixhi_ok, mixlo_ok = sem("mix_mm"), sem("mixhi_ok"), sem("mixlo_ok")
        gqk_ok = sem("gqk_ok")
        w_in = [sem("w_in0"), sem("w_in1")]
        whi_ok, wlo_ok = sem("whi_ok"), sem("wlo_ok")
        q_mm, k_mm, s_mm = sem("q_mm"), sem("k_mm"), sem("s_mm")
        q_sq, k_sq, q_ok, k_ok, s_ok, sum_ok = (sem(n) for n in ("q_sq", "k_sq", "q_ok", "k_ok", "s_ok", "sum_ok"))
        ssm, ang_ok, fn_ok, tab_ok = (sem(n) for n in ("ssm", "ang_ok", "fn_ok", "tab_ok"))
        kern_mm, kern_ok, kern_d, kpad_out = sem("kern_mm"), sem("kern_ok"), sem("kern_d"), sem("kpad_out")
        vk_mm, vq_mm, var_ok, std_ok, norm = (sem(n) for n in ("vk_mm", "vq_mm", "var_ok", "std_ok", "norm"))
        bo_in, acc_set = sem("bo_in"), sem("acc_set")
        wv_in, wo_in = sem("wv_in"), sem("wo_in")
        wvhi_ok, wvlo_ok, wohi_ok, wolo_ok = sem("wvhi_ok"), sem("wvlo_ok"), sem("wohi_ok"), sem("wolo_ok")
        v_mm, v_ok, pv_mm, ahi_ok, alo_ok = (sem(n) for n in ("v_mm", "v_ok", "pv_mm", "ahi_ok", "alo_ok"))
        wo_mm, acc_ok = sem("wo_mm"), sem("acc_ok")
        blocks_zero, soft, e_ok, p_ok = sem("blocks_zero"), sem("soft"), sem("e_ok"), sem("p_ok")
        toep_in0, toep_in1, ffn_in, bias_in = (sem(n) for n in ("toep_in0", "toep_in1", "ffn_in", "bias_in"))
        la_in, lora_in, lora_tr, lora, b_turned, lora_out = (sem(n) for n in ("la_in", "lora_in", "lora_tr", "lora", "b_turned", "lora_out"))
        a_in, b_in, fhi_ok, flo_ok, yhi_ok, ylo_ok = (sem(n) for n in ("a_in", "b_in", "fhi_ok", "flo_ok", "yhi_ok", "ylo_ok"))
        mask_ok, x2p_ok, xt_mm = sem("mask_ok"), sem("x2p_ok"), sem("xt_mm")
        conv_mm, y_ok, ax_one, ax_mm, ax_ok = (sem(n) for n in ("conv_mm", "y_ok", "ax_one", "ax_mm", "ax_ok"))
        out_mm, out_ok = sem("out_mm"), sem("out_ok")
        out_dma = [sem("out_dma0"), sem("out_dma1")]

        x_rows = x.rearrange("(g p) f -> p g f", p=P)
        out_rows = out.rearrange("(g p) f -> g p f", p=P)
        wqk_cols = [w.rearrange("(c p) n -> p c n", p=P) for w in (wq, wk)]
        wv_cols = wv.rearrange("(c p) n -> p c n", p=P)
        wo_rows = wo.rearrange("(h d) n -> d h n", d=HD)

        def every_partition(ap, n, parts=P):
            return bass.AP(ap.tensor, 0, [[0, parts], [1, n]])

        def repeat(ap, axis, n):
            dims = [list(d) for d in ap.ap]
            dims.insert(axis, [0, n])
            return bass.AP(ap.tensor, ap.offset, dims)

        def backwards(ap):
            dims = [list(d) for d in ap.ap]
            n = dims[-1][1]
            dims[-1] = [-1, n]
            return bass.AP(ap.tensor, ap.offset + n - 1, dims)

        def chunks_backwards(tile):
            return backwards(tile[:].rearrange("p h (c n) -> p (h c) n", n=P))

        def quadrant(b):
            return slice(32 * b, 32 * b + 32)

        block = ctx.enter_context(nc.Block())

        @block.sync
        def _(sp):
            def load_x(n):
                sp.dma_start(x_nat[:, 2 * n:2 * n + 2, :], x_rows[:, 2 * n:2 * n + 2, :]).then_inc(x_in[n], 16)

            load_x(0)
            load_x(1)

            def load_qk(h, slot):
                for m in range(2):
                    sp.dma_start(w_raw[:, slot, m], wqk_cols[m][:, :, bass.ds(h * HD, HD)]).then_inc(w_in[slot], 16)

            load_qk(0, 0)
            load_x(2)
            load_x(3)
            load_qk(1, 1)
            sp.dma_start(small[:, SM["log_dt"], :], every_partition(log_dt, 32)).then_inc(misc_in, 16)
            sp.dma_start(len_i[:], every_partition(lengths, BATCH)).then_inc(misc_in, 16)
            sp.dma_start(d_row[:], every_partition(ssm_d, 32, 1)).then_inc(misc_in, 16)
            sp.dma_start(gate_b[:].rearrange("p b n -> p (b n)"), every_partition(gate, G * NLORA)).then_inc(lora_in, 16)
            sp.dma_start(lbs_nat[:], lora_bs.rearrange("(c p) r -> p c r", p=P)).then_inc(lora_in, 16)
            for c in range(KC):
                sp.dma_start(lb_nat[:, c], lora_b.rearrange("n (c p) r -> c p n r", p=P)[c]).then_inc(lora_in, 16)
            for q in range(4):
                sp.dma_start(las_nat[quadrant(q)], lora_as.rearrange("r (c q f) -> q r c f", q=4, f=32)[q]).then_inc(la_in, 16)
                for c in range(KC):
                    cols = slice(P * c + 32 * q, P * c + 32 * q + 32)
                    sp.dma_start(la_nat[quadrant(q), c], lora_a[:, :, cols].rearrange("n r f -> r n f")).then_inc(la_in, 16)
            with sp.Fori(1, HEADS // 2) as i:
                for j in range(2):
                    sp.wait_ge(wlo_ok, i * 2 + (j - 1))
                    load_qk(i * 2 + j, j)

            def load_v(t):
                sp.dma_start(wv_raw[:], wv_cols[:, :, bass.ds(t * 512, 512)]).then_inc(wv_in, 16)

            def load_o(t):
                sp.dma_start(wo_raw[:], wo_rows[:, bass.ds(t * QUAD, QUAD), :]).then_inc(wo_in, 16)

            sp.wait_ge(lora, 4 * (NLORA - 1) + 2)
            sp.wait_ge(lora_tr, 3)
            load_v(0)
            sp.dma_start(a_scr[:, :, :, RANK:].rearrange("p c g r -> p (c g) r"),
                         a_sum[:].rearrange("p c g r -> p (c g) r")).then_inc(lora_out, 16)
            for c in range(KC):
                sp.dma_start(a_scr[:, c, :, 0:RANK], repeat(las_t[:, c, :], 1, G)).then_inc(lora_out, 16)
            sp.wait_ge(b_turned, 1)
            for q in range(4):
                sp.dma_start(b_scr.rearrange("r g (c q o) -> q r (g c) o", q=4, o=32)[q],
                             b_out[quadrant(q)].rearrange("r g c o -> r (g c) o")).then_inc(lora_out, 16)
                sp.dma_start(bs_scr.rearrange("r (c q o) -> q r c o", q=4, o=32)[q], lbs_t[quadrant(q)]).then_inc(lora_out, 16)
            sp.wait_ge(lora_out, 16 * 13)
            load_o(0)
            sp.wait_ge(kern_d, 2)
            sp.dma_start(kpad[:, 0:P], kzero[:, :]).then_inc(kpad_out, 16)
            sp.dma_start(kpad[:, P:].rearrange("h (a c) -> a h c", a=CA), k_sb[:]).then_inc(kpad_out, 16)
            with sp.Fori(1, NQ) as t:
                sp.wait_ge(wvlo_ok, t)
                load_v(t)
                sp.wait_ge(wolo_ok, t)
                load_o(t)
            sp.wait_ge(kpad_out, 32)
            sp.wait_ge(soft, 6 * (NQ - 1) + 1)
            sp.dma_start(toep0[:], bass.AP(kpad.tensor, 1, [[1, P], [PADL, 16], [1, 512]])).then_inc(toep_in0, 16)
            sp.wait_ge(wvlo_ok, NQ)
            sp.dma_start(ffn_raw[:], ffn_w.rearrange("(c p) n -> p c n", p=P)).then_inc(ffn_in, 16)
            sp.wait_ge(v_mm, G * NQ)
            sp.dma_start(toep1[:], bass.AP(kpad.tensor, 16 * PADL + 1, [[1, P], [PADL, 16], [1, 512]])).then_inc(toep_in1, 16)
            sp.wait_ge(wolo_ok, NQ)
            sp.dma_start(a_all[:].rearrange("p c g r -> p (c g r)"), a_scr.rearrange("p c g r -> p (c g r)")).then_inc(a_in, 16)
            sp.wait_ge(wo_mm, G * NQ)
            sp.dma_start(b_all[0:RANK], bass.AP(bs_scr.tensor, 0, [[FEAT, RANK], [0, G], [1, FEAT]])).then_inc(b_in, 16)
            sp.dma_start(b_all[RANK:2 * RANK].rearrange("r g o -> r (g o)"),
                         b_scr.rearrange("r g o -> r (g o)")).then_inc(b_in, 16)
            sp.dma_start(b_all[2 * RANK:2 * RANK + 1], bass.AP(ffn_b.tensor, 0, [[0, 1], [0, G], [1, FEAT]])).then_inc(bias_in, 16)
            for g in range(G):
                sp.wait_ge(out_ok, g + 1)
                sp.dma_start(out_rows[g], o_stage[:, g % 2, :]).then_inc(out_dma[g % 2], 16)
            for n in range(2):
                sp.wait_ge(out_dma[n], 16 * G // 2)

        @block.gpsimd
        def _(pool):
            gp = nc.gpsimd
            gp.iota(cond_no[:], [[0, 1]], base=0, channel_multiplier=1,
                    allow_small_or_imprecise_dtypes=True).then_inc(sel_const, 1)
            pool.wait_ge(sel_const, 1)
            gp.memset(ident[:], 0.0).then_inc(const_ok, 1)
            pool.wait_ge(const_ok, 1)
            gp.affine_select(out=ident[:], in_=ident[:], compare_op=ALU.not_equal, fill=1.0, base=0,
                             pattern=[[-1, P]], channel_multiplier=1).then_inc(const_ok, 1)
            pool.wait_ge(c_in, 16)
            for part in range(2):
                src = prm_nat[:, 9, :].rearrange("h (n two) -> h n two", two=2)[:, :, part]
                gp.tensor_copy(prm_nat[:, 7 + part, :].rearrange("h (d n) -> h d n", d=2),
                               repeat(src, 1, 2)).then_inc(c_dup, 1)
            gp.memset(ones[:], 1.0).then_inc(const_ok, 1)
            gp.memset(sumsq[:], 0.0).then_inc(sumsq_set, 1)

            pool.wait_ge(misc_in, 48)
            count = [0]

            def step(ins):
                count[0] += 1
                ins.then_inc(ssm, 1)
                pool.wait_ge(ssm, count[0])

            gp.iota(lidx[:], [[P, KC]], base=0, channel_multiplier=1, allow_small_or_imprecise_dtypes=True)
            step(gp.tensor_copy(len_f[:], len_i[:]))
            for c in range(KC):
                last = gp.tensor_scalar(mask[:, c, :], len_f[:], lidx[:, c:c + 1], None, ALU.is_gt)
            last.then_inc(mask_ok, 1)
            pool.wait_ge(prm_ok, 1)
            gp.tensor_tensor(gqk[:], param("gq"), param("gk"), ALU.mult).then_inc(gqk_ok, 1)

            gp.iota(mult[:, 0:32], [[1, 32]], base=0, channel_multiplier=0, allow_small_or_imprecise_dtypes=True)
            gp.iota(mult[:, 32:64], [[0, 2], [32, 16]], base=0, channel_multiplier=0, allow_small_or_imprecise_dtypes=True)
            gp.memset(mult[:, 64:66], 1.0)
            step(gp.memset(mult[:, 66:67], 0.5))
            step(gp.memset(quarter[:], 0.0))
            step(gp.memset(quarter[0:64, 0:32], 0.25))
            step(gp.memset(quarter[:, 48:64], 0.25))
            step(gp.memset(quarter[:, 65:66], 0.25))
            def exp_in_place(x, k, poly):
                step(gp.tensor_scalar(x, x, 88.0, -87.0, ALU.min, ALU.max))
                step(gp.tensor_scalar(k, x, 1.4426950408889634, None, ALU.mult))
                step(gp.tensor_scalar(k, k, MAGIC, None, ALU.add))
                step(gp.tensor_scalar(k, k, -MAGIC, None, ALU.add))
                for part in (LN2_HI, LN2_LO):
                    step(gp.tensor_scalar(poly, k, -part, None, ALU.mult))
                    step(gp.tensor_tensor(x, x, poly, ALU.add))
                step(gp.tensor_scalar(poly, x, EXP_COEFFS[0], EXP_COEFFS[1], ALU.mult, ALU.add))
                for coeff in EXP_COEFFS[2:]:
                    step(gp.tensor_tensor(poly, poly, x, ALU.mult))
                    step(gp.tensor_scalar(poly, poly, coeff, None, ALU.add))
                step(gp.tensor_scalar(k, k, 127.0, None, ALU.add))
                step(gp.tensor_scalar(k.bitcast(I32), k, 8388608.0, None, ALU.mult))
                step(gp.tensor_tensor(x, poly, k, ALU.mult))

            step(gp.tensor_copy(sm("dt"), sm("log_dt")))
            exp_in_place(sm("dt"), sm("t0"), sm("t1"))
            step(gp.tensor_copy(sm("ea"), param("log_a")))
            exp_in_place(sm("ea"), sm("t0"), sm("t1"))
            step(gp.tensor_tensor(sm("t0"), sm("ea"), sm("dt"), ALU.mult))
            step(gp.tensor_scalar(sm("xr"), sm("t0"), -1.0, None, ALU.mult))
            step(gp.tensor_tensor(sm("th"), param("a_im"), sm("dt"), ALU.mult))
            step(gp.tensor_tensor(sm("t0"), sm("ea"), sm("ea"), ALU.mult))
            step(gp.tensor_tensor(sm("t1"), param("a_im"), param("a_im"), ALU.mult))
            step(gp.tensor_tensor(sm("den"), sm("t0"), sm("t1"), ALU.add))
            step(gp.memset(sm("t2"), -1.0))
            step(gp.tensor_tensor(sm("rden"), sm("den"), sm("t2"), ALU.pow))
            step(gp.tensor_copy(sm("ex"), sm("xr")))
            exp_in_place(sm("ex"), sm("t0"), sm("t1"))
            step(gp.tensor_tensor(ang[:], repeat(mult[:], 2, 32), repeat(sm("th"), 1, 67), ALU.mult))
            step(gp.tensor_tensor(expo[:], repeat(mult[:, 0:48], 2, 32), repeat(sm("xr"), 1, 48), ALU.mult))
            for a, b in ((0, 32), (32, 64), (64, 67)):
                k, pr, an = turns[:, 0:b - a, :], prod[:, 0:b - a, :], ang[:, a:b, :]
                qt = repeat(quarter[:, a:b], 2, 32)
                step(gp.tensor_scalar(k, an, 1.0 / (2 * PI), None, ALU.mult))
                step(gp.tensor_tensor(k, k, qt, ALU.add))
                step(gp.tensor_scalar(k, k, MAGIC, None, ALU.add))
                step(gp.tensor_scalar(k, k, -MAGIC, None, ALU.add))
                for part in (C1, C2, C3):
                    step(gp.tensor_scalar(pr, k, -part, None, ALU.mult))
                    step(gp.tensor_tensor(an, an, pr, ALU.add))
                step(gp.tensor_scalar(pr, qt, 2 * PI, None, ALU.mult))
                step(gp.tensor_tensor(an, an, pr, ALU.add))
                step(gp.tensor_scalar(an, an, PI_F32, -PI_F32, ALU.min, ALU.max))
            for a, b in ((0, 32), (32, 48)):
                exp_in_place(expo[:, a:b, :], turns[:, 0:b - a, :], prod[:, 0:b - a, :])
            gp.memset(sm("t2"), 0.0).then_inc(ang_ok, 1)
            pool.wait_ge(fn_ok, 2)
            sin_th, cos_th, sin_half = ang[:, 64, :], ang[:, 65, :], ang[:, 66, :]
            step(gp.tensor_scalar(sm("t0"), sm("ex"), 1.0, None, ALU.add))
            step(gp.tensor_tensor(sm("t0"), sm("t0"), sm("thx"), ALU.mult))
            step(gp.tensor_tensor(sm("er"), sm("t0"), cos_th, ALU.mult))
            step(gp.tensor_tensor(sm("t1"), sin_half, sin_half, ALU.mult))
            step(gp.tensor_scalar(sm("t1"), sm("t1"), -2.0, None, ALU.mult))
            step(gp.tensor_tensor(sm("er"), sm("er"), sm("t1"), ALU.add))
            step(gp.tensor_tensor(sm("ei"), sm("ex"), sin_th, ALU.mult))
            step(gp.tensor_tensor(sm("t0"), sm("ei"), param("a_im"), ALU.mult))
            step(gp.tensor_tensor(sm("t1"), sm("er"), sm("ea"), ALU.mult))
            step(gp.tensor_tensor(sm("nr"), sm("t0"), sm("t1"), ALU.subtract))
            step(gp.tensor_tensor(sm("t0"), sm("er"), param("a_im"), ALU.mult))
            step(gp.tensor_tensor(sm("t1"), sm("ei"), sm("ea"), ALU.mult))
            step(gp.tensor_tensor(sm("ni"), sm("t0"), sm("t1"), ALU.add))
            step(gp.tensor_scalar(sm("t2"), sm("rden"), 2.0, None, ALU.mult))
            step(gp.tensor_tensor(sm("nr"), sm("nr"), sm("t2"), ALU.mult))
            step(gp.tensor_tensor(sm("ni"), sm("ni"), sm("t2"), ALU.mult))
            step(gp.tensor_scalar(sm("ni"), sm("ni"), -1.0, None, ALU.mult))
            step(gp.tensor_tensor(sm("t0"), param("c_re"), sm("nr"), ALU.mult))
            step(gp.tensor_tensor(sm("t1"), param("c_im"), sm("ni"), ALU.mult))
            step(gp.tensor_tensor(sm("cr2"), sm("t0"), sm("t1"), ALU.subtract))
            step(gp.tensor_tensor(sm("t0"), param("c_re"), sm("ni"), ALU.mult))
            step(gp.tensor_tensor(sm("t1"), param("c_im"), sm("nr"), ALU.mult))
            step(gp.tensor_tensor(sm("ci2"), sm("t0"), sm("t1"), ALU.add))
            step(gp.tensor_copy(sm("er", 0, 64), sm("cr2", 0, 64)))
            step(gp.tensor_scalar(sm("er", 64, P), sm("ci2", 64, P), -1.0, None, ALU.mult))
            step(gp.tensor_scalar(sm("ei", 0, 64), sm("ci2", 0, 64), -1.0, None, ALU.mult))
            step(gp.tensor_scalar(sm("ei", 64, P), sm("cr2", 64, P), -1.0, None, ALU.mult))
            step(gp.tensor_tensor(expo[:, 0:32, :], expo[:, 0:32, :], ang[:, 0:32, :], ALU.mult))
            for cols, coeff in ((slice(32, 48), "ei"), (slice(48, 64), "er")):
                step(gp.tensor_tensor(ang[:, cols, :], ang[:, cols, :], expo[:, 32:48, :], ALU.mult))
                step(gp.tensor_tensor(ang[:, cols, :], ang[:, cols, :], repeat(sm(coeff), 1, 16), ALU.mult))
            gp.tensor_tensor(ang[:, 32:48, :], ang[:, 32:48, :], ang[:, 48:64, :], ALU.add).then_inc(tab_ok, 1)
            gp.memset(kzero[:], 0.0).then_inc(kern_d, 1)
            pool.wait_ge(kern_ok, 1)
            gp.tensor_tensor(k_sb[0:1, :, 0], k_sb[0:1, :, 0], d_row[:, :], ALU.add).then_inc(kern_d, 1)
            pool.wait_ge(bo_in, 16)
            for g in range(G):
                gp.tensor_tensor(backwards(acc[:, g, :].rearrange("p (c n) -> p c n", n=P)),
                                 x_nat[:, g, :].rearrange("p (c n) -> p c n", n=P),
                                 bo_rows[:].rearrange("p (c n) -> p c n", n=P), ALU.add).then_inc(acc_set, 1)
            pool.wait_ge(sum_ok, 2 * HEADS)
            gp.memset(p_blocks[:], 0.0).then_inc(blocks_zero, 1)
            pool.wait_ge(p_ok, NQ)
            gp.memset(ax[2 * RANK:2 * RANK + 1, :, :], 1.0).then_inc(ax_one, 1)

        @block.tensor
        def _(pe):
            mm = nc.tensor.matmul

            def product3(out, terms, close=True):
                last = None
                for n, (lh, ll, rh, rl) in enumerate(terms):
                    mm(out, lh, rh, start=(n == 0), stop=False)
                    mm(out, lh, rl, start=False, stop=False)
                    last = mm(out, ll, rh, start=False, stop=(close and n == len(terms) - 1))
                return last

            pe.wait_ge(cond_in, 32)
            pe.wait_ge(hot_ok, 1)
            for n in range(2):
                last = mm(bank(n), onehot[:].rearrange("n q b -> n (q b)"), cond_nat[:, 512 * n:512 * n + 512],
                          start=True, stop=True)
            last.then_inc(mixw_mm, 1)

            pe.wait_ge(mixw_ok, 1)
            for g in range(G):
                pe.wait_ge(x_in[g // 2], 16)
                if g >= 6:
                    pe.wait_ge(mixlo_ok, g - 5)
                for c in range(KC):
                    last = mm(bank(2 + g % 6)[:, P * c:P * c + P], x_nat[:, g, P * c:P * c + P],
                              mix_w[:, g, :], start=True, stop=True)
                last.then_inc(mix_mm, 1)

            pe.wait_ge(mixt_ok, 1)
            pe.wait_ge(const_ok, 2)
            pe.wait_ge(prm_in, 16 * 9)
            pe.wait_ge(c_dup, 2)
            for n in range(9):
                last = nc.tensor.transpose(bank(1)[:, 32 * n:32 * n + 32], prm_nat[:, n, :], ident[0:32, 0:32])
            last.then_inc(prm_mm, 1)

            def head_scores(h, slot):
                pe.wait_ge(q_ok, h * 2 + 2)
                pe.wait_ge(k_ok, h * 2 + 2)
                if not (isinstance(h, int) and h < 1):
                    pe.wait_ge(s_ok, h)
                for g in range(G):
                    last = mm(bank(4, 1024)[:, P * g:P * g + P], qk_sb[:, slot, 0, P * g:P * g + P],
                              qk_sb[:, slot, 1, P * g:P * g + P], start=True, stop=True)
                last.then_inc(s_mm, 1)

            def head_qk(h, slot, first=False):
                pe.wait_ge(wlo_ok, h + 1)
                for m, (done, free) in enumerate(((q_mm, q_ok), (k_mm, k_ok))):
                    for n in range(2):
                        if not first:
                            pe.wait_ge(free, h * 2 + (n - 1))
                        elif m == 0:
                            pe.wait_ge(mixlo_ok, 4 * n + 4)
                        product3(bank(2 * m + n),
                                 [(w_hi[:, slot, m, c, :], w_lo[:, slot, m, c, :],
                                   mix_hi[:, c, HALF * n:HALF * n + HALF], mix_lo[:, c, HALF * n:HALF * n + HALF])
                                  for c in range(KC)]).then_inc(done, 1)
                        if m == 0 and n == 0 and not first:
                            head_scores(h - 1, 1 - slot)

            pe.wait_ge(prm_ok, 1)
            head_qk(0, 0, first=True)
            head_qk(1, 1)
            with pe.Fori(1, HEADS // 2 - 1) as i:
                for j in range(2):
                    head_qk(i * 2 + j, j)
            head_qk(HEADS - 2, 0)
            pe.wait_ge(tab_ok, 1)
            for h in range(SEQ):
                last = mm(bank(6, 1024)[0:CA, CL * h:CL * h + CL], ang[:, 32:48, h], expo[:, 0:CL, h],
                          start=True, stop=True)
            last.then_inc(kern_mm, 1)
            head_qk(HEADS - 1, 1)
            head_scores(HEADS - 1, 1)

            def value_group(t, g, free=True):
                if free:
                    pe.wait_ge(v_ok, t * G + (g - 1))
                product3(bank(g % 2),
                         [(mix_hi[:, c, P * g:P * g + P], mix_lo[:, c, P * g:P * g + P],
                           wv_hi[:, c, :], wv_lo[:, c, :]) for c in range(KC)]).then_inc(v_mm, 1)

            def attend(t, first=False):
                pe.wait_ge(p_ok, t + 1)
                pe.wait_ge(v_ok, t * G + G)
                for u in range(8):
                    h, half = u % QUAD, u // QUAD
                    if not (first and u < 4):
                        pe.wait_ge(alo_ok, t * 8 + (u - 3))
                    for g in range(4 * half, 4 * half + 4):
                        last = mm(bank(2 + u % 4)[:, P * (g % 4):P * (g % 4) + P],
                                  v_sb[:, g, HD * h:HD * h + HD], p_blocks[:, h, g, :], start=True, stop=True)
                    last.then_inc(pv_mm, 1)

            def project_group(t, g, free=True):
                if free:
                    pe.wait_ge(acc_ok, t * 8 + (g - 1))
                tok = slice(P * g, P * g + P)
                product3(bank(6 + g % 2),
                         [(attn_hi[:, h, tok], attn_lo[:, h, tok], wo_hi[:, h, :], wo_lo[:, h, :])
                          for h in range(QUAD)]).then_inc(wo_mm, 1)

            def project(t, first=False):
                pe.wait_ge(wolo_ok, t + 1)
                pe.wait_ge(alo_ok, t * 8 + 8)
                for g in range(G):
                    project_group(t, g, free=not (first and g < 2))

            pe.wait_ge(q_ok, 2 * HEADS)
            pe.wait_ge(wvlo_ok, 1)
            value_group(0, 0, free=False)
            pe.wait_ge(sum_ok, 2 * HEADS)
            pe.wait_ge(kern_ok, 1)
            for n in range(2):
                last = mm(bank(6 + n), ones[:, :], sumsq[:, 1, HALF * n:HALF * n + HALF], start=True, stop=True)
            last.then_inc(vk_mm, 1)
            pe.wait_ge(k_ok, 2 * HEADS)
            for g in range(G):
                last = mm(bank(2)[:, g:g + 1], sumsq[:, 0, P * g:P * g + P], ones[:, 0:1], start=True, stop=True)
            last.then_inc(vq_mm, 1)
            value_group(0, 1, free=False)
            for g in range(2, G):
                value_group(0, g)
            pe.wait_ge(var_ok, 5)
            pe.wait_ge(s_ok, HEADS)
            attend(0, first=True)
            pe.wait_ge(wvlo_ok, 2)
            for g in range(G):
                value_group(1, g)
            project(0, first=True)
            with pe.Fori(1, NQ - 1) as t:
                attend(t)
                pe.wait_ge(wvlo_ok, t + 2)
                for g in range(G):
                    value_group(t + 1, g)
                project(t)
            attend(NQ - 1)
            def transpose_x2(g):
                pe.wait_ge(acc_ok, 8 * (NQ - 1) + g + 1)
                if g >= 4:
                    pe.wait_ge(x2p_ok, g - 3)
                for c in range(KC):
                    last = nc.tensor.transpose(bank(2 + g % 4)[:, P * c:P * c + P], acc[:, g, P * c:P * c + P],
                                               ident[:, :])
                last.then_inc(xt_mm, 1)

            pe.wait_ge(wolo_ok, NQ)
            for g in range(G):
                if g % 4 == 0:
                    pe.wait_ge(alo_ok, 8 * (NQ - 1) + 4 + g)
                project_group(NQ - 1, g)
                if g >= 2:
                    transpose_x2(g - 2)

            transpose_x2(6)
            transpose_x2(7)

            pe.wait_ge(x2p_ok, G)
            for s in range(SEQ):
                if s % 4 == 0:
                    u = s // 4
                    if u >= 2:
                        pe.wait_ge(y_ok, u - 1)
                    if s == 0:
                        pe.wait_ge(toep_in0, 16)
                    if s == 16:
                        pe.wait_ge(toep_in1, 16)
                toep = toep0 if s < 16 else toep1
                for d in range(KC):
                    last = mm(bank(2 + (s // 4) % 2)[:, P * (s % 4) + 32 * d:P * (s % 4) + P],
                              toep[:, s % 16, P * d:P * d + P], x2p[:, s, 0:KC - d, :],
                              start=(d == 0), stop=(d == KC - 1), skip_group_check=True)
                if s % 4 == 3:
                    last.then_inc(conv_mm, 1)

            def down(g):
                if g >= 2:
                    pe.wait_ge(ax_ok, g - 1)
                for c in range(KC):
                    last = mm(bank(4 + g % 2)[0:2 * RANK, 0:P], a_all[:, c, g, :],
                              y_t[:, c, BPG * g:BPG * g + BPG, :], start=(c == 0), stop=(c == KC - 1))
                last.then_inc(ax_mm, 1)

            pe.wait_ge(y_ok, 8)
            pe.wait_ge(a_in, 16)
            down(0)
            down(1)
            pe.wait_ge(yhi_ok, 8)
            pe.wait_ge(ylo_ok, 8)
            pe.wait_ge(fhi_ok, 1)
            pe.wait_ge(flo_ok, 1)
            for g in range(G):
                o = bank(6 + g % 2)
                if g >= 2:
                    pe.wait_ge(out_ok, g - 1)
                batches = slice(BPG * g, BPG * g + BPG)
                product3(o, [(y_hi[:, c, batches, :], y_lo[:, c, batches, :], ffn_hi[:, c, :], ffn_lo[:, c, :])
                             for c in range(KC)], close=False)
                pe.wait_ge(ax_ok, g + 1)
                if g == 0:
                    pe.wait_ge(ax_one, 1)
                    pe.wait_ge(bias_in, 16)
                    pe.wait_ge(b_in, 32)
                mm(o, ax[:, g % 2, :], b_all[:, g, :], start=False, stop=True).then_inc(out_mm, 1)
                if g + 2 < G:
                    down(g + 2)

        @block.scalar
        def _(act):
            sc = nc.scalar
            spacer = act.alloc_register("spacer")

            def here(index):
                if isinstance(index, int):
                    return index
                act.reg_mov(spacer, index)
                return act.snap(spacer, min_val=0, max_val=HEADS - 1)
            act.dma_start(cond_i[:], every_partition(cond_idx, BATCH, NCOND)).then_inc(cond_in, 16)
            act.dma_start(cond_nat[:], cond_w.rearrange("n c d -> n (c d)")).then_inc(cond_in, 16)
            act.dma_start(prm_nat[:, 9, :], ssm_c.rearrange("h n two -> h (n two)")).then_inc(c_in, 16)
            for n, v in enumerate((bq, bk, gq, gk, bv)):
                act.dma_start(prm_nat[:, n, :], v.rearrange("(h d) -> h d", d=HD)).then_inc(prm_in, 16)
            for n, v in ((5, log_a), (6, a_im)):
                for k in range(2):
                    act.dma_start(prm_nat[:, n, NSTATE * k:NSTATE * k + NSTATE], v).then_inc(prm_in, 16)

            def split_hi(h, slot):
                for m in range(2):
                    last = sc.activation(w_hi[:, slot, m].rearrange("p c n -> p (c n)"),
                                         w_raw[:, slot, m].rearrange("p c n -> p (c n)"), ACT.Copy)
                last.then_inc(whi_ok, 1)

            act.wait_ge(w_in[0], 32)
            split_hi(0, 0)
            for g in range(G):
                act.wait_ge(mix_mm, g + 1)
                sc.activation(mix_hi[:, :, P * g:P * g + P],
                              bank(2 + g % 6).rearrange("p (c t) -> p c t", c=KC), ACT.Copy).then_inc(mixhi_ok, 1)
            act.wait_ge(prm_mm, 1)
            sc.activation(params[:].rearrange("p n h -> p (n h)"), bank(1, 288), ACT.Copy).then_inc(prm_ok, 1)


            def head(h, slot, first=False, last_head=False, w_count=None):
                if not last_head:
                    act.wait_ge(w_in[1 - slot], w_count)
                    if not first:
                        act.wait_ge(k_mm, h * 2)
                    split_hi(h + 1, 1 - slot)
                for n in range(2):
                    tok = slice(HALF * n, HALF * n + HALF)
                    act.wait_ge(q_mm, h * 2 + n + 1)
                    if n == 0 and not (isinstance(h, int) and h < 2):
                        act.wait_ge(sum_ok, h * 2 - 2)
                    at = here(h)
                    sc.activation(sq[:, slot, 0, tok], bank(n), ACT.Square,
                                  bias=params[:, PARAM["bq"], bass.ds(at, 1)]).then_inc(q_sq, 1)
                for n in range(2):
                    tok = slice(HALF * n, HALF * n + HALF)
                    act.wait_ge(k_mm, h * 2 + n + 1)
                    at = here(h)
                    sc.activation(sq[:, slot, 1, tok], bank(2 + n), ACT.Square,
                                  bias=params[:, PARAM["bk"], bass.ds(at, 1)]).then_inc(k_sq, 1)
                    if n == 0 and not (isinstance(h, int) and h < 2):
                        act.wait_ge(s_mm, h - 1)
                    at = here(h)
                    sc.activation(qk_sb[:, slot, 1, tok], bank(2 + n), ACT.Identity,
                                  bias=params[:, PARAM["bk"], bass.ds(at, 1)]).then_inc(k_ok, 1)

            def heads(lo, hi):
                with act.Fori(lo, hi) as i:
                    head(i * 2, 0, w_count=i * 32 + 32)
                    head(i * 2 + 1, 1, w_count=i * 32 + 64)

            head(0, 0, first=True, w_count=32)
            head(1, 1, w_count=64)
            heads(1, 12)
            act.wait_ge(ang_ok, 1)
            sc.activation(sm("thx"), sm("xr"), ACT.Tanh, scale=0.5).then_inc(fn_ok, 1)
            sc.activation(ang[:], ang[:], ACT.Sin).then_inc(fn_ok, 1)
            heads(12, HEADS // 2 - 1)
            head(HEADS - 2, 0, w_count=16 * HEADS)
            act.wait_ge(kern_mm, 1)
            act.wait_ge(kern_d, 1)
            sc.activation(k_sb[:].rearrange("a h c -> a (h c)"), bank(6, 1024)[0:CA, :], ACT.Copy).then_inc(kern_ok, 1)
            act.dma_start(bo_rows[:], every_partition(bo, FEAT)).then_inc(bo_in, 16)
            act.wait_ge(wv_in, 16)
            act.wait_ge(lora_out, 16 * 13)
            sc.activation(wv_hi[:].rearrange("p c n -> p (c n)"), wv_raw[:].rearrange("p c n -> p (c n)"),
                          ACT.Copy).then_inc(wvhi_ok, 1)
            head(HEADS - 1, 1, last_head=True)

            def value_out(t, g):
                act.wait_ge(v_mm, t * G + (g + 1))
                sc.activation(v_sb[:, g, :], bank(g % 2), ACT.Copy).then_inc(v_ok, 1)

            def exp_scores(t):
                act.wait_ge(soft, t * 6 + 3)
                sc.activation(sm_e[:], sm_s[:], ACT.Exp).then_inc(e_ok, 1)

            def attn_out(t, units=range(8)):
                for u in units:
                    h, half = u % QUAD, u // QUAD
                    act.wait_ge(pv_mm, t * 8 + (u + 1))
                    at = here(t * QUAD + h)
                    sc.activation(attn_hi[:, h, HALF * half:HALF * half + HALF], bank(2 + u % 4), ACT.Identity,
                                  bias=params[:, PARAM["bv"], bass.ds(at, 1)]).then_inc(ahi_ok, 1)

            def split_o(t):
                act.wait_ge(wo_in, t * 16 + 16)
                sc.activation(chunks_backwards(wo_hi), wo_raw[:].rearrange("p h (c n) -> p (h c) n", n=P),
                              ACT.Copy).then_inc(wohi_ok, 1)

            def split_v(t):
                act.wait_ge(wv_in, t * 16 + 16)
                act.wait_ge(v_mm, t * G)
                sc.activation(wv_hi[:].rearrange("p c n -> p (c n)"), wv_raw[:].rearrange("p c n -> p (c n)"),
                              ACT.Copy).then_inc(wvhi_ok, 1)

            value_out(0, 0)
            act.wait_ge(norm, 1)
            sc.activation(var_k[:], inv_norm[:], ACT.Sqrt).then_inc(std_ok, 1)
            for g in range(1, 4):
                value_out(0, g)
            act.wait_ge(acc_set, G)
            exp_scores(0)
            for g in range(4, G):
                value_out(0, g)
            split_v(1)

            def quad(t):
                attn_out(t)
                split_o(t)
                for g in range(5):
                    value_out(t + 1, g)
                exp_scores(t + 1)
                for g in range(5, G):
                    value_out(t + 1, g)

            quad(0)
            split_v(2)
            with act.Fori(1, NQ - 2) as t:
                quad(t)
                split_v(t + 2)
            quad(NQ - 2)
            attn_out(NQ - 1, range(4))
            split_o(NQ - 1)
            attn_out(NQ - 1, range(4, 8))

            def x2_out(g):
                act.wait_ge(xt_mm, g + 1)
                sc.activation(x2p[:, :, :, BPG * g:BPG * g + BPG].rearrange("p s c b -> p c b s"),
                              bank(2 + g % 4).rearrange("p (c b s) -> p c b s", c=KC, b=BPG), ACT.Copy).then_inc(x2p_ok, 1)

            for g in range(G):
                x2_out(g)
            act.wait_ge(ffn_in, 16)
            act.wait_ge(v_mm, G * NQ)
            sc.activation(ffn_hi[:].rearrange("p c n -> p (c n)"), ffn_raw[:].rearrange("p c n -> p (c n)"),
                          ACT.Copy).then_inc(fhi_ok, 1)
            for u in range(8):
                act.wait_ge(y_ok, u + 1)
                part = slice(4 * u, 4 * u + 4)
                sc.activation(y_hi[:, :, :, part], y_t[:, :, :, part], ACT.Copy).then_inc(yhi_ok, 1)

        @block.vector
        def _(dve):
            v = nc.vector
            v.memset(mix_w[:], 0.0).then_inc(zero_ok, 1)
            dve.wait_ge(cond_in, 32)
            v.tensor_copy(cond_f[:], cond_i[:]).then_inc(condf_ok, 1)
            dve.wait_ge(condf_ok, 1)
            dve.wait_ge(sel_const, 1)
            v.tensor_scalar(onehot[:], repeat(cond_f[:], 1, BPG), cond_no[:, 0:1], None, ALU.is_equal).then_inc(hot_ok, 1)

            def split_lo(h, slot):
                dve.wait_ge(whi_ok, h + 1)
                for m in range(2):
                    last = v.tensor_tensor(w_lo[:, slot, m].rearrange("p c n -> p (c n)"),
                                           w_raw[:, slot, m].rearrange("p c n -> p (c n)"),
                                           w_hi[:, slot, m].rearrange("p c n -> p (c n)").bitcast(F32), ALU.subtract)
                last.then_inc(wlo_ok, 1)

            dve.wait_ge(mixw_mm, 1)
            v.transpose(mix_t[:], bank(0, 1024).rearrange("p (c d) -> p d c", d=32)).then_inc(mixt_ok, 1)
            dve.wait_ge(mixt_ok, 1)
            dve.wait_ge(zero_ok, 1)
            for b in range(BPG):
                last = v.tensor_copy(mix_w[quadrant(b), :, quadrant(b)],
                                     mix_t[quadrant(b)].rearrange("p d (g b) -> p g d b", b=BPG)[:, :, :, b])
            last.then_inc(mixw_ok, 1)
            split_lo(0, 0)
            for g in range(G):
                tok = slice(P * g, P * g + P)
                dve.wait_ge(mixhi_ok, g + 1)
                v.tensor_tensor(mix_lo[:, :, tok], bank(2 + g % 6).rearrange("p (c t) -> p c t", c=KC),
                                mix_hi[:, :, tok].bitcast(F32), ALU.subtract).then_inc(mixlo_ok, 1)

            def extract(h):
                dve.wait_ge(s_mm, h + 1)
                dst = scores[:].rearrange("p h g k -> p (h g k)")[:, bass.ds(h * (G * 32), G * 32)]
                for b in range(BPG):
                    src = bank(4, 1024)[quadrant(b), :].rearrange("p (g k) -> p g k", g=G)[:, :, quadrant(b)]
                    last = v.tensor_copy(dst[quadrant(b), :].rearrange("p (g k) -> p g k", g=G), src)
                last.then_inc(s_ok, 1)

            def head(h, slot, first=False, last_head=False):
                if not last_head:
                    if not first:
                        dve.wait_ge(k_mm, h * 2)
                    split_lo(h + 1, 1 - slot)
                for n in range(2):
                    tok = slice(HALF * n, HALF * n + HALF)
                    dve.wait_ge(q_sq, h * 2 + n + 1)
                    if n == 0 and not (isinstance(h, int) and h < 2):
                        dve.wait_ge(s_mm, h - 1)
                    v.tensor_scalar(qk_sb[:, slot, 0, tok], bank(n), params[:, PARAM["bq"], bass.ds(h, 1)],
                                    gqk[:, bass.ds(h, 1)], ALU.add, ALU.mult).then_inc(q_ok, 1)
                    if n == 0 and not first:
                        if isinstance(h, int) and h == 1:
                            dve.wait_ge(mask_ok, 1)
                        extract(h - 1)
                for m, done in enumerate((q_sq, k_sq)):
                    if m == 1:
                        dve.wait_ge(done, h * 2 + 2)
                    if not first:
                        dve.wait_ge(sum_ok, h * 2 + (m - 1))
                    v.tensor_tensor(sumsq[:, m, :], sumsq[:, m, :], sq[:, slot, m, :], ALU.add).then_inc(sum_ok, 1)

            dve.wait_ge(gqk_ok, 1)
            dve.wait_ge(sumsq_set, 1)
            def mix_lora(n, which, first=False):
                gates = gate_b[:, :, bass.ds(n, 1)].rearrange("p g n -> p (g n)")
                if which == 0:
                    weights = repeat(la_t[:, :, bass.ds(n, 1), :].rearrange("p c n r -> p c (n r)"), 2, G)
                    gates = repeat(repeat(gates, 2, RANK), 1, KC)
                    total, dims = a_sum[:], dict(x=KC, y=G)
                else:
                    weights = repeat(lb_nat[:, :, bass.ds(n, 1), :].rearrange("p c n r -> p c (n r)"), 1, G)
                    gates = repeat(repeat(gates, 2, RANK), 2, KC)
                    total, dims = b_sum[:], dict(x=G, y=KC)
                term = total if first else gated[:].rearrange("p (x y r) -> p x y r", **dims)
                if not first:
                    dve.wait_ge(lora, n * 4 + (2 * which - 2))
                v.tensor_tensor(term, weights, gates, ALU.mult).then_inc(lora, 1)
                if not first:
                    dve.wait_ge(lora, n * 4 + (2 * which - 1))
                    v.tensor_tensor(total, total, term, ALU.add).then_inc(lora, 1)

            head(0, 0, first=True)
            head(1, 1)
            dve.wait_ge(la_in, 16 * 20)
            v.transpose(la_t[:].rearrange("p c n r -> p (c n) r"), la_nat[:].rearrange("p c n f -> p (c n) f")).then_inc(lora_tr, 1)
            v.transpose(las_t[:], las_nat[:]).then_inc(lora_tr, 1)
            dve.wait_ge(lora_in, 16 * 6)
            v.transpose(lbs_t[:], lbs_nat[:]).then_inc(lora_tr, 1)
            dve.wait_ge(lora_tr, 1)
            mix_lora(0, 0, first=True)
            mix_lora(0, 1, first=True)
            with dve.Fori(1, HEADS // 2 - 4) as i:
                for j in range(2):
                    head(i * 2 + j, j)
                    mix_lora(i, j)
            with dve.Fori(HEADS // 2 - 4, HEADS // 2 - 2) as i:
                for j in range(2):
                    head(i * 2 + j, j)
                    for which in range(2):
                        mix_lora(i * 2 + (j + NLORA - HEADS + 4), which)
            dve.wait_ge(lora, 4 * (NLORA - 1) + 2)
            v.transpose(b_out[:].rearrange("p g c o -> p (g c) o"), b_sum[:].rearrange("p g c r -> p (g c) r")).then_inc(b_turned, 1)
            for j in range(3):
                head(HEADS - 4 + j, j % 2)

            def split_v(t, parts=(0, 1, 2, 3)):
                if 0 in parts:
                    dve.wait_ge(wvhi_ok, t + 1)
                for c in parts:
                    last = v.tensor_tensor(wv_lo[:, c, :], wv_raw[:, c, :], wv_hi[:, c, :].bitcast(F32), ALU.subtract)
                if KC - 1 in parts:
                    last.then_inc(wvlo_ok, 1)

            dve.wait_ge(lora_out, 16 * 13)
            split_v(0)
            head(HEADS - 1, 1, last_head=True)

            dve.wait_ge(vk_mm, 1)
            for b in range(BPG):
                src = bank(6, 1024)[quadrant(b), :].rearrange("p (g k) -> p g k", g=G)[:, :, quadrant(b)]
                v.tensor_scalar(var_k[quadrant(b)], src, 1.0 / INNER, RMS_EPS, ALU.mult, ALU.add).then_inc(var_ok, 1)
            dve.wait_ge(vq_mm, 1)
            v.tensor_scalar(var_q[:], bank(2, G), 1.0 / INNER, RMS_EPS, ALU.mult, ALU.add).then_inc(var_ok, 1)
            dve.wait_ge(var_ok, 5)
            v.scalar_tensor_tensor(inv_norm[:], var_k[:], float(HD), repeat(var_q[:], 2, 32),
                                   ALU.mult, ALU.mult).then_inc(norm, 1)
            dve.wait_ge(std_ok, 1)
            tmp = sm_s[:, 0]
            dve.wait_ge(kpad_out, 32)
            v.reciprocal(tmp, var_k[:]).then_inc(norm, 1)
            dve.wait_ge(norm, 2)
            v.tensor_tensor(tmp, tmp, inv_norm[:], ALU.mult).then_inc(norm, 1)
            dve.wait_ge(norm, 3)
            v.tensor_tensor(tmp, tmp, var_k[:], ALU.add).then_inc(norm, 1)
            dve.wait_ge(norm, 4)
            v.tensor_scalar(tmp, tmp, 0.5, None, ALU.mult).then_inc(norm, 1)
            dve.wait_ge(norm, 5)
            v.reciprocal(inv_norm[:], tmp).then_inc(norm, 1)
            dve.wait_ge(norm, 6)
            extract(HEADS - 1)

            def flat(tile):
                return tile[:].rearrange("p h g k -> p (h g) k")

            def soft_max(t):
                src = scores[:].rearrange("p h g k -> p (h g k)")[:, bass.ds(t * (QUAD * G * 32), QUAD * G * 32)]
                v.tensor_tensor(sm_s[:].rearrange("p h g k -> p h (g k)"),
                                src.rearrange("p (h n) -> p h n", h=QUAD),
                                repeat(inv_norm[:].rearrange("p g k -> p (g k)"), 1, QUAD), ALU.mult).then_inc(soft, 1)
                dve.wait_ge(soft, t * 6 + 1)
                v.tensor_reduce(row_max[:], flat(sm_s), AX_X, ALU.max).then_inc(soft, 1)
                dve.wait_ge(soft, t * 6 + 2)
                v.tensor_tensor(flat(sm_s), flat(sm_s), repeat(row_max[:], 2, 32), ALU.subtract).then_inc(soft, 1)

            def soft_norm(t):
                dve.wait_ge(e_ok, t + 1)
                v.tensor_reduce(row_sum[:], flat(sm_e), AX_X, ALU.add).then_inc(soft, 1)
                dve.wait_ge(soft, t * 6 + 4)
                v.reciprocal(row_inv[:], row_sum[:]).then_inc(soft, 1)
                dve.wait_ge(soft, t * 6 + 5)
                v.tensor_tensor(flat(sm_e), flat(sm_e), repeat(row_inv[:], 2, 32), ALU.mult).then_inc(soft, 1)
                dve.wait_ge(soft, t * 6 + 6)
                dve.wait_ge(pv_mm, t * 8) if not isinstance(t, int) or t > 0 else None
                for b in range(BPG):
                    last = v.transpose(p_blocks[quadrant(b), :, :, quadrant(b)].rearrange("p h g q -> p (h g) q"),
                                       sm_e[quadrant(b)].rearrange("p h g k -> p (h g) k"))
                last.then_inc(p_ok, 1)

            soft_max(0)
            dve.wait_ge(blocks_zero, 1)
            soft_norm(0)
            split_v(1)

            def attn_out(t, units=range(8)):
                for u in units:
                    h, half = u % QUAD, u // QUAD
                    tok = slice(HALF * half, HALF * half + HALF)
                    dve.wait_ge(ahi_ok, t * 8 + (u + 1))
                    v.scalar_tensor_tensor(attn_lo[:, h, tok], bank(2 + u % 4),
                                           params[:, PARAM["bv"], bass.ds(t * QUAD + h, 1)],
                                           attn_hi[:, h, tok].bitcast(F32), ALU.add, ALU.subtract).then_inc(alo_ok, 1)

            def split_o(t):
                dve.wait_ge(wohi_ok, t + 1)
                v.tensor_tensor(chunks_backwards(wo_lo), wo_raw[:].rearrange("p h (c n) -> p (h c) n", n=P),
                                chunks_backwards(wo_hi).bitcast(F32), ALU.subtract).then_inc(wolo_ok, 1)

            def accumulate(t, groups, first=False):
                for g in groups:
                    dve.wait_ge(wo_mm, t * 8 + (g + 1))
                    if not first:
                        dve.wait_ge(acc_ok, t * 8 + (g - 7))
                    v.tensor_tensor(acc[:, g, :], bank(6 + g % 2), acc[:, g, :], ALU.add).then_inc(acc_ok, 1)

            def quad(t, first=False, split=True):
                attn_out(t)
                split_o(t)
                soft_max(t + 1)
                soft_norm(t + 1)
                accumulate(t, (0, 1, 2), first)
                for c in range(KC):
                    if split:
                        split_v(t + 2, (c,))
                    accumulate(t, (3 + c,), first)
                accumulate(t, (7,), first)

            dve.wait_ge(acc_set, G)
            quad(0, first=True)
            with dve.Fori(1, NQ - 2) as t:
                quad(t)
            quad(NQ - 2, split=False)
            attn_out(NQ - 1, range(4))
            split_o(NQ - 1)
            attn_out(NQ - 1, range(4, 8))
            accumulate(NQ - 1, range(8))

            dve.wait_ge(fhi_ok, 1)
            v.tensor_tensor(ffn_lo[:].rearrange("p c n -> p (c n)"), ffn_raw[:].rearrange("p c n -> p (c n)"),
                            ffn_hi[:].rearrange("p c n -> p (c n)").bitcast(F32), ALU.subtract).then_inc(flo_ok, 1)
            dve.wait_ge(mask_ok, 1)

            def y_low(u):
                dve.wait_ge(yhi_ok, u + 1)
                part = slice(4 * u, 4 * u + 4)
                v.tensor_tensor(y_lo[:, :, :, part], y_t[:, :, :, part], y_hi[:, :, :, part].bitcast(F32),
                                ALU.subtract).then_inc(ylo_ok, 1)

            for u in range(8):
                dve.wait_ge(conv_mm, u + 1)
                v.tensor_tensor(y_t[:, :, :, 4 * u:4 * u + 4].rearrange("p c b s -> p s c b"),
                                bank(2 + u % 2).rearrange("p (s c b) -> p s c b", s=4, c=KC),
                                repeat(mask[:], 1, 4), ALU.mult).then_inc(y_ok, 1)
                if u > 0:
                    y_low(u - 1)
            y_low(7)
            def down_out(g):
                dve.wait_ge(ax_mm, g + 1)
                if g >= 2:
                    dve.wait_ge(out_mm, g - 1)
                v.tensor_copy(ax[0:2 * RANK, g % 2, :], bank(4 + g % 2)[0:2 * RANK, 0:P]).then_inc(ax_ok, 1)

            down_out(0)
            for g in range(G):
                if g + 1 < G:
                    down_out(g + 1)
                dve.wait_ge(out_mm, g + 1)
                if g >= 2:
                    dve.wait_ge(out_dma[g % 2], 16 * (g // 2))
                v.tensor_tensor(o_stage[:, g % 2, :].rearrange("p (c n) -> p c n", n=P),
                                bank(6 + g % 2).rearrange("p (c n) -> p c n", n=P),
                                backwards(acc[:, g, :].rearrange("p (c n) -> p c n", n=P)), ALU.add).then_inc(out_ok, 1)


_INS = [("x", "x", (TOK, FEAT), F32), ("cond_idx", "itok_B_0_15", (BATCH,), I32),
        ("lengths", "itok_B_78_3631", (BATCH,), I32), ("cond_w", "L0_cond_weights", (NCOND, 32, 32), F32),
        ("wq", "L0_attn_Wq", (FEAT, INNER), F32), ("bq", "L0_attn_bq", (INNER,), F32),
        ("wk", "L0_attn_Wk", (FEAT, INNER), F32), ("bk", "L0_attn_bk", (INNER,), F32),
        ("wv", "L0_attn_Wv", (FEAT, INNER), F32), ("bv", "L0_attn_bv", (INNER,), F32),
        ("wo", "L0_attn_Wo", (INNER, FEAT), F32), ("bo", "L0_attn_bo", (FEAT,), F32),
        ("gq", "L0_attn_gq", (INNER,), F32), ("gk", "L0_attn_gk", (INNER,), F32),
        ("log_dt", "L0_cond2_log_dt", (SEQ,), F32), ("ssm_c", "L0_cond2_C", (SEQ, NSTATE, 2), F32),
        ("log_a", "L0_cond2_log_A_real", (SEQ, NSTATE), F32), ("a_im", "L0_cond2_A_imag", (SEQ, NSTATE), F32),
        ("ssm_d", "L0_cond2_D", (SEQ,), F32), ("gate", "L0_ffn_gate", (G, NLORA), F32),
        ("ffn_w", "L0_ffn_kernel", (FEAT, FEAT), F32), ("ffn_b", "L0_ffn_bias", (FEAT,), F32),
        ("lora_a", "L0_ffn_lora_A", (NLORA, RANK, FEAT), F32), ("lora_b", "L0_ffn_lora_B", (NLORA, FEAT, RANK), F32),
        ("lora_as", "L0_ffn_lora_A_shared", (RANK, FEAT), F32), ("lora_bs", "L0_ffn_lora_B_shared", (FEAT, RANK), F32)]


def kernel(**inputs):
    import numpy as np
    import concourse.bacc as bacc
    from concourse.bass_utils import run_bass_kernel_spmd

    nc = bacc.Bacc("TRN2", target_bir_lowering=False, num_devices=1)
    arrays, args = {}, {}
    for name, key, shape, dt in _INS:
        arrays[f"in_{name}"] = np.ascontiguousarray(inputs[key]).reshape(shape)
        args[name] = nc.dram_tensor(f"in_{name}", shape, dt, kind="ExternalInput").ap()
    for name, shape in (("a_scr", (P, KC, G, 2 * RANK)), ("b_scr", (RANK, G, FEAT)), ("bs_scr", (RANK, FEAT))):
        args[name] = nc.dram_tensor(f"{name}_dram", shape, F32, kind="Internal").ap()
    args["kpad"] = nc.dram_tensor("kpad_dram", (SEQ, PADL), F32, kind="Internal").ap()
    args["out"] = nc.dram_tensor("out_dram", (TOK, FEAT), F32, kind="ExternalOutput").ap()
    build_program(nc, **args)
    result = run_bass_kernel_spmd(nc, [arrays], core_ids=[0])
    return result.results[0]["out_dram"].reshape(BATCH, SEQ, FEAT)
```
